# Optimizing a Trainium2 kernel written in Bass

```python
import numpy as np
import jax
import jax.numpy as jnp

def _softmax(x, axis=-1):
    return jax.nn.softmax(x, axis=axis)

def _gelu(x):
    return jax.nn.gelu(x, approximate=True)

def _silu(x):
    return jax.nn.silu(x)

def _sigmoid(x):
    return jax.nn.sigmoid(x)

def _layernorm(x, axis=-1, eps=1e-05):
    m = jnp.mean(x, axis=axis, keepdims=True)
    v = jnp.var(x, axis=axis, keepdims=True)
    return (x - m) / jnp.sqrt(v + eps)

def _scatter_add(tgt, idx, src, axis=0):
    return tgt.at[idx].add(src)

def _segment_sum(src, seg, n):
    return jax.ops.segment_sum(src, seg, n)
kernel_name = 'mk_adj_preln_d4_adj_r2_e85238'

def setup_inputs(seed: int=0):
    np.random.seed(seed)
    _w = jnp.asarray

    def _rec_inputs():
        import jax
        import jax.numpy as jnp
        _gk = jax.random.key(seed)
        x = -0.0001538 + 1 * jax.random.normal(jax.random.fold_in(_gk, 1), (64, 128, 384), jnp.float32)
        _a = jax.random.bernoulli(jax.random.fold_in(_gk, 2), 0.0625, (64, 128, 128))
        _a = jnp.logical_or(_a, jnp.swapaxes(_a, -1, -2))
        _a = jnp.logical_or(_a, jnp.eye(128, dtype=bool))
        _af = _a.astype(jnp.float32)
        _af = _af * jax.random.uniform(jax.random.fold_in(_gk, 3), (64, 128, 128), jnp.float32, 0.05, 4.42607)
        adj = _af
        return (x, adj)
    x, adj = _rec_inputs()

    def _L0_gnn_setup():
        import jax, jax.numpy as jnp
        import numpy as np
        NUM_HEADS = 12
        HIDDEN = 384
        HEAD = HIDDEN // NUM_HEADS
        B, N = (16, 256)
        key = jax.random.key(seed)
        ks = jax.random.split(key, 9)
        s = 0.02
        return {'x': jax.random.normal(ks[0], (B, N, HIDDEN), jnp.float32), 'spatial_encoding': jax.random.normal(ks[1], (B, N, N), jnp.float32), 'edge_encoding': jax.random.normal(ks[2], (B, N, N), jnp.float32), 'Wq': jax.random.normal(ks[3], (HIDDEN, HIDDEN), jnp.float32) * s, 'Wk': jax.random.normal(ks[4], (HIDDEN, HIDDEN), jnp.float32) * s, 'Wv': jax.random.normal(ks[5], (HIDDEN, HIDDEN), jnp.float32) * s, 'bv': jax.random.normal(ks[6], (HIDDEN,), jnp.float32) * s, 'Wo': jax.random.normal(ks[7], (HIDDEN, HIDDEN), jnp.float32) * s, 'bo': jax.random.normal(ks[8], (HIDDEN,), jnp.float32) * s}
    _L0_gnn_all = _L0_gnn_setup()
    _L0_gnn_in = {k: v for k, v in _L0_gnn_all.items() if k in ('Wq', 'Wk', 'Wv', 'bv', 'Wo', 'bo')}
    del _L0_gnn_all

    def _L1_gnn_setup():
        import jax, jax.numpy as jnp
        import numpy as np
        LN_EPS = 1e-12

        def _digcn_forward(hidden_state, adjacency_matrix, Wl, bl, Ws, bs, Wr, br, ln_w, ln_b):
            B, S, D = hidden_state.shape
            temper = jnp.asarray(D, jnp.float32) ** 0.5
            i = jnp.arange(S)
            upper = (i[None, :] > i[:, None]).astype(hidden_state.dtype)
            lower = (i[None, :] < i[:, None]).astype(hidden_state.dtype)

            def layer(h, params):
                wl, b_l, ws, b_s, wr, b_r, g, beta = params
                u = jnp.einsum('bid,bjd->bij', h, h) / temper
                a = jax.nn.softmax(u, axis=-1)
                delta = a * adjacency_matrix
                attn = delta / (jnp.sum(delta, axis=-1, keepdims=True) + 1e-10)
                hl = h @ wl.T + b_l
                hs = h @ ws.T + b_s
                hr = h @ wr.T + b_r
                diag_a = jnp.diagonal(attn, axis1=1, axis2=2)
                ctx = jnp.einsum('bij,bjd->bid', attn * upper, hl) + diag_a[..., None] * hs + jnp.einsum('bij,bjd->bid', attn * lower, hr)
                mean = ctx.mean(-1, keepdims=True)
                var = ctx.var(-1, keepdims=True)
                o = (ctx - mean) / jnp.sqrt(var + LN_EPS) * g + beta
                return (jax.nn.relu(o), None)
            out, _ = jax.lax.scan(layer, hidden_state, (Wl, bl, Ws, bs, Wr, br, ln_w, ln_b))
            return out
        key = jax.random.key(seed)
        ks = jax.random.split(key, 6)
        B, S, D, L = (8, 512, 384, 2)
        scale = (1.0 / D) ** 0.5
        hidden_state = jax.random.normal(ks[0], (B, S, D), jnp.float32)
        adjacency_matrix = (jax.random.uniform(ks[1], (B, S, S)) < 0.05).astype(jnp.float32)
        Wl = jax.random.normal(ks[2], (L, D, D), jnp.float32) * scale
        Ws = jax.random.normal(ks[3], (L, D, D), jnp.float32) * scale
        Wr = jax.random.normal(ks[4], (L, D, D), jnp.float32) * scale
        bl = jnp.zeros((L, D), jnp.float32)
        bs = jnp.zeros((L, D), jnp.float32)
        br = jnp.zeros((L, D), jnp.float32)
        ln_w = jnp.ones((L, D), jnp.float32)
        ln_b = jnp.zeros((L, D), jnp.float32)
        return dict(hidden_state=hidden_state, adjacency_matrix=adjacency_matrix, Wl=Wl, bl=bl, Ws=Ws, bs=bs, Wr=Wr, br=br, ln_w=ln_w, ln_b=ln_b)
    _L1_gnn_all = _L1_gnn_setup()
    _L1_gnn_in = {k: v for k, v in _L1_gnn_all.items() if k in ('Wl', 'bl', 'Ws', 'bs', 'Wr', 'br', 'ln_w', 'ln_b')}
    del _L1_gnn_all

    def _L2_gnn_setup():
        import jax, jax.numpy as jnp
        import numpy as np
        B, S, H, L = (32, 256, 384, 2)

        def _layer_norm(z, a, b, eps=0.001):
            mu = jnp.mean(z, axis=-1, keepdims=True)
            sigma = jnp.std(z, axis=-1, keepdims=True, ddof=1)
            return (z - mu) / (sigma + eps) * a + b
        key = jax.random.key(seed)
        ks = jax.random.split(key, 6)
        hidden_state = jax.random.normal(ks[0], (B, S, H), dtype=jnp.float32)
        adjacency_matrix = (jax.random.uniform(ks[1], (B, S, S)) < 0.2).astype(jnp.float32)
        W_left = 0.05 * jax.random.normal(ks[2], (L, H, H), dtype=jnp.float32)
        W_right = 0.05 * jax.random.normal(ks[3], (L, H, H), dtype=jnp.float32)
        W_lin = 0.05 * jax.random.normal(ks[4], (L, H, H), dtype=jnp.float32)
        b_lin = jnp.zeros((L, H), dtype=jnp.float32)
        ln_a = jnp.ones((L, H), dtype=jnp.float32)
        ln_b = jnp.zeros((L, H), dtype=jnp.float32)
        return {'hidden_state': hidden_state, 'adjacency_matrix': adjacency_matrix, 'W_left': W_left, 'W_right': W_right, 'W_lin': W_lin, 'b_lin': b_lin, 'ln_a': ln_a, 'ln_b': ln_b}
    _L2_gnn_all = _L2_gnn_setup()
    _L2_gnn_in = {k: v for k, v in _L2_gnn_all.items() if k in ('W_left', 'W_right', 'W_lin', 'b_lin', 'ln_a', 'ln_b')}
    del _L2_gnn_all

    def _L3_gnn_setup():
        import jax, jax.numpy as jnp
        import numpy as np
        B, N, D, H = (8, 512, 384, 12)
        HD = D // H

        def _split_heads(x):
            b, n, _ = x.shape
            return x.reshape(b, n, H, HD).transpose(0, 2, 1, 3)
        key = jax.random.key(seed)
        ks = jax.random.split(key, 10)
        input_graph = jax.random.normal(ks[0], (B, N, D), dtype=jnp.float32)
        u = jax.random.uniform(ks[1], (B, N, N), dtype=jnp.float32)
        keep = jax.random.uniform(ks[2], (B, N, N)) < 0.15
        adj = jnp.where(keep, u, 0.0)
        s = 1.0 / np.sqrt(D)
        Wq = jax.random.normal(ks[3], (D, D), dtype=jnp.float32) * s
        bq = jnp.zeros((D,), dtype=jnp.float32)
        Wk = jax.random.normal(ks[4], (D, D), dtype=jnp.float32) * s
        bk = jnp.zeros((D,), dtype=jnp.float32)
        Wv = jax.random.normal(ks[5], (D, D), dtype=jnp.float32) * s
        bv = jnp.zeros((D,), dtype=jnp.float32)
        beta = jnp.asarray(0.1, dtype=jnp.float32)
        return {'input_graph': input_graph, 'adj': adj, 'Wq': Wq, 'bq': bq, 'Wk': Wk, 'bk': bk, 'Wv': Wv, 'bv': bv, 'beta': beta}
    _L3_gnn_all = _L3_gnn_setup()
    _L3_gnn_in = {k: v for k, v in _L3_gnn_all.items() if k in ('Wq', 'bq', 'Wk', 'bk', 'Wv', 'bv', 'beta')}
    del _L3_gnn_all
    return {'x': x, 'adj': adj, 'L0_gnn_Wq': _L0_gnn_in['Wq'], 'L0_gnn_Wk': _L0_gnn_in['Wk'], 'L0_gnn_Wv': _L0_gnn_in['Wv'], 'L0_gnn_bv': _L0_gnn_in['bv'], 'L0_gnn_Wo': _L0_gnn_in['Wo'], 'L0_gnn_bo': _L0_gnn_in['bo'], 'L1_gnn_Wl': _L1_gnn_in['Wl'], 'L1_gnn_bl': _L1_gnn_in['bl'], 'L1_gnn_Ws': _L1_gnn_in['Ws'], 'L1_gnn_bs': _L1_gnn_in['bs'], 'L1_gnn_Wr': _L1_gnn_in['Wr'], 'L1_gnn_br': _L1_gnn_in['br'], 'L1_gnn_ln_w': _L1_gnn_in['ln_w'], 'L1_gnn_ln_b': _L1_gnn_in['ln_b'], 'L2_gnn_W_left': _L2_gnn_in['W_left'], 'L2_gnn_W_right': _L2_gnn_in['W_right'], 'L2_gnn_W_lin': _L2_gnn_in['W_lin'], 'L2_gnn_b_lin': _L2_gnn_in['b_lin'], 'L2_gnn_ln_a': _L2_gnn_in['ln_a'], 'L2_gnn_ln_b': _L2_gnn_in['ln_b'], 'L3_gnn_Wq': _L3_gnn_in['Wq'], 'L3_gnn_bq': _L3_gnn_in['bq'], 'L3_gnn_Wk': _L3_gnn_in['Wk'], 'L3_gnn_bk': _L3_gnn_in['bk'], 'L3_gnn_Wv': _L3_gnn_in['Wv'], 'L3_gnn_bv': _L3_gnn_in['bv'], 'L3_gnn_beta': _L3_gnn_in['beta']}

def reference(x, adj, L0_gnn_Wq, L0_gnn_Wk, L0_gnn_Wv, L0_gnn_bv, L0_gnn_Wo, L0_gnn_bo, L1_gnn_Wl, L1_gnn_bl, L1_gnn_Ws, L1_gnn_bs, L1_gnn_Wr, L1_gnn_br, L1_gnn_ln_w, L1_gnn_ln_b, L2_gnn_W_left, L2_gnn_W_right, L2_gnn_W_lin, L2_gnn_b_lin, L2_gnn_ln_a, L2_gnn_ln_b, L3_gnn_Wq, L3_gnn_bq, L3_gnn_Wk, L3_gnn_bk, L3_gnn_Wv, L3_gnn_bv, L3_gnn_beta):
    import jax
    import jax.numpy as jnp

    def _L0_gnn_ref(x, spatial_encoding, edge_encoding, Wq, Wk, Wv, bv, Wo, bo):
        import jax, jax.numpy as jnp
        import numpy as np
        NUM_HEADS = 12
        HIDDEN = 384
        HEAD = HIDDEN // NUM_HEADS
        B, N = (16, 256)
        b, n, h = x.shape
        scale = jnp.asarray(HIDDEN, x.dtype) ** (-0.5)
        q = (x @ Wq.T).reshape(b, n, NUM_HEADS, HEAD)
        k = (x @ Wk.T).reshape(b, n, NUM_HEADS, HEAD)
        v = (x @ Wv.T + bv).reshape(b, n, NUM_HEADS, HEAD)
        bias = (spatial_encoding + edge_encoding)[:, None]
        scores = jnp.einsum('bqhd,bkhd->bhqk', q, k) * scale + bias
        row_nonzero = jnp.any(scores != 0, axis=-1, keepdims=True)
        scores = jnp.where(row_nonzero, scores, -jnp.inf)
        p = jax.nn.softmax(scores, axis=-1)
        p = jnp.nan_to_num(p)
        out = jnp.einsum('bhqk,bkhd->bqhd', p, v).reshape(b, n, h)
        return out @ Wo.T + bo

    def _L1_gnn_ref(hidden_state, adjacency_matrix, Wl, bl, Ws, bs, Wr, br, ln_w, ln_b):
        import jax, jax.numpy as jnp
        import numpy as np
        LN_EPS = 1e-12

        def _digcn_forward(hidden_state, adjacency_matrix, Wl, bl, Ws, bs, Wr, br, ln_w, ln_b):
            B, S, D = hidden_state.shape
            temper = jnp.asarray(D, jnp.float32) ** 0.5
            i = jnp.arange(S)
            upper = (i[None, :] > i[:, None]).astype(hidden_state.dtype)
            lower = (i[None, :] < i[:, None]).astype(hidden_state.dtype)

            def layer(h, params):
                wl, b_l, ws, b_s, wr, b_r, g, beta = params
                u = jnp.einsum('bid,bjd->bij', h, h) / temper
                a = jax.nn.softmax(u, axis=-1)
                delta = a * adjacency_matrix
                attn = delta / (jnp.sum(delta, axis=-1, keepdims=True) + 1e-10)
                hl = h @ wl.T + b_l
                hs = h @ ws.T + b_s
                hr = h @ wr.T + b_r
                diag_a = jnp.diagonal(attn, axis1=1, axis2=2)
                ctx = jnp.einsum('bij,bjd->bid', attn * upper, hl) + diag_a[..., None] * hs + jnp.einsum('bij,bjd->bid', attn * lower, hr)
                mean = ctx.mean(-1, keepdims=True)
                var = ctx.var(-1, keepdims=True)
                o = (ctx - mean) / jnp.sqrt(var + LN_EPS) * g + beta
                return (jax.nn.relu(o), None)
            out, _ = jax.lax.scan(layer, hidden_state, (Wl, bl, Ws, bs, Wr, br, ln_w, ln_b))
            return out
        return _digcn_forward(hidden_state, adjacency_matrix, Wl, bl, Ws, bs, Wr, br, ln_w, ln_b)

    def _L2_gnn_ref(hidden_state, adjacency_matrix, W_left, W_right, W_lin, b_lin, ln_a, ln_b):
        import jax, jax.numpy as jnp
        import numpy as np
        B, S, H, L = (32, 256, 384, 2)

        def _layer_norm(z, a, b, eps=0.001):
            mu = jnp.mean(z, axis=-1, keepdims=True)
            sigma = jnp.std(z, axis=-1, keepdims=True, ddof=1)
            return (z - mu) / (sigma + eps) * a + b
        temper = float(np.sqrt(H))
        adj = adjacency_matrix
        adj_tri = jnp.triu(adj, k=1)
        diag_mask = jnp.triu(adj, k=0) - adj_tri
        h = hidden_state
        for l in range(L):
            m_left = jnp.einsum('bsh,oh->bso', h, W_left[l])
            m_right = jnp.einsum('bsh,oh->bso', h, W_right[l])
            u_left = jnp.einsum('bih,bjh->bij', h, m_left) / temper
            u_right = jnp.einsum('bih,bjh->bij', h, m_right) / temper
            u = u_left * adj_tri + u_left * diag_mask + u_right * jnp.swapaxes(adj_tri, 1, 2)
            delta_exp_u = jnp.exp(u) * adj
            attention = delta_exp_u / (jnp.sum(delta_exp_u, axis=2, keepdims=True) + 1e-10)
            h_lin = jnp.einsum('bsh,oh->bso', h, W_lin[l]) + b_lin[l]
            ctx = jnp.matmul(attention, h_lin)
            h = jax.nn.relu(_layer_norm(ctx, ln_a[l], ln_b[l]))
        return h

    def _L3_gnn_ref(input_graph, adj, Wq, bq, Wk, bk, Wv, bv, beta):
        import jax, jax.numpy as jnp
        import numpy as np
        B, N, D, H = (8, 512, 384, 12)
        HD = D // H

        def _split_heads(x):
            b, n, _ = x.shape
            return x.reshape(b, n, H, HD).transpose(0, 2, 1, 3)
        q = _split_heads(input_graph @ Wq + bq)
        k = _split_heads(input_graph @ Wk + bk)
        v = _split_heads(input_graph @ Wv + bv)
        scores = jnp.einsum('bhqd,bhkd->bhqk', q, k) / jnp.sqrt(jnp.asarray(HD, input_graph.dtype))
        adj_e = adj[:, None, :, :]
        scores = scores + beta * adj_e
        scores = jnp.where(adj_e > 0, scores, jnp.asarray(-9000000000000000.0, scores.dtype))
        probs = jax.nn.softmax(scores, axis=-1)
        out = jnp.einsum('bhqk,bhkd->bhqd', probs, v)
        return out.transpose(0, 2, 1, 3).reshape(input_graph.shape[0], input_graph.shape[1], D)
    h = jnp.maximum(_layernorm(x, axis=-1), 0.0)
    x = x + _L0_gnn_ref(h, adj, adj, L0_gnn_Wq, L0_gnn_Wk, L0_gnn_Wv, L0_gnn_bv, L0_gnn_Wo, L0_gnn_bo)
    h = jnp.maximum(_layernorm(x, axis=-1), 0.0)
    x = x + _L1_gnn_ref(h, adj, L1_gnn_Wl, L1_gnn_bl, L1_gnn_Ws, L1_gnn_bs, L1_gnn_Wr, L1_gnn_br, L1_gnn_ln_w, L1_gnn_ln_b)
    h = jnp.maximum(_layernorm(x, axis=-1), 0.0)
    x = x + _L2_gnn_ref(h, adj, L2_gnn_W_left, L2_gnn_W_right, L2_gnn_W_lin, L2_gnn_b_lin, L2_gnn_ln_a, L2_gnn_ln_b)
    h = jnp.maximum(_layernorm(x, axis=-1), 0.0)
    x = x + _L3_gnn_ref(h, adj, L3_gnn_Wq, L3_gnn_bq, L3_gnn_Wk, L3_gnn_bk, L3_gnn_Wv, L3_gnn_bv, L3_gnn_beta)
    return x

_drawn_inputs = setup_inputs


def setup_inputs(seed=0):
    import zlib

    import numpy as np

    out = dict(_drawn_inputs(seed))
    spreads = {'L1_gnn_bl': (0.0, 0.68),
     'L1_gnn_bs': (0.0, 0.1),
     'L1_gnn_br': (0.0, 0.652),
     'L1_gnn_ln_w': (1.0, 0.2),
     'L1_gnn_ln_b': (0.0, 0.1),
     'L2_gnn_b_lin': (0.0, 0.1),
     'L2_gnn_ln_a': (1.0, 0.2),
     'L2_gnn_ln_b': (0.0, 0.1),
     'L3_gnn_bq': (0.0, 0.8),
     'L3_gnn_bk': (0.0, 0.8),
     'L3_gnn_bv': (0.0, 0.1)}
    factors = {'L0_gnn_Wq': 8.0, 'L0_gnn_Wk': 8.0, 'L0_gnn_bv': 6.997, 'L0_gnn_bo': 3.216}
    for name, (base, spread) in spreads.items():
        noise = np.random.default_rng([zlib.crc32(name.encode()), seed]).standard_normal(out[name].shape)
        drawn = base * np.exp(spread * noise) if base else spread * noise
        out[name] = jnp.asarray(drawn.astype(out[name].dtype))
    for name, factor in factors.items():
        out[name] = (out[name] * factor).astype(out[name].dtype)
    return out
```

```python
from contextlib import ExitStack

import concourse.bass as bass
from concourse import mybir

F32 = mybir.dt.float32
F32R = mybir.dt.float32r
ALU = mybir.AluOpType
ACT = mybir.ActivationFunctionType
AX = mybir.AxisListType

P = 128
D = 384
C = D // P
G = 2
T = G * P
HEADS = 12
HD = D // HEADS
R = P // HD
BANK = 512
LN_EPS = 1e-5


class Signal:

    def __init__(self, sem, per, base):
        self.sem, self.per, self.base = sem, per, base


class Signals:

    START = 32

    def __init__(self, nc, ctx, pairs):
        self.nc, self.ctx, self.pairs = nc, ctx, pairs
        self.count, self.sems, self.open, self.fresh = {}, {}, [], []

    def sem(self, name, start):
        if name not in self.sems:
            self.sems[name] = self.ctx.enter_context(self.nc.semaphore(name))
            self.count[name] = start
            if start:
                self.fresh.append(self.sems[name])
        return self.sems[name]

    def __call__(self, name, per):
        sem = self.sem(name, self.START)
        self.open.append((name, per))
        return Signal(sem, per, self.count[name])

    def once(self, name, n):
        sem = self.sem(name, 0)
        self.count[name] += n
        return Signal(sem, 0, self.count[name] - n)

    def raise_fresh(self):
        nc, fresh, self.fresh = self.nc, self.fresh, []
        with nc.Block() as block:
            @block.sync
            def _(sp):
                for sem in fresh:
                    sp.sem_inc(sem, self.START)

    def end_phase(self):
        for name, per in self.open:
            self.count[name] += per * self.pairs
        self.open = []


def at(signal, k, j):
    return signal.base + signal.per * k + j


def dma_at(signal, k, parity):
    return signal.base + signal.per * (k - parity) + 2 * signal.per


class Split:

    def __init__(self, hi, lo):
        self.hi, self.lo = hi, lo


def product(nc, out, left, right, first=True, last=True):
    n = len(left)
    for c in range(n):
        (lh, ll), (rh, rl) = left[c], right[c]
        nc.tensor.matmul(out, lh, rh, start=first and c == 0, stop=False)
        nc.tensor.matmul(out, lh, rl, start=False, stop=False)
        ins = nc.tensor.matmul(out, ll, rh, start=False, stop=last and c == n - 1)
    return ins


def steps(engine, pairs):
    with engine.Fori(0, (pairs - 2) // 2) as i:
        for parity in range(2):
            yield 2 * i + parity, parity, True
    yield pairs - 2, 0, False


class Core:
    pass


def load_weights(nc, core, ctx, names, consts):
    splits = []
    for name in names:
        hi = ctx.enter_context(nc.sbuf_tensor(f"{name}_hi", [P, C, D], F32R))
        lo = ctx.enter_context(nc.sbuf_tensor(f"{name}_lo", [P, C, D], F32R))
        splits.append(Split(hi, lo))
    sig = core.signals
    with ExitStack() as staging:
        raw = [staging.enter_context(nc.sbuf_tensor(f"{n}_raw", [P, C, D], F32)) for n in names]
        consts_in = core.signals.once("consts_in", 16 * len(consts))
        weight_in = [core.signals.once(f"weight{j}_in", 16) for j in range(len(names))]
        hi_done = core.signals.once("weight_hi_done", len(names))
        lo_done = core.signals.once("weight_lo_done", len(names))
        block = staging.enter_context(nc.Block())

        @block.sync
        def _(sp):
            for j, name in enumerate(names):
                sp.dma_start(raw[j][:, :, :], core.dram[name]).then_inc(weight_in[j].sem, 16)
            for dst, src in consts:
                sp.dma_start(dst, src).then_inc(consts_in.sem, 16)
            sp.wait_ge(consts_in.sem, consts_in.base + 16 * len(consts))

        @block.scalar
        def _(act):
            for j in range(len(names)):
                act.wait_ge(weight_in[j].sem, weight_in[j].base + 16)
                nc.scalar.activation(splits[j].hi[:, :, :], raw[j][:, :, :], ACT.Copy).then_inc(hi_done.sem, 1)

        @block.vector
        def _(dve):
            for j in range(len(names)):
                dve.wait_ge(hi_done.sem, hi_done.base + j + 1)
                nc.vector.tensor_tensor(splits[j].lo[:, :, :], raw[j][:, :, :],
                                        splits[j].hi[:, :, :].bitcast(F32), ALU.subtract).then_inc(lo_done.sem, 1)
    return splits


def chunk(ap, c):
    return ap[:, c, :]



class Residual:

    SLOTS = 4

    def __init__(self, nc, core, ctx, tag, src, dst):
        self.nc, self.core, self.src, self.dst = nc, core, src, dst
        self.buffer = ctx.enter_context(nc.sbuf_tensor(f"{tag}_x", [P, self.SLOTS * G, D], F32))
        self.loaded = [core.signals(f"x_loaded{j}", 8) for j in range(2)]
        self.stored = [core.signals(f"x_stored{j}", 8) for j in range(2)]

    def pair(self, k):
        return self.buffer[:, bass.ds(G * (k & (self.SLOTS - 1)), G), :]

    def graph(self, k, g):
        return self.buffer[:, bass.ds(G * (k & (self.SLOTS - 1)) + g, 1), :][:, 0, :]

    def wait_loaded(self, engine, k, parity):
        engine.wait_ge(self.loaded[parity].sem, dma_at(self.loaded[parity], k, parity))

    def load(self, sp, norm, k, parity):
        sp.wait_ge(self.stored[parity].sem, dma_at(self.stored[parity], k - self.SLOTS, parity))
        sp.sem_inc(self.core.unwatched.sem, 1)
        sp.wait_ge(norm.ready.sem, at(norm.ready, k - 1, 0))
        sp.sem_inc(self.core.unwatched.sem, 1)
        sp.dma_start(self.pair(k), self.src[bass.ds(G * k, G), :, :].rearrange("g p d -> p g d")
                     ).then_inc(self.loaded[parity].sem, 16)

    def store(self, sp, k, parity):
        sp.dma_start(self.dst[bass.ds(G * k, G), :, :].rearrange("g p d -> p g d"), self.pair(k)
                     ).then_inc(self.stored[parity].sem, 16)

    def wait_stored(self, sp):
        for s in self.stored:
            sp.wait_ge(s.sem, s.base + s.per * self.core.pairs)


class InputNorm:

    def __init__(self, nc, core, ctx, tag, x):
        self.nc, self.core, self.x = nc, core, x
        self.xhat = ctx.enter_context(nc.sbuf_tensor(f"{tag}_xhat", [P, G, D], F32))
        self.stats = ctx.enter_context(nc.sbuf_tensor(f"{tag}_in_stats", [P, G, 6], F32))
        self.moments = ctx.enter_context(nc.sbuf_tensor(f"{tag}_in_moments", [P, G, 2], F32))
        self.log = ctx.enter_context(nc.sbuf_tensor(f"{tag}_in_log", [P, G], F32))
        self.rstd = ctx.enter_context(nc.sbuf_tensor(f"{tag}_in_rstd", [P, G], F32))
        self.stats_done = core.signals("in_stats_done", G)
        self.var_ready = core.signals("in_var_ready", G)
        self.log_done = core.signals("in_log_done", 1)
        self.rstd_ready = core.signals("in_rstd_ready", 1)
        self.ready = core.signals("xhat_ready", G)

    def dve_moments(self, dve, k, parity):
        nc = self.nc
        self.x.wait_loaded(dve, k, parity)
        for g in range(G):
            nc.vector.bn_stats(self.stats[:, g, :], self.x.graph(k, g)).then_inc(self.stats_done.sem, 1)
        for g in range(G):
            dve.wait_ge(self.stats_done.sem, at(self.stats_done, k, g + 1))
            dve.sem_inc(self.core.unwatched.sem, 1)
            nc.vector.bn_aggr(self.moments[:, g, :], self.stats[:, g, :]).then_inc(self.var_ready.sem, 1)

    def act_rstd(self, act, k):
        nc = self.nc
        act.wait_ge(self.var_ready.sem, at(self.var_ready, k, G))
        nc.scalar.activation(self.log[:, :], self.moments[:, :, 1], ACT.Ln, bias=self.core.ln_eps[:, :]
                             ).then_inc(self.log_done.sem, 1)
        act.wait_ge(self.log_done.sem, at(self.log_done, k, 1))
        nc.scalar.activation(self.rstd[:, :], self.log[:, :], ACT.Exp, scale=-0.5).then_inc(self.rstd_ready.sem, 1)

    def dve_xhat(self, dve, k):
        nc = self.nc
        dve.wait_ge(self.rstd_ready.sem, at(self.rstd_ready, k, 1))
        for g in range(G):
            nc.vector.tensor_scalar(self.xhat[:, g, :], self.x.graph(k, g), self.moments[:, g, 0:1],
                                    self.rstd[:, g:g + 1], ALU.subtract, ALU.mult).then_inc(self.ready.sem, 1)



def attention_phase(nc, core, names, biases, is_first):
    NP = core.pairs
    HP = HD + 1
    scale = D ** -0.5 if is_first else HD ** -0.5
    tag = "l0" if is_first else "l3"
    with ExitStack() as ctx:
        def sb(name, shape, dt=F32):
            return ctx.enter_context(nc.sbuf_tensor(f"{tag}_{name}", shape, dt))

        bv = sb("bv", [P, D])
        consts = [(bv[:, :], core.dram[biases[0]].partition_broadcast(P))]
        if is_first:
            bo = sb("bo", [P, D])
            consts.append((bo[:, :], core.dram[biases[1]].partition_broadcast(P)))
        else:
            bqk_raw = sb("bqk_raw", [P, 2, C])
            bqk = sb("bqk", [P, 2, C])
            beta = sb("beta", [P, 1])
            consts.append((bqk_raw[:, 0, :], core.dram[biases[1]]))
            consts.append((bqk_raw[:, 1, :], core.dram[biases[2]]))
            consts.append((beta[:, :], core.dram[biases[3]].partition_broadcast(P)))
        weights = load_weights(nc, core, ctx, names, consts)
        wq, wk, wv = weights[:3]

        x = Residual(nc, core, ctx, tag, core.dram["x" if is_first else "x_mid"], core.dram["x_mid" if is_first else "out"])
        norm = InputNorm(nc, core, ctx, tag, x)
        hT = Split(sb("hT_hi", [P, C, T], F32R), sb("hT_lo", [P, C, T], F32R))
        hT_f = sb("hT", [P, C, T])
        qT = sb("qT", [P, 2, C, T])
        kT = sb("kT", [P, 2, C, T])
        v = sb("v", [P, 2, G, HEADS, HP])
        adj = sb("adj", [P, 2, G, P])
        bias = sb("bias", [P, 2, G, P])
        s = sb("s", [P, G, R, C, P])
        s_max = sb("s_max", [P, G, HEADS])
        s_abs = sb("s_abs", [P, G, HEADS])
        probsT = sb("probsT", [P, G, C, R, P])
        rsum = sb("rsum", [P, G, C, R])
        factor = sb("factor", [P, G, C, R])
        o = sb("o", [P, G, C, R, HD])
        if is_first:
            oT = Split(sb("oT_hi", [P, G, C, P], F32R), sb("oT_lo", [P, G, C, P], F32R))
            xb = sb("xb", [P, G, D])

        SO = ctx.enter_context(nc.psum_tensor(f"{tag}_SO", [P, R, BANK], F32))
        S = SO[:, :, 0:C * P].rearrange("p r (c k) -> p r c k", c=C)
        O = SO[:, :, C * P:C * P + C * HP].rearrange("p r (c e) -> p r c e", c=C)
        back = [ctx.enter_context(nc.psum_tensor(f"{tag}_back{j}", [P, BANK], F32)) for j in range(2)]
        front = [ctx.enter_context(nc.psum_tensor(f"{tag}_front{j}", [P, BANK], F32)) for j in range(2)]

        sig = core.signals
        FI = 4
        BG = 5 if is_first else 3
        front_full = [sig(f"front_full{j}", FI) for j in range(2)]
        front_free = [sig(f"front_free{j}", FI) for j in range(2)]
        back_full = [sig(f"back_full{j}", BG) for j in range(2)]
        back_free = [sig(f"back_free{j}", BG) for j in range(2)]
        adj_in = [sig(f"adj_in{j}", 8) for j in range(2)]
        hi_ready = sig("hi_ready", 2)
        lo_ready = sig("lo_ready", 2)
        s_full = sig("s_full", G)
        s_taken = sig("s_taken", G)
        max_ready = sig("max_ready", G)
        shifted = sig("shifted", G)
        probs_ready = sig("probs_ready", G)
        o_full = sig("o_full", G)
        rsum_ready = sig("rsum_ready", G)
        o_ready = sig("o_ready", G)
        bias_ready = sig("bias_ready", 1)
        ones_set = core.signals.once("ones_set", 1)
        if is_first:
            abs_ready = sig("abs_ready", G)
            factor_ready = sig("factor_ready", G)
            oT_hi_ready = sig("oT_hi_ready", G)
            xb_ready = sig("xb_ready", G)
        else:
            x_done = sig("x_done", G)
            bias_step = sig("bias_step", 2)
            bqk_set = core.signals.once("bqk_set", 1)

        def wait_in(engine, signals, k, parity):
            engine.wait_ge(signals[parity].sem, dma_at(signals[parity], k, parity))

        core.signals.raise_fresh()
        block = ctx.enter_context(nc.Block())

        @block.sync
        def _(sp):
            def load_adj(k, parity):
                sp.wait_ge(bias_ready.sem, at(bias_ready, k - 1, 0))
                sp.sem_inc(core.unwatched.sem, 1)
                sp.dma_start(adj[:, parity, :, :],
                             core.dram["adj"][bass.ds(G * k, G), :, :].rearrange("g p d -> p g d")
                             ).then_inc(adj_in[parity].sem, 16)

            def store(k, parity):
                if is_first:
                    for n in (C + 1, BG + C + 1):
                        sp.wait_ge(back_free[n % 2].sem, at(back_free[n % 2], k, n // 2 + 1))
                        sp.sem_inc(core.unwatched.sem, 1)
                else:
                    sp.wait_ge(x_done.sem, at(x_done, k, G))
                    sp.sem_inc(core.unwatched.sem, 1)
                x.store(sp, k, parity)

            for k in range(2):
                x.load(sp, norm, k, k)
                load_adj(k, k)

            for k, parity, more in steps(sp, NP):
                if more:
                    x.load(sp, norm, k + 2, parity)
                    load_adj(k + 2, parity)
                store(k, parity)

            store(NP - 1, 1)
            x.wait_stored(sp)

        @block.tensor
        def _(pe):
            def take_front(k, n):
                pe.wait_ge(front_free[n % 2].sem, at(front_free[n % 2], k, n // 2))
                return front[n % 2]

            def take_back(k, n):
                pe.wait_ge(back_free[n % 2].sem, at(back_free[n % 2], k, n // 2))
                return back[n % 2]

            def transpose_h(k):
                pe.wait_ge(norm.ready.sem, at(norm.ready, k, G))
                for n, chunks in enumerate(((0, 1), (2,))):
                    slot = take_front(k, n)
                    for i, c in enumerate(chunks):
                        for g in range(G):
                            ins = nc.tensor.transpose(slot[:, i * T + g * P:i * T + (g + 1) * P],
                                                      norm.xhat[:, g, c * P:(c + 1) * P], core.ident[:, :])
                    ins.then_inc(front_full[n % 2].sem, 1)

            def project(k, w, n0, first):
                if first:
                    pe.wait_ge(lo_ready.sem, at(lo_ready, k, 2))
                for n, chunks in enumerate(((0, 1), (2,))):
                    slot = take_front(k, n0 + n)
                    for i, o_c in enumerate(chunks):
                        f = slice(o_c * P, (o_c + 1) * P)
                        ins = product(nc, slot[:, i * T:(i + 1) * T],
                                      [(w.hi[:, c, f], w.lo[:, c, f]) for c in range(C)],
                                      [(hT.hi[:, c, :], hT.lo[:, c, :]) for c in range(C)])
                    ins.then_inc(front_full[(n0 + n) % 2].sem, 1)

            def values(k, g):
                n = 6 + g
                slot = take_front(k, n)
                t = slice(g * P, (g + 1) * P)
                product(nc, slot[:, 0:D], [(hT.hi[:, c, t], hT.lo[:, c, t]) for c in range(C)],
                        [(wv.hi[:, c, :], wv.lo[:, c, :]) for c in range(C)]).then_inc(front_full[n % 2].sem, 1)

            def scores(k, parity, g):
                if g == 0:
                    pe.wait_ge(front_free[0].sem, at(front_free[0], k, 3))
                    pe.wait_ge(front_free[1].sem, at(front_free[1], k, 3))
                    pe.wait_ge(o_ready.sem, at(o_ready, k, 0))
                pe.wait_ge(s_taken.sem, at(s_taken, k, g))
                t = slice(g * P, (g + 1) * P)
                for c in range(C):
                    for r in range(R):
                        rows = slice(r * HD, (r + 1) * HD)
                        ins = nc.tensor.matmul(S[:, r, c, :], qT[rows, parity, c, t], kT[rows, parity, c, t],
                                               start=True, stop=True)
                ins.then_inc(s_full.sem, 1)

            def transpose_probs(k, g):
                pe.wait_ge(probs_ready.sem, at(probs_ready, k, g + 1))
                for c in range(C):
                    n = g * BG + c
                    slot = take_back(k, n)
                    for r in range(R):
                        ins = nc.tensor.transpose(slot[:, r * P:(r + 1) * P], s[:, g, r, c, :], core.ident[:, :])
                    ins.then_inc(back_full[n % 2].sem, 1)

            def attend(k, parity, g):
                if g == 0:
                    pe.wait_ge(front_free[0].sem, at(front_free[0], k, 4))
                    pe.wait_ge(front_free[1].sem, at(front_free[1], k, 4))
                pe.wait_ge(s_taken.sem, at(s_taken, k, G))
                pe.wait_ge(o_ready.sem, at(o_ready, k, g))
                for c in range(C):
                    n = g * BG + c
                    pe.wait_ge(back_free[n % 2].sem, at(back_free[n % 2], k, n // 2 + 1))
                    for r in range(R):
                        ins = nc.tensor.matmul(O[:, r, c, :], probsT[:, g, c, r, :], v[:, parity, g, c * R + r, :],
                                               start=True, stop=True)
                ins.then_inc(o_full.sem, 1)

            def transpose_o(k, g):
                pe.wait_ge(o_ready.sem, at(o_ready, k, g + 1))
                n = g * BG + C
                slot = take_back(k, n)
                for c in range(C):
                    ins = nc.tensor.transpose(slot[:, c * P:(c + 1) * P],
                                              o[:, g, c, :, :].rearrange("p r e -> p (r e)"), core.ident[:, :])
                ins.then_inc(back_full[n % 2].sem, 1)

            def project_out(k, g):
                wo = weights[3]
                pe.wait_ge(back_free[(g * BG + C) % 2].sem, at(back_free[(g * BG + C) % 2], k, (g * BG + C) // 2 + 1))
                n = g * BG + C + 1
                slot = take_back(k, n)
                product(nc, slot[:, 0:D], [(oT.hi[:, g, c, :], oT.lo[:, g, c, :]) for c in range(C)],
                        [(wo.hi[:, c, :], wo.lo[:, c, :]) for c in range(C)]).then_inc(back_full[n % 2].sem, 1)

            transpose_h(0)
            project(0, wq, 2, True)
            project(0, wk, 4, False)
            values(0, 0)
            values(0, 1)

            for k, parity, more in steps(pe, NP):
                transpose_h(k + 1)
                scores(k, parity, 0)
                project(k + 1, wq, 2, True)
                scores(k, parity, 1)
                project(k + 1, wk, 4, False)
                values(k + 1, 0)
                values(k + 1, 1)
                transpose_probs(k, 0)
                attend(k, parity, 0)
                if is_first:
                    transpose_o(k, 0)
                    project_out(k, 0)
                transpose_probs(k, 1)
                attend(k, parity, 1)
                if is_first:
                    transpose_o(k, 1)
                    project_out(k, 1)

            k, parity = NP - 1, 1
            scores(k, parity, 0)
            scores(k, parity, 1)
            for g in range(G):
                transpose_probs(k, g)
                attend(k, parity, g)
                if is_first:
                    transpose_o(k, g)
                    project_out(k, g)

        @block.scalar
        def _(act):
            def high_h(k):
                for n, chunks in enumerate(((0, 1), (2,))):
                    act.wait_ge(front_full[n].sem, at(front_full[n], k, 1))
                    cs = slice(chunks[0], chunks[-1] + 1)
                    src = front[n][:, 0:len(chunks) * T].rearrange("p (c t) -> p c t", t=T)
                    nc.scalar.activation(hT_f[:, cs, :], src, ACT.Relu).then_inc(front_free[n].sem, 1)
                for n, chunks in enumerate(((0, 1), (2,))):
                    cs = slice(chunks[0], chunks[-1] + 1)
                    act.wait_ge(front_free[n].sem, at(front_free[n], k, 1))
                    nc.scalar.activation(hT.hi[:, cs, :], hT_f[:, cs, :], ACT.Copy).then_inc(hi_ready.sem, 1)

            def copy_qk(k, parity, which, dst, n0):
                for n, chunks in enumerate(((0, 1), (2,))):
                    slot = (n0 + n) % 2
                    act.wait_ge(front_full[slot].sem, at(front_full[slot], k, (n0 + n) // 2 + 1))
                    if is_first:
                        cs = slice(chunks[0], chunks[-1] + 1)
                        src = front[slot][:, 0:len(chunks) * T].rearrange("p (c t) -> p c t", t=T)
                        ins = nc.scalar.activation(dst[:, parity, cs, :], src, ACT.Copy,
                                                   scale=scale if which == 0 else 1.0)
                    else:
                        for i, c in enumerate(chunks):
                            ins = nc.scalar.activation(dst[:, parity, c, :], front[slot][:, i * T:(i + 1) * T],
                                                       ACT.Identity, bias=bqk[:, which, c:c + 1],
                                                       scale=scale if which == 0 else 1.0)
                    ins.then_inc(front_free[slot].sem, 1)

            def exps(k, g):
                act.wait_ge(shifted.sem, at(shifted, k, g + 1))
                flat = s[:, g].rearrange("p r c k -> p (r c k)")
                nc.scalar.activation(flat, flat, ACT.Exp).then_inc(probs_ready.sem, 1)

            def copy_probsT(k, g):
                for c in range(C):
                    n = g * BG + c
                    act.wait_ge(back_full[n % 2].sem, at(back_full[n % 2], k, n // 2 + 1))
                    nc.scalar.activation(probsT[:, g, c].rearrange("p r k -> p (r k)"), back[n % 2][:, :],
                                         ACT.Copy).then_inc(back_free[n % 2].sem, 1)

            def high_o(k, g):
                n = g * BG + C
                act.wait_ge(back_full[n % 2].sem, at(back_full[n % 2], k, n // 2 + 1))
                nc.scalar.activation(oT.hi[:, g].rearrange("p c t -> p (c t)"), back[n % 2][:, 0:D],
                                     ACT.Copy).then_inc(oT_hi_ready.sem, 1)

            norm.act_rstd(act, 0)
            if not is_first:
                nc.scalar.activation(bqk[:, 0, :], bqk_raw[:, 0, :], ACT.Copy, scale=scale)
                nc.scalar.activation(bqk[:, 1, :], bqk_raw[:, 1, :], ACT.Copy).then_inc(bqk_set.sem, 1)
            high_h(0)
            if not is_first:
                act.wait_ge(bqk_set.sem, bqk_set.base + 1)
            copy_qk(0, 0, 0, qT, 2)
            norm.act_rstd(act, 1)
            copy_qk(0, 0, 1, kT, 4)

            for k, parity, more in steps(act, NP):
                high_h(k + 1)
                copy_qk(k + 1, 1 - parity, 0, qT, 2)
                copy_qk(k + 1, 1 - parity, 1, kT, 4)
                exps(k, 0)
                copy_probsT(k, 0)
                exps(k, 1)
                if is_first:
                    high_o(k, 0)
                if more:
                    norm.act_rstd(act, k + 2)
                copy_probsT(k, 1)
                if is_first:
                    high_o(k, 1)

            k = NP - 1
            exps(k, 0)
            copy_probsT(k, 0)
            exps(k, 1)
            if is_first:
                high_o(k, 0)
            copy_probsT(k, 1)
            if is_first:
                high_o(k, 1)

        @block.vector
        def _(dve):
            def low_h(k):
                for n, chunks in enumerate(((0, 1), (2,))):
                    dve.wait_ge(hi_ready.sem, at(hi_ready, k, n + 1))
                    cs = slice(chunks[0], chunks[-1] + 1)
                    nc.vector.tensor_tensor(hT.lo[:, cs, :], hT_f[:, cs, :], hT.hi[:, cs, :].bitcast(F32),
                                            ALU.subtract).then_inc(lo_ready.sem, 1)

            def take_scores(k, parity, g):
                if g == 0:
                    dve.wait_ge(bias_ready.sem, at(bias_ready, k, 1))
                dve.wait_ge(s_full.sem, at(s_full, k, g + 1))
                dve.wait_ge(o_full.sem, at(o_full, k - 1, g + 1))
                b = bias[:, parity, g, :]
                nc.vector.tensor_tensor(s[:, g], S, b[:, None, None, :].to_broadcast([P, R, C, P]), ALU.add
                                        ).then_inc(s_taken.sem, 1)

            def shift_scores(k, g):
                flat = s[:, g].rearrange("p r c k -> p (r c) k")
                dve.wait_ge(s_taken.sem, at(s_taken, k, g + 1))
                nc.vector.tensor_reduce(s_max[:, g, :], flat, AX.X, ALU.max).then_inc(max_ready.sem, 1)
                if is_first:
                    nc.vector.tensor_reduce(s_abs[:, g, :], flat, AX.X, ALU.max, apply_absolute_value=True
                                            ).then_inc(abs_ready.sem, 1)
                read = abs_ready if is_first else max_ready
                dve.wait_ge(read.sem, at(read, k, g + 1))
                nc.vector.tensor_tensor(flat, flat, s_max[:, g, :, None].to_broadcast([P, HEADS, P]),
                                        ALU.subtract).then_inc(shifted.sem, 1)

            def take_values(k, parity, g):
                dve.wait_ge(front_full[g].sem, at(front_full[g], k, FI))
                nc.vector.tensor_tensor(v[:, parity, g, :, 0:HD],
                                        front[g][:, 0:D].rearrange("p (h e) -> p h e", e=HD),
                                        bv[:, :].rearrange("p (h e) -> p h e", e=HD), ALU.add
                                        ).then_inc(front_free[g].sem, 1)

            def normalise(k, g):
                dve.wait_ge(o_full.sem, at(o_full, k, g + 1))
                sums = O[:, :, :, HD].rearrange("p r c -> p c r")
                nc.vector.reciprocal(rsum[:, g], sums).then_inc(rsum_ready.sem, 1)
                dve.wait_ge(rsum_ready.sem, at(rsum_ready, k, g + 1))
                f = rsum
                if is_first:
                    f = factor
                    dve.wait_ge(abs_ready.sem, at(abs_ready, k, g + 1))
                    nc.vector.scalar_tensor_tensor(
                        out=factor[:, g], in0=s_abs[:, g, :].rearrange("p (r c) -> p c r", c=C), scalar=0.0,
                        in1=rsum[:, g], op0=ALU.not_equal, op1=ALU.mult).then_inc(factor_ready.sem, 1)
                    dve.wait_ge(factor_ready.sem, at(factor_ready, k, g + 1))
                nc.vector.tensor_tensor(o[:, g], O[:, :, :, 0:HD].rearrange("p r c e -> p c r e"),
                                        f[:, g, :, :, None].to_broadcast([P, C, R, HD]), ALU.mult
                                        ).then_inc(o_ready.sem, 1)

            def low_o(k, g):
                n = g * BG + C
                dve.wait_ge(oT_hi_ready.sem, at(oT_hi_ready, k, g + 1))
                nc.vector.tensor_tensor(oT.lo[:, g].rearrange("p c t -> p (c t)"), back[n % 2][:, 0:D],
                                        oT.hi[:, g].rearrange("p c t -> p (c t)").bitcast(F32), ALU.subtract
                                        ).then_inc(back_free[n % 2].sem, 1)

            def update_x(k, g):
                xg = x.graph(k, g)
                if is_first:
                    n = g * BG + C + 1
                    dve.wait_ge(xb_ready.sem, at(xb_ready, k, g + 1))
                    dve.wait_ge(back_full[n % 2].sem, at(back_full[n % 2], k, n // 2 + 1))
                    nc.vector.tensor_tensor(xg, back[n % 2][:, 0:D], xb[:, g, :], ALU.add
                                            ).then_inc(back_free[n % 2].sem, 1)
                else:
                    dve.wait_ge(o_ready.sem, at(o_ready, k, g + 1))
                    nc.vector.tensor_tensor(xg, xg, o[:, g].rearrange("p c r e -> p (c r e)"), ALU.add
                                            ).then_inc(x_done.sem, 1)

            norm.dve_moments(dve, 0, 0)
            norm.dve_xhat(dve, 0)
            norm.dve_moments(dve, 1, 1)
            low_h(0)
            norm.dve_xhat(dve, 1)
            dve.wait_ge(ones_set.sem, ones_set.base + 1)
            take_values(0, 0, 0)
            take_values(0, 0, 1)

            for k, parity, more in steps(dve, NP):
                low_h(k + 1)
                take_scores(k, parity, 0)
                shift_scores(k, 0)
                take_scores(k, parity, 1)
                take_values(k + 1, 1 - parity, 0)
                take_values(k + 1, 1 - parity, 1)
                shift_scores(k, 1)
                if more:
                    norm.dve_moments(dve, k + 2, parity)
                normalise(k, 0)
                if is_first:
                    low_o(k, 0)
                if more:
                    norm.dve_xhat(dve, k + 2)
                update_x(k, 0)
                normalise(k, 1)
                if is_first:
                    low_o(k, 1)
                update_x(k, 1)

            k = NP - 1
            for g in range(G):
                take_scores(k, 1, g)
                shift_scores(k, g)
            for g in range(G):
                normalise(k, g)
                if is_first:
                    low_o(k, g)
                update_x(k, g)

        @block.gpsimd
        def _(pool):
            def add_bo(k, parity):
                x.wait_loaded(pool, k, parity)
                for g in range(G):
                    n = g * BG + C + 1
                    pool.wait_ge(back_free[n % 2].sem, at(back_free[n % 2], k - 1, n // 2 + 1))
                    nc.gpsimd.tensor_tensor(xb[:, g, :], x.graph(k, g), bo[:, :],
                                            ALU.add).then_inc(xb_ready.sem, 1)

            def make_bias(k, parity):
                wait_in(pool, adj_in, k, parity)
                pool.wait_ge(s_taken.sem, at(s_taken, k - 1, 0))
                pool.sem_inc(core.unwatched.sem, 1)
                if is_first:
                    nc.gpsimd.tensor_scalar(bias[:, parity], adj[:, parity], 2.0, 0.0, ALU.mult, ALU.add
                                            ).then_inc(bias_ready.sem, 1)
                    return
                nc.gpsimd.tensor_scalar(bias[:, parity], adj[:, parity], 0.0, -9e15, ALU.is_le, ALU.mult
                                        ).then_inc(bias_step.sem, 1)
                nc.gpsimd.tensor_scalar(adj[:, parity], adj[:, parity], beta[:, 0:1], 0.0, ALU.mult, ALU.add
                                        ).then_inc(bias_step.sem, 1)
                pool.wait_ge(bias_step.sem, at(bias_step, k, 2))
                nc.gpsimd.tensor_tensor(bias[:, parity], bias[:, parity], adj[:, parity], ALU.add
                                        ).then_inc(bias_ready.sem, 1)

            nc.gpsimd.memset(v[:, :, :, :, HD:HP], 1.0).then_inc(ones_set.sem, 1)
            make_bias(0, 0)

            for k, parity, more in steps(pool, NP):
                make_bias(k + 1, 1 - parity)
                if is_first:
                    add_bo(k, parity)

            if is_first:
                add_bo(NP - 1, 1)


    sig.end_phase()



class Stage:

    def __init__(self, nc, core, ctx, kind, index, weights, biases, norm):
        self.nc, self.core, self.kind, self.index, self.norm = nc, core, kind, index, norm
        self.weights, self.biases = weights, biases
        tag = f"{'first' if index == 0 else 'second'}"
        self.name = f"l{kind}_{tag}"
        sig = lambda n, per: core.signals(f"{tag}_{n}", per)

        def sb(name, shape, dt=F32):
            return ctx.enter_context(nc.sbuf_tensor(f"{self.name}_{name}", shape, dt))

        self.hT_f = sb("hT", [P, C, T])
        self.hT = Split(sb("hT_hi", [P, C, T], F32R), sb("hT_lo", [P, C, T], F32R))
        self.adj = sb("adj", [P, 2, G, P])
        self.c = sb("c", [P, G, D])
        self.t = sb("t", [P, G, D])
        self.stats = sb("stats", [P, G, 6])
        self.moments = sb("moments", [P, G, 2])
        self.log = sb("log", [P, G])
        self.rstd = sb("rstd", [P, G])
        self.r = sb("r", [P, G])
        self.q = sb("q", [P, G])
        if kind == 1:
            self.left = sb("hl", [P, G, D])
            self.right = sb("hr", [P, G, D])
            self.self_ = sb("hs", [P, G, D])
            self.self_bias = sb("hs_bias", [P, G, D])
            self.e = sb("e", [P, G, P])
            self.E = sb("delta", [P, G, P])
            self.ET = sb("deltaT", [P, G, 2, P])
            self.sum_e = sb("sum_e", [P, G])
            self.sum_d = sb("sum_d", [P, G])
            self.diag = sb("diag", [P, G])
            self.diag_r = sb("diag_r", [P, G])
            self.row_max = sb("row_max", [P, G])
            self.shift = sb("shift", [P, G])
            self.junk = sb("junk", [P, G, P])
        else:
            self.adjT = sb("adjT", [P, 2, G, P])
            self.mT = sb("mT", [P, 2, C, T])
            self.lin = sb("lin", [P, G, D + 1])
            self.w = sb("w", [P, 2, G, 2, P])
            self.uw = sb("uw", [P, G, 2, P])
            self.u = sb("u", [P, G, P])
            self.e = sb("e", [P, G, P])
            self.E = sb("deltaT", [P, G, P])
            self.std = sb("std", [P, G])
        ps = lambda n: ctx.enter_context(nc.psum_tensor(f"{self.name}_{n}", [P, BANK], F32))
        self.ring = [ps("ring0"), ps("ring1")]
        self.U = ps("U")
        self.ctx = ps("ctx")

        self.full = [sig(f"ring_full{j}", 4) for j in range(2)]
        self.free = [sig(f"ring_free{j}", 4) for j in range(2)]
        self.adj_in = [sig(f"adj_in{j}", 8 * kind) for j in range(2)]
        self.hi_ready = sig("hi_ready", 1)
        self.lo_ready = sig("lo_ready", 1)
        self.u_full = sig("u_full", 1)
        self.shift_ready = sig("shift_ready", 1)
        self.e_ready = sig("e_ready", G if kind == 1 else 1)
        self.E_ready = sig("delta_ready", G if kind == 1 else 1)
        if kind == 1:
            self.ET_full = sig("deltaT_full", 1)
            self.ET_ready = sig("deltaT_ready", 1)
            self.diag_ready = sig("diag_ready", 1)
            self.self_bias_ready = sig("self_bias_ready", G)
            self.self_ready = sig("self_ready", G)
        else:
            self.w_ready = sig("w_ready", 2)
        self.ctx_full = sig("ctx_full", G)
        self.ctx_free = sig("ctx_free", G)
        self.var_ready = sig("var_ready", G)
        self.log_done = sig("log_done", 1)
        self.rstd_ready = sig("rstd_ready", 1)
        self.t_ready = sig("t_ready", G)
        self.stats_done = sig("stats_done", G)
        self.q_done = sig("q_done", kind)
        self.r_done = sig("r_done", kind)
        if kind == 1:
            self.max_done = sig("max_done", 1)
            self.diag_done = sig("diag_done", G)
        else:
            self.uw_done = sig("uw_done", 1)
            self.std_done = sig("std_done", 1)
            self.inverse_done = sig("inverse_done", 1)
        if index == 1:
            self.final_link = sig("final_link", 3)
            self.final_done = sig("final_done", 1)


    def take(self, pe, k, n):
        pe.wait_ge(self.free[n % 2].sem, at(self.free[n % 2], k, n // 2))
        return self.ring[n % 2]

    def h_copied(self, engine, k):
        for slot in range(2):
            engine.wait_ge(self.free[slot].sem, at(self.free[slot], k, 1))

    def adj_loaded(self, engine, k, parity):
        engine.wait_ge(self.adj_in[parity].sem, dma_at(self.adj_in[parity], k, parity))


    def load_adj(self, sp, k, parity):
        sp.wait_ge(self.E_ready.sem, at(self.E_ready, k - 1, 0))
        sp.sem_inc(self.core.unwatched.sem, 1)
        sp.dma_start(self.adj[:, parity, :, :],
                     self.core.dram["adj"][bass.ds(G * k, G), :, :].rearrange("g p d -> p g d")
                     ).then_inc(self.adj_in[parity].sem, 16)
        if self.kind == 2:
            sp.dma_start(self.adjT[:, parity, :, :],
                         self.core.dram["adjT"][bass.ds(G * k, G), :, :].rearrange("g p d -> p g d")
                         ).then_inc(self.adj_in[parity].sem, 16)


    def pe_transpose_h(self, pe, k):
        nc = self.nc
        src, ready = self.source
        pe.wait_ge(ready.sem, at(ready, k, G))
        for n, chunks in enumerate(((0, 1), (2,))):
            slot = self.take(pe, k, n)
            for i, c in enumerate(chunks):
                for g in range(G):
                    ins = nc.tensor.transpose(slot[:, i * T + g * P:i * T + (g + 1) * P],
                                              src[:, g, c * P:(c + 1) * P], self.core.ident[:, :])
            ins.then_inc(self.full[n % 2].sem, 1)

    def pe_linear(self, pe, k, w, g, n):
        slot = self.take(pe, k, n)
        t = slice(g * P, (g + 1) * P)
        product(self.nc, slot[:, 0:D], [(self.hT.hi[:, c, t], self.hT.lo[:, c, t]) for c in range(C)],
                [(w.hi[:, c, :], w.lo[:, c, :]) for c in range(C)]).then_inc(self.full[n % 2].sem, 1)

    def pe_messages(self, pe, k, w, n0):
        nc = self.nc
        for n, chunks in enumerate(((0, 1), (2,))):
            slot = self.take(pe, k, n0 + n)
            for i, o_c in enumerate(chunks):
                f = slice(o_c * P, (o_c + 1) * P)
                ins = product(nc, slot[:, i * T:(i + 1) * T],
                              [(w.hi[:, c, f], w.lo[:, c, f]) for c in range(C)],
                              [(self.hT.hi[:, c, :], self.hT.lo[:, c, :]) for c in range(C)])
            ins.then_inc(self.full[(n0 + n) % 2].sem, 1)


    def pe_gram(self, pe, k):
        nc = self.nc
        self.h_copied(pe, k)
        pe.wait_ge(self.E_ready.sem, at(self.E_ready, k, 0))
        for g in range(G):
            t = slice(g * P, (g + 1) * P)
            for c in range(C):
                ins = nc.tensor.matmul(self.U[:, t], self.hT_f[:, c, t], self.hT_f[:, c, t],
                                       start=c == 0, stop=c == C - 1)
        ins.then_inc(self.u_full.sem, 1)

    def pe_linears(self, pe, k, g):
        if g == 0:
            pe.wait_ge(self.lo_ready.sem, at(self.lo_ready, k, 1))
        for i in range(3):
            self.pe_linear(pe, k, self.weights[i], g, 2 + 3 * g + i)

    def pe_transpose_delta(self, pe, k):
        nc = self.nc
        pe.wait_ge(self.E_ready.sem, at(self.E_ready, k, G))
        pe.wait_ge(self.ET_ready.sem, at(self.ET_ready, k, 0))
        for g in range(G):
            ins = nc.tensor.transpose(self.U[:, T + g * P:T + (g + 1) * P], self.E[:, g, :], self.core.ident[:, :])
        ins.then_inc(self.ET_full.sem, 1)

    def pe_context(self, pe, k, g):
        nc = self.nc
        if g == 0:
            pe.wait_ge(self.ET_ready.sem, at(self.ET_ready, k, 1))
        for n in (2 + 3 * g, 3 + 3 * g):
            pe.wait_ge(self.free[n % 2].sem, at(self.free[n % 2], k, n // 2 + 1))
        pe.wait_ge(self.ctx_free.sem, at(self.ctx_free, k, g))
        nc.tensor.matmul(self.ctx[:, 0:D], self.ET[:, g, 0, :], self.left[:, g, :], start=True, stop=False)
        nc.tensor.matmul(self.ctx[:, 0:D], self.ET[:, g, 1, :], self.right[:, g, :], start=False, stop=True
                         ).then_inc(self.ctx_full.sem, 1)


    def pe_scores(self, pe, k):
        nc = self.nc
        self.h_copied(pe, k)
        for n in (4, 5):
            pe.wait_ge(self.free[n % 2].sem, at(self.free[n % 2], k, n // 2 + 1))
        pe.wait_ge(self.shift_ready.sem, at(self.shift_ready, k, 0))
        for g in range(G):
            t = slice(g * P, (g + 1) * P)
            for side in range(2):
                out = self.U[:, (2 * g + side) * P:(2 * g + side + 1) * P]
                for c in range(C):
                    ins = nc.tensor.matmul(out, self.mT[:, side, c, t], self.hT_f[:, c, t],
                                           start=c == 0, stop=c == C - 1)
        ins.then_inc(self.u_full.sem, 1)

    def pe_gather(self, pe, k, g):
        nc = self.nc
        if g == 0:
            pe.wait_ge(self.E_ready.sem, at(self.E_ready, k, 1))
        n = 6 + g
        pe.wait_ge(self.free[n % 2].sem, at(self.free[n % 2], k, n // 2 + 1))
        pe.wait_ge(self.ctx_free.sem, at(self.ctx_free, k, g))
        nc.tensor.matmul(self.ctx[:, 0:D + 1], self.E[:, g, :], self.lin[:, g, :], start=True, stop=True
                         ).then_inc(self.ctx_full.sem, 1)


    def act_h(self, act, k):
        nc = self.nc
        for n, chunks in enumerate(((0, 1), (2,))):
            act.wait_ge(self.full[n].sem, at(self.full[n], k, 1))
            for i, c in enumerate(chunks):
                src = self.ring[n][:, i * T:(i + 1) * T]
                if self.index == 0:
                    ins = nc.scalar.activation(self.hT_f[:, c, :], src, ACT.Relu)
                else:
                    ins = nc.scalar.activation(self.hT_f[:, c, :], src, ACT.Relu, bias=self.betaT[:, c:c + 1],
                                               scale=self.gammaT[:, c:c + 1])
            ins.then_inc(self.free[n].sem, 1)
        self.h_copied(act, k)
        nc.scalar.activation(self.hT.hi[:, :, :], self.hT_f[:, :, :], ACT.Copy).then_inc(self.hi_ready.sem, 1)

    def act_exps(self, act, k):
        nc = self.nc
        act.wait_ge(self.shift_ready.sem, at(self.shift_ready, k, 1))
        for g in range(G):
            nc.scalar.activation(self.e[:, g, :], self.U[:, g * P:(g + 1) * P], ACT.Exp,
                                 bias=self.shift[:, g:g + 1], scale=D ** -0.5, accum_out=self.sum_e[:, g:g + 1]
                                 ).then_inc(self.e_ready.sem, 1)

    def act_self(self, act, k, g):
        nc = self.nc
        n = 4 + 3 * g
        if g == 0:
            act.wait_ge(self.diag_ready.sem, at(self.diag_ready, k, 1))
        act.wait_ge(self.full[n % 2].sem, at(self.full[n % 2], k, n // 2 + 1))
        nc.scalar.activation(self.self_[:, g, :], self.ring[n % 2][:, 0:D], ACT.Copy,
                             scale=self.diag_r[:, g:g + 1]).then_inc(self.free[n % 2].sem, 1)

    def act_messages(self, act, k, side):
        nc = self.nc
        for n, chunks in enumerate(((0, 1), (2,))):
            m = 2 + 2 * side + n
            act.wait_ge(self.full[m % 2].sem, at(self.full[m % 2], k, m // 2 + 1))
            cs = slice(chunks[0], chunks[-1] + 1)
            nc.scalar.activation(self.mT[:, side, cs, :],
                                 self.ring[m % 2][:, 0:len(chunks) * T].rearrange("p (c t) -> p c t", t=T),
                                 ACT.Copy).then_inc(self.free[m % 2].sem, 1)

    def act_exp_u(self, act, k):
        nc = self.nc
        act.wait_ge(self.shift_ready.sem, at(self.shift_ready, k, 1))
        nc.scalar.activation(self.e[:, :, :], self.u[:, :, :], ACT.Exp, scale=D ** -0.5).then_inc(self.e_ready.sem, 1)

    def act_rstd(self, act, k):
        nc = self.nc
        act.wait_ge(self.var_ready.sem, at(self.var_ready, k, G))
        if self.kind == 1:
            nc.scalar.activation(self.log[:, :], self.moments[:, :, 1], ACT.Ln, bias=self.core.eps_l1[:, :]
                                 ).then_inc(self.log_done.sem, 1)
            act.wait_ge(self.log_done.sem, at(self.log_done, k, 1))
            nc.scalar.activation(self.rstd[:, :], self.log[:, :], ACT.Exp, scale=-0.5).then_inc(self.rstd_ready.sem, 1)
        else:
            nc.scalar.activation(self.log[:, :], self.moments[:, :, 1], ACT.Ln, bias=self.core.eps_l2[:, :],
                                 scale=D / (D - 1)).then_inc(self.log_done.sem, 1)
            act.wait_ge(self.log_done.sem, at(self.log_done, k, 1))
            nc.scalar.activation(self.std[:, :], self.log[:, :], ACT.Exp, scale=0.5).then_inc(self.rstd_ready.sem, 1)


    def dve_low_h(self, dve, k):
        dve.wait_ge(self.hi_ready.sem, at(self.hi_ready, k, 1))
        self.nc.vector.tensor_tensor(self.hT.lo[:, :, :], self.hT_f[:, :, :], self.hT.hi[:, :, :].bitcast(F32),
                                     ALU.subtract).then_inc(self.lo_ready.sem, 1)

    def dve_shift(self, dve, k):
        nc = self.nc
        dve.wait_ge(self.u_full.sem, at(self.u_full, k, 1))
        nc.vector.tensor_reduce(self.row_max[:, :], self.U[:, 0:T].rearrange("p (g j) -> p g j", g=G),
                                AX.X, ALU.max).then_inc(self.max_done.sem, 1)
        dve.wait_ge(self.max_done.sem, at(self.max_done, k, 1))
        nc.vector.tensor_scalar(self.shift[:, :], self.row_max[:, :], -(D ** -0.5), None, ALU.mult
                                ).then_inc(self.shift_ready.sem, 1)

    def dve_delta(self, dve, k, parity):
        nc = self.nc
        self.adj_loaded(dve, k, parity)
        for g in range(G):
            dve.wait_ge(self.e_ready.sem, at(self.e_ready, k, g + 1))
            nc.vector.scalar_tensor_tensor(out=self.E[:, g, :], in0=self.e[:, g, :], scalar=1.0,
                                           in1=self.adj[:, parity, g, :], op0=ALU.mult, op1=ALU.mult,
                                           accum_out=self.sum_d[:, g:g + 1]).then_inc(self.E_ready.sem, 1)
        dve.wait_ge(self.E_ready.sem, at(self.E_ready, k, G))
        nc.vector.scalar_tensor_tensor(out=self.q[:, :], in0=self.sum_e[:, :], scalar=1e-10, in1=self.sum_d[:, :],
                                       op0=ALU.mult, op1=ALU.add).then_inc(self.q_done.sem, 1)
        for g in range(G):
            nc.vector.scalar_tensor_tensor(out=self.junk[:, g, :], in0=self.E[:, g, :], scalar=1.0,
                                           in1=self.core.ident[:, :], op0=ALU.mult, op1=ALU.mult,
                                           accum_out=self.diag[:, g:g + 1]).then_inc(self.diag_done.sem, 1)
        dve.wait_ge(self.q_done.sem, at(self.q_done, k, 1))
        nc.vector.reciprocal(self.r[:, :], self.q[:, :]).then_inc(self.r_done.sem, 1)
        dve.wait_ge(self.diag_done.sem, at(self.diag_done, k, G))
        dve.wait_ge(self.r_done.sem, at(self.r_done, k, 1))
        nc.vector.tensor_tensor(self.diag_r[:, :], self.diag[:, :], self.r[:, :], ALU.mult
                                ).then_inc(self.diag_ready.sem, 1)

    def dve_sides(self, dve, k, g):
        nc = self.nc
        for i, (dst, b) in enumerate(((self.left, self.biases[0]), (self.right, self.biases[1]))):
            n = 2 + 3 * g + i
            dve.wait_ge(self.full[n % 2].sem, at(self.full[n % 2], k, n // 2 + 1))
            nc.vector.tensor_tensor(dst[:, g, :], self.ring[n % 2][:, 0:D], b[:, :], ALU.add
                                    ).then_inc(self.free[n % 2].sem, 1)

    def dve_triangles(self, dve, k):
        nc = self.nc
        dve.wait_ge(self.ET_full.sem, at(self.ET_full, k, 1))
        src = self.U[:, T:2 * T].rearrange("p (g i) -> p g i", g=G)[:, :, None, :].to_broadcast([P, G, 2, P])
        mask = self.core.triangles[:, None, :, :].to_broadcast([P, G, 2, P])
        nc.vector.tensor_tensor(self.ET[:, :, :, :], src, mask, ALU.mult).then_inc(self.ET_ready.sem, 1)

    def dve_weighted(self, dve, k, parity):
        nc = self.nc
        dve.wait_ge(self.w_ready.sem, at(self.w_ready, k, 2))
        dve.wait_ge(self.u_full.sem, at(self.u_full, k, 1))
        nc.vector.tensor_tensor(self.uw[:, :, :, :].rearrange("p g s i -> p (g s i)"), self.U[:, :],
                                self.w[:, parity].rearrange("p g s i -> p (g s i)"), ALU.mult
                                ).then_inc(self.uw_done.sem, 1)
        dve.wait_ge(self.uw_done.sem, at(self.uw_done, k, 1))
        nc.vector.tensor_tensor(self.u[:, :, :], self.uw[:, :, 0, :], self.uw[:, :, 1, :], ALU.add
                                ).then_inc(self.shift_ready.sem, 1)

    def dve_delta_t(self, dve, k, parity):
        nc = self.nc
        dve.wait_ge(self.e_ready.sem, at(self.e_ready, k, 1))
        nc.vector.tensor_tensor(self.E[:, :, :], self.e[:, :, :], self.adjT[:, parity], ALU.mult
                                ).then_inc(self.E_ready.sem, 1)

    def dve_lin(self, dve, k, g):
        nc = self.nc
        n = 6 + g
        dve.wait_ge(self.full[n % 2].sem, at(self.full[n % 2], k, n // 2 + 1))
        nc.vector.tensor_tensor(self.lin[:, g, 0:D], self.ring[n % 2][:, 0:D], self.biases[0][:, :], ALU.add
                                ).then_inc(self.free[n % 2].sem, 1)

    def dve_context(self, dve, k):
        nc = self.nc
        for g in range(G):
            dve.wait_ge(self.ctx_full.sem, at(self.ctx_full, k, g + 1))
            if self.kind == 1:
                dve.wait_ge(self.self_ready.sem, at(self.self_ready, k, g + 1))
                ins = nc.vector.scalar_tensor_tensor(out=self.c[:, g, :], in0=self.ctx[:, 0:D], scalar=self.r[:, g:g + 1],
                                                     in1=self.self_[:, g, :], op0=ALU.mult, op1=ALU.add)
            else:
                nc.vector.tensor_scalar(self.q[:, g:g + 1], self.ctx[:, D:D + 1], 1e-10, None, ALU.add
                                        ).then_inc(self.q_done.sem, 1)
                dve.wait_ge(self.q_done.sem, at(self.q_done, k, g + 1))
                nc.vector.reciprocal(self.r[:, g:g + 1], self.q[:, g:g + 1]).then_inc(self.r_done.sem, 1)
                dve.wait_ge(self.r_done.sem, at(self.r_done, k, g + 1))
                ins = nc.vector.tensor_scalar(self.c[:, g, :], self.ctx[:, 0:D], self.r[:, g:g + 1], None, ALU.mult)
            ins.then_inc(self.ctx_free.sem, 1)
            dve.wait_ge(self.ctx_free.sem, at(self.ctx_free, k, g + 1))
            nc.vector.bn_stats(self.stats[:, g, :], self.c[:, g, :]).then_inc(self.stats_done.sem, 1)
            dve.wait_ge(self.stats_done.sem, at(self.stats_done, k, g + 1))
            dve.sem_inc(self.core.unwatched.sem, 1)
            nc.vector.bn_aggr(self.moments[:, g, :], self.stats[:, g, :]).then_inc(self.var_ready.sem, 1)

    def dve_normalise(self, dve, k):
        nc = self.nc
        dve.wait_ge(self.rstd_ready.sem, at(self.rstd_ready, k, 1))
        if self.index == 1:
            dve.wait_ge(self.final_done.sem, at(self.final_done, k, 0))
        if self.kind == 2:
            nc.vector.tensor_scalar(self.std[:, :], self.std[:, :], 1e-3, None, ALU.add).then_inc(self.std_done.sem, 1)
            dve.wait_ge(self.std_done.sem, at(self.std_done, k, 1))
            nc.vector.reciprocal(self.rstd[:, :], self.std[:, :]).then_inc(self.inverse_done.sem, 1)
            dve.wait_ge(self.inverse_done.sem, at(self.inverse_done, k, 1))
        for g in range(G):
            nc.vector.tensor_scalar(self.t[:, g, :], self.c[:, g, :], self.moments[:, g, 0:1], self.rstd[:, g:g + 1],
                                    ALU.subtract, ALU.mult).then_inc(self.t_ready.sem, 1)


    def pool_self(self, pool, k):
        nc = self.nc
        pool.wait_ge(self.diag_ready.sem, at(self.diag_ready, k, 1))
        pool.sem_inc(self.core.unwatched.sem, 1)
        for g in range(G):
            nc.gpsimd.tensor_scalar(self.self_bias[:, g, :], self.biases[2][:, :], self.diag_r[:, g:g + 1], 0.0,
                                    ALU.mult, ALU.add).then_inc(self.self_bias_ready.sem, 1)
        for g in range(G):
            n = 4 + 3 * g
            pool.wait_ge(self.self_bias_ready.sem, at(self.self_bias_ready, k, g + 1))
            pool.wait_ge(self.free[n % 2].sem, at(self.free[n % 2], k, n // 2 + 1))
            nc.gpsimd.tensor_tensor(self.self_[:, g, :], self.self_[:, g, :], self.self_bias[:, g, :], ALU.add
                                    ).then_inc(self.self_ready.sem, 1)

    def pool_w(self, pool, k, parity):
        nc = self.nc
        self.adj_loaded(pool, k, parity)
        pool.wait_ge(self.uw_done.sem, at(self.uw_done, k - 1, 0))
        pool.sem_inc(self.core.unwatched.sem, 1)
        nc.gpsimd.affine_select(out=self.w[:, parity, :, 0, :], in_=self.adjT[:, parity], compare_op=ALU.is_ge, fill=0.0,
                                base=0, pattern=[[0, G], [-1, P]], channel_multiplier=1
                                ).then_inc(self.w_ready.sem, 1)
        nc.gpsimd.affine_select(out=self.w[:, parity, :, 1, :], in_=self.adj[:, parity], compare_op=ALU.is_gt, fill=0.0,
                                base=0, pattern=[[0, G], [1, P]], channel_multiplier=-1
                                ).then_inc(self.w_ready.sem, 1)

    def pool_final(self, pool, k):
        nc = self.nc
        pool.wait_ge(self.t_ready.sem, at(self.t_ready, k, G))
        wide = [P, G, D]
        x = self.x.pair(k)
        nc.gpsimd.tensor_tensor(self.t[:, :, :], self.t[:, :, :], self.gamma[:, None, :].to_broadcast(wide), ALU.mult
                                ).then_inc(self.final_link.sem, 1)
        pool.wait_ge(self.final_link.sem, at(self.final_link, k, 1))
        nc.gpsimd.tensor_tensor(self.t[:, :, :], self.t[:, :, :], self.beta[:, None, :].to_broadcast(wide), ALU.add
                                ).then_inc(self.final_link.sem, 1)
        pool.wait_ge(self.final_link.sem, at(self.final_link, k, 2))
        pool.sem_inc(self.core.unwatched.sem, 1)
        nc.gpsimd.tensor_scalar(self.t[:, :, :], self.t[:, :, :], 0.0, 0.0, ALU.max, ALU.add
                                ).then_inc(self.final_link.sem, 1)
        pool.wait_ge(self.final_link.sem, at(self.final_link, k, 3))
        nc.gpsimd.tensor_tensor(x, x, self.t[:, :, :], ALU.add).then_inc(self.final_done.sem, 1)


def graph_phase(nc, core, kind):
    NP = core.pairs
    names = {1: ["l1_wl{}", "l1_wr{}", "l1_ws{}"], 2: ["l2_left{}", "l2_right{}", "l2_lin{}"]}[kind]
    bias_names = {1: ["l1_bl{}", "l1_br{}", "l1_bs{}"], 2: ["l2_b{}"]}[kind]
    with ExitStack() as ctx:
        def sb(name, shape, dt=F32):
            return ctx.enter_context(nc.sbuf_tensor(f"g{kind}_{name}", shape, dt))

        biases = [[sb(b.format(j), [P, D]) for b in bias_names] for j in range(2)]
        gammaT, betaT = sb("gammaT", [P, C]), sb("betaT", [P, C])
        gamma, beta = sb("gamma", [P, D]), sb("beta", [P, D])
        dram = core.dram
        consts = [(biases[j][i][:, :], dram[b.format(j)].partition_broadcast(P))
                  for j in range(2) for i, b in enumerate(bias_names)]
        consts += [(gammaT[:, :], dram[f"l{kind}_gammaT"]), (betaT[:, :], dram[f"l{kind}_betaT"]),
                   (gamma[:, :], dram[f"l{kind}_gamma"].partition_broadcast(P)),
                   (beta[:, :], dram[f"l{kind}_beta"].partition_broadcast(P))]
        weights = load_weights(nc, core, ctx, [n.format(j) for j in range(2) for n in names], consts)
        x = Residual(nc, core, ctx, f"l{kind}", dram["x_mid"], dram["x_mid"])
        norm = InputNorm(nc, core, ctx, f"l{kind}", x)
        A = Stage(nc, core, ctx, kind, 0, weights[:3], biases[0], norm)
        B = Stage(nc, core, ctx, kind, 1, weights[3:], biases[1], norm)
        A.source = (norm.xhat, norm.ready)
        B.source = (A.t, A.t_ready)
        B.x = x
        B.gammaT, B.betaT, B.gamma, B.beta = gammaT, betaT, gamma, beta
        core.signals.raise_fresh()
        block = ctx.enter_context(nc.Block())

        @block.sync
        def _(sp):
            for k in range(2):
                x.load(sp, norm, k, k)
            for k in range(2):
                A.load_adj(sp, k, k)
            for k in range(2):
                B.load_adj(sp, k, k)

            def store(k, parity):
                sp.wait_ge(B.final_done.sem, at(B.final_done, k, 1))
                sp.sem_inc(core.unwatched.sem, 1)
                x.store(sp, k, parity)

            for k, parity, more in steps(sp, NP):
                if more:
                    A.load_adj(sp, k + 2, parity)
                    x.load(sp, norm, k + 2, parity)
                    B.load_adj(sp, k + 2, parity)
                store(k, parity)

            store(NP - 1, 1)
            x.wait_stored(sp)

        @block.tensor
        def _(pe):
            if kind == 1:
                A.pe_transpose_h(pe, 0)
                A.pe_gram(pe, 0)
                A.pe_linears(pe, 0, 0)
                A.pe_linears(pe, 0, 1)
                A.pe_transpose_delta(pe, 0)
                A.pe_context(pe, 0, 0)
                A.pe_context(pe, 0, 1)

                for k, parity, more in steps(pe, NP):
                    A.pe_transpose_h(pe, k + 1)
                    A.pe_gram(pe, k + 1)
                    A.pe_linears(pe, k + 1, 0)
                    B.pe_transpose_h(pe, k)
                    A.pe_linears(pe, k + 1, 1)
                    B.pe_gram(pe, k)
                    A.pe_transpose_delta(pe, k + 1)
                    B.pe_linears(pe, k, 0)
                    A.pe_context(pe, k + 1, 0)
                    A.pe_context(pe, k + 1, 1)
                    B.pe_linears(pe, k, 1)
                    B.pe_transpose_delta(pe, k)
                    B.pe_context(pe, k, 0)
                    B.pe_context(pe, k, 1)

                k = NP - 1
                B.pe_transpose_h(pe, k)
                B.pe_gram(pe, k)
                B.pe_linears(pe, k, 0)
                B.pe_linears(pe, k, 1)
                B.pe_transpose_delta(pe, k)
                B.pe_context(pe, k, 0)
                B.pe_context(pe, k, 1)
            else:
                def solo(S, k):
                    S.pe_transpose_h(pe, k)
                    pe.wait_ge(S.lo_ready.sem, at(S.lo_ready, k, 1))
                    S.pe_messages(pe, k, S.weights[0], 2)
                    S.pe_messages(pe, k, S.weights[1], 4)
                    S.pe_linear(pe, k, S.weights[2], 0, 6)
                    S.pe_linear(pe, k, S.weights[2], 1, 7)
                    S.pe_scores(pe, k)
                    S.pe_gather(pe, k, 0)
                    S.pe_gather(pe, k, 1)

                solo(A, 0)

                for k, parity, more in steps(pe, NP):
                    A.pe_transpose_h(pe, k + 1)
                    pe.wait_ge(A.lo_ready.sem, at(A.lo_ready, k + 1, 1))
                    A.pe_messages(pe, k + 1, A.weights[0], 2)
                    B.pe_transpose_h(pe, k)
                    A.pe_messages(pe, k + 1, A.weights[1], 4)
                    pe.wait_ge(B.lo_ready.sem, at(B.lo_ready, k, 1))
                    B.pe_messages(pe, k, B.weights[0], 2)
                    A.pe_scores(pe, k + 1)
                    B.pe_messages(pe, k, B.weights[1], 4)
                    A.pe_linear(pe, k + 1, A.weights[2], 0, 6)
                    A.pe_linear(pe, k + 1, A.weights[2], 1, 7)
                    B.pe_scores(pe, k)
                    A.pe_gather(pe, k + 1, 0)
                    A.pe_gather(pe, k + 1, 1)
                    B.pe_linear(pe, k, B.weights[2], 0, 6)
                    B.pe_linear(pe, k, B.weights[2], 1, 7)
                    B.pe_gather(pe, k, 0)
                    B.pe_gather(pe, k, 1)

                solo(B, NP - 1)

        @block.scalar
        def _(act):
            if kind == 1:
                def solo(S, k):
                    S.act_h(act, k)
                    S.act_exps(act, k)
                    S.act_self(act, k, 0)
                    S.act_self(act, k, 1)
                    S.act_rstd(act, k)

                norm.act_rstd(act, 0)
                norm.act_rstd(act, 1)
                solo(A, 0)

                for k, parity, more in steps(act, NP):
                    A.act_h(act, k + 1)
                    A.act_exps(act, k + 1)
                    A.act_self(act, k + 1, 0)
                    B.act_h(act, k)
                    A.act_self(act, k + 1, 1)
                    B.act_exps(act, k)
                    B.act_self(act, k, 0)
                    A.act_rstd(act, k + 1)
                    if more:
                        norm.act_rstd(act, k + 2)
                    B.act_self(act, k, 1)
                    B.act_rstd(act, k)
            else:
                def solo(S, k):
                    S.act_h(act, k)
                    S.act_messages(act, k, 0)
                    S.act_messages(act, k, 1)
                    S.act_exp_u(act, k)
                    S.act_rstd(act, k)

                norm.act_rstd(act, 0)
                norm.act_rstd(act, 1)
                solo(A, 0)

                for k, parity, more in steps(act, NP):
                    A.act_h(act, k + 1)
                    A.act_messages(act, k + 1, 0)
                    B.act_h(act, k)
                    A.act_messages(act, k + 1, 1)
                    B.act_messages(act, k, 0)
                    A.act_exp_u(act, k + 1)
                    B.act_messages(act, k, 1)
                    B.act_exp_u(act, k)
                    A.act_rstd(act, k + 1)
                    if more:
                        norm.act_rstd(act, k + 2)
                    B.act_rstd(act, k)

            solo(B, NP - 1)

        @block.vector
        def _(dve):
            if kind == 1:
                def solo(S, k, parity, early):
                    S.dve_low_h(dve, k)
                    early()
                    S.dve_shift(dve, k)
                    S.dve_sides(dve, k, 0)
                    S.dve_delta(dve, k, parity)
                    S.dve_sides(dve, k, 1)
                    S.dve_triangles(dve, k)
                    S.dve_context(dve, k)
                    S.dve_normalise(dve, k)

                norm.dve_moments(dve, 0, 0)
                norm.dve_xhat(dve, 0)
                norm.dve_moments(dve, 1, 1)
                solo(A, 0, 0, lambda: norm.dve_xhat(dve, 1))

                for k, parity, more in steps(dve, NP):
                    A.dve_low_h(dve, k + 1)
                    A.dve_shift(dve, k + 1)
                    A.dve_sides(dve, k + 1, 0)
                    A.dve_delta(dve, k + 1, 1 - parity)
                    B.dve_low_h(dve, k)
                    A.dve_sides(dve, k + 1, 1)
                    B.dve_shift(dve, k)
                    A.dve_triangles(dve, k + 1)
                    B.dve_sides(dve, k, 0)
                    B.dve_delta(dve, k, parity)
                    A.dve_context(dve, k + 1)
                    if more:
                        norm.dve_moments(dve, k + 2, parity)
                    A.dve_normalise(dve, k + 1)
                    B.dve_sides(dve, k, 1)
                    if more:
                        norm.dve_xhat(dve, k + 2)
                    B.dve_triangles(dve, k)
                    B.dve_context(dve, k)
                    B.dve_normalise(dve, k)
            else:
                def solo(S, k, parity, early):
                    S.dve_low_h(dve, k)
                    early()
                    S.dve_lin(dve, k, 0)
                    S.dve_lin(dve, k, 1)
                    S.dve_weighted(dve, k, parity)
                    S.dve_delta_t(dve, k, parity)
                    S.dve_context(dve, k)
                    S.dve_normalise(dve, k)

                for S in (A, B):
                    nc.vector.memset(S.lin[:, :, D:D + 1], 1.0)
                norm.dve_moments(dve, 0, 0)
                norm.dve_xhat(dve, 0)
                norm.dve_moments(dve, 1, 1)
                solo(A, 0, 0, lambda: norm.dve_xhat(dve, 1))

                for k, parity, more in steps(dve, NP):
                    A.dve_low_h(dve, k + 1)
                    B.dve_low_h(dve, k)
                    A.dve_weighted(dve, k + 1, 1 - parity)
                    A.dve_delta_t(dve, k + 1, 1 - parity)
                    A.dve_lin(dve, k + 1, 0)
                    A.dve_lin(dve, k + 1, 1)
                    B.dve_weighted(dve, k, parity)
                    B.dve_delta_t(dve, k, parity)
                    A.dve_context(dve, k + 1)
                    if more:
                        norm.dve_moments(dve, k + 2, parity)
                    A.dve_normalise(dve, k + 1)
                    B.dve_lin(dve, k, 0)
                    B.dve_lin(dve, k, 1)
                    if more:
                        norm.dve_xhat(dve, k + 2)
                    B.dve_context(dve, k)
                    B.dve_normalise(dve, k)

            solo(B, NP - 1, 1, lambda: None)

        @block.gpsimd
        def _(pool):
            def prepare(S, k, parity):
                if kind == 1:
                    S.pool_self(pool, k)
                else:
                    S.pool_w(pool, k, parity)

            prepare(A, 0, 0)

            for k, parity, more in steps(pool, NP):
                prepare(A, k + 1, 1 - parity)
                prepare(B, k, parity)
                B.pool_final(pool, k)

            prepare(B, NP - 1, 1)
            B.pool_final(pool, NP - 1)


    core.signals.end_phase()



def graph_layers_kernel(nc, dram, graphs, phases=(0, 1, 2, 3)):
    core = Core()
    core.dram, core.pairs = dram, graphs // G
    with ExitStack() as ctx:
        def sb(name, shape, dt=F32):
            return ctx.enter_context(nc.sbuf_tensor(name, shape, dt))

        core.signals = Signals(nc, ctx, core.pairs)

        core.unwatched = core.signals.once("unwatched", 0)
        dram["x_mid"] = nc.dram_tensor("x_mid", [graphs, P, D], F32, kind="Internal").ap()
        core.ident = sb("ident", [P, P])
        core.triangles = sb("triangles", [P, 2, P])
        core.ln_eps = sb("ln_eps", [P, 1])
        core.eps_l1 = sb("eps_l1", [P, 1])
        core.eps_l2 = sb("eps_l2", [P, 1])
        filled = core.signals.once("constants_filled", 5)
        with nc.Block() as block:
            @block.gpsimd
            def _(pool):
                nc.gpsimd.memset(core.ident[:, :], 0.0).then_inc(filled.sem, 1)
                nc.gpsimd.memset(core.triangles[:, :, :], 1.0).then_inc(filled.sem, 1)
                nc.gpsimd.memset(core.ln_eps[:, :], LN_EPS)
                nc.gpsimd.memset(core.eps_l1[:, :], 1e-12)
                nc.gpsimd.memset(core.eps_l2[:, :], 1e-18)
                pool.wait_ge(filled.sem, filled.base + 2)
                nc.gpsimd.affine_select(out=core.ident[:, :], in_=core.ident[:, :], compare_op=ALU.not_equal, fill=1.0,
                                        base=0, pattern=[[-1, P]], channel_multiplier=1).then_inc(filled.sem, 1)
                nc.gpsimd.affine_select(out=core.triangles[:, 0, :], in_=core.triangles[:, 0, :],
                                        compare_op=ALU.is_gt, fill=0.0, base=0, pattern=[[-1, P]],
                                        channel_multiplier=1).then_inc(filled.sem, 1)
                nc.gpsimd.affine_select(out=core.triangles[:, 1, :], in_=core.triangles[:, 1, :],
                                        compare_op=ALU.is_gt, fill=0.0, base=0, pattern=[[1, P]],
                                        channel_multiplier=-1).then_inc(filled.sem, 1)

            @block.scalar
            def _(act):
                nc.scalar.preload_act_table_set("natural_log_exp_and_others")

        if 0 in phases:
            attention_phase(nc, core, ["l0_wq", "l0_wk", "l0_wv", "l0_wo"], ["l0_bv", "l0_bo"], True)
        if 1 in phases:
            graph_phase(nc, core, 1)
        if 2 in phases:
            graph_phase(nc, core, 2)
        if 3 in phases:
            attention_phase(nc, core, ["l3_wq", "l3_wk", "l3_wv"], ["l3_bv", "l3_bq", "l3_bk", "l3_beta"], False)


def layout(inputs):
    import numpy as np

    def chunks(w):
        return np.ascontiguousarray(w.reshape(C, P, D).transpose(1, 0, 2))

    def column(b):
        return np.ascontiguousarray(b.reshape(C, P).T)

    a = {n: np.asarray(v) for n, v in inputs.items()}
    out = {"x": a["x"], "adj": a["adj"], "adjT": np.ascontiguousarray(a["adj"].transpose(0, 2, 1))}
    for name, key in (("wq", "Wq"), ("wk", "Wk"), ("wv", "Wv"), ("wo", "Wo")):
        out[f"l0_{name}"] = chunks(a[f"L0_gnn_{key}"].T)
    out["l0_bv"], out["l0_bo"] = a["L0_gnn_bv"], a["L0_gnn_bo"]
    for j in range(2):
        for s in "lsr":
            out[f"l1_w{s}{j}"] = chunks(a[f"L1_gnn_W{s}"][j].T)
            out[f"l1_b{s}{j}"] = a[f"L1_gnn_b{s}"][j]
        for name, key in (("left", "W_left"), ("right", "W_right"), ("lin", "W_lin")):
            out[f"l2_{name}{j}"] = chunks(a[f"L2_gnn_{key}"][j].T)
        out[f"l2_b{j}"] = a["L2_gnn_b_lin"][j]
    for layer, g, b in ((1, "L1_gnn_ln_w", "L1_gnn_ln_b"), (2, "L2_gnn_ln_a", "L2_gnn_ln_b")):
        out[f"l{layer}_gammaT"], out[f"l{layer}_betaT"] = column(a[g][0]), column(a[b][0])
        out[f"l{layer}_gamma"], out[f"l{layer}_beta"] = a[g][1], a[b][1]
    for name, key in (("wq", "Wq"), ("wk", "Wk"), ("wv", "Wv")):
        out[f"l3_{name}"] = chunks(a[f"L3_gnn_{key}"])
    out["l3_bq"], out["l3_bk"] = column(a["L3_gnn_bq"]), column(a["L3_gnn_bk"])
    out["l3_bv"], out["l3_beta"] = a["L3_gnn_bv"], a["L3_gnn_beta"].reshape(1)
    return {n: np.ascontiguousarray(v) for n, v in out.items()}


def kernel(**inputs):
    import concourse.bacc as _bacc
    from concourse.bass_utils import run_bass_kernel_spmd

    arrays = layout(inputs)
    nc = _bacc.Bacc("TRN2", target_bir_lowering=False, num_devices=1)
    dram = {n: nc.dram_tensor(f"in_{n}", a.shape, F32, kind="ExternalInput").ap() for n, a in arrays.items()}
    dram["out"] = nc.dram_tensor("out", arrays["x"].shape, F32, kind="ExternalOutput").ap()
    graph_layers_kernel(nc, dram, arrays["x"].shape[0])
    got = run_bass_kernel_spmd(nc, [{f"in_{n}": a for n, a in arrays.items()}], core_ids=[0])
    return got.results[0]["out"]
```

```python
from contextlib import ExitStack

import concourse.bass as bass
from concourse import mybir

F32 = mybir.dt.float32
F32R = mybir.dt.float32r
ALU = mybir.AluOpType
ACT = mybir.ActivationFunctionType
AX = mybir.AxisListType

P = 128
D = 384
C = D // P
G = 2
T = G * P
HEADS = 12
HD = D // HEADS
R = P // HD
BANK = 512
LN_EPS = 1e-5


class Signal:

    def __init__(self, sem, per, base):
        self.sem, self.per, self.base = sem, per, base


class Signals:

    START = 32

    def __init__(self, nc, ctx, pairs):
        self.nc, self.ctx, self.pairs = nc, ctx, pairs
        self.count, self.sems, self.open, self.fresh = {}, {}, [], []

    def sem(self, name, start):
        if name not in self.sems:
            self.sems[name] = self.ctx.enter_context(self.nc.semaphore(name))
            self.count[name] = start
            if start:
                self.fresh.append(self.sems[name])
        return self.sems[name]

    def __call__(self, name, per):
        sem = self.sem(name, self.START)
        self.open.append((name, per))
        return Signal(sem, per, self.count[name])

    def once(self, name, n):
        sem = self.sem(name, 0)
        self.count[name] += n
        return Signal(sem, 0, self.count[name] - n)

    def raise_fresh(self):
        nc, fresh, self.fresh = self.nc, self.fresh, []
        with nc.Block() as block:
            @block.sync
            def _(sp):
                for sem in fresh:
                    sp.sem_inc(sem, self.START)

    def end_phase(self):
        for name, per in self.open:
            self.count[name] += per * self.pairs
        self.open = []


def at(signal, k, j):
    return signal.base + signal.per * k + j


def dma_at(signal, k, parity):
    return signal.base + signal.per * (k - parity) + 2 * signal.per


class Split:

    def __init__(self, hi, lo):
        self.hi, self.lo = hi, lo


def product(nc, out, left, right, first=True, last=True):
    n = len(left)
    for c in range(n):
        (lh, ll), (rh, rl) = left[c], right[c]
        nc.tensor.matmul(out, lh, rh, start=first and c == 0, stop=False)
        nc.tensor.matmul(out, lh, rl, start=False, stop=False)
        ins = nc.tensor.matmul(out, ll, rh, start=False, stop=last and c == n - 1)
    return ins


def steps(engine, pairs):
    with engine.Fori(0, (pairs - 2) // 2) as i:
        for parity in range(2):
            yield 2 * i + parity, parity, True
    yield pairs - 2, 0, False


def late_steps(engine, pairs):
    with engine.Fori(0, (pairs - 4) // 2) as i:
        yield 2 * i + 1, 1
        yield 2 * i + 2, 0
    yield pairs - 3, 1


class Core:
    pass


def load_weights(nc, core, ctx, names, consts):
    splits = []
    for name in names:
        hi = ctx.enter_context(nc.sbuf_tensor(f"{name}_hi", [P, C, D], F32R))
        lo = ctx.enter_context(nc.sbuf_tensor(f"{name}_lo", [P, C, D], F32R))
        splits.append(Split(hi, lo))
    sig = core.signals
    with ExitStack() as staging:
        raw = [staging.enter_context(nc.sbuf_tensor(f"{n}_raw", [P, C, D], F32)) for n in names]
        consts_in = core.signals.once("consts_in", 16 * len(consts))
        weight_in = [core.signals.once(f"weight{j}_in", 16) for j in range(len(names))]
        hi_done = core.signals.once("weight_hi_done", len(names))
        lo_done = core.signals.once("weight_lo_done", len(names))
        block = staging.enter_context(nc.Block())

        @block.sync
        def _(sp):
            for j, name in enumerate(names):
                sp.dma_start(raw[j][:, :, :], core.dram[name]).then_inc(weight_in[j].sem, 16)
            for dst, src in consts:
                sp.dma_start(dst, src).then_inc(consts_in.sem, 16)
            sp.wait_ge(consts_in.sem, consts_in.base + 16 * len(consts))

        @block.scalar
        def _(act):
            for j in range(len(names)):
                act.wait_ge(weight_in[j].sem, weight_in[j].base + 16)
                nc.scalar.activation(splits[j].hi[:, :, :], raw[j][:, :, :], ACT.Copy).then_inc(hi_done.sem, 1)

        @block.vector
        def _(dve):
            for j in range(len(names)):
                dve.wait_ge(hi_done.sem, hi_done.base + j + 1)
                nc.vector.tensor_tensor(splits[j].lo[:, :, :], raw[j][:, :, :],
                                        splits[j].hi[:, :, :].bitcast(F32), ALU.subtract).then_inc(lo_done.sem, 1)
    return splits


def chunk(ap, c):
    return ap[:, c, :]



class Residual:

    SLOTS = 4

    def __init__(self, nc, core, ctx, tag, src, dst):
        self.nc, self.core, self.src, self.dst = nc, core, src, dst
        self.buffer = ctx.enter_context(nc.sbuf_tensor(f"{tag}_x", [P, self.SLOTS * G, D], F32))
        self.loaded = [core.signals(f"x_loaded{j}", 8) for j in range(2)]
        self.stored = [core.signals(f"x_stored{j}", 8) for j in range(2)]

    def pair(self, k):
        return self.buffer[:, bass.ds(G * (k & (self.SLOTS - 1)), G), :]

    def graph(self, k, g):
        return self.buffer[:, bass.ds(G * (k & (self.SLOTS - 1)) + g, 1), :][:, 0, :]

    def wait_loaded(self, engine, k, parity):
        engine.wait_ge(self.loaded[parity].sem, dma_at(self.loaded[parity], k, parity))

    def load(self, sp, norm, k, parity):
        sp.wait_ge(self.stored[parity].sem, dma_at(self.stored[parity], k - self.SLOTS, parity))
        sp.sem_inc(self.core.unwatched.sem, 1)
        sp.wait_ge(norm.ready.sem, at(norm.ready, k - 1, 0))
        sp.sem_inc(self.core.unwatched.sem, 1)
        sp.dma_start(self.pair(k), self.src[bass.ds(G * k, G), :, :].rearrange("g p d -> p g d")
                     ).then_inc(self.loaded[parity].sem, 16)

    def store(self, sp, k, parity):
        sp.dma_start(self.dst[bass.ds(G * k, G), :, :].rearrange("g p d -> p g d"), self.pair(k)
                     ).then_inc(self.stored[parity].sem, 16)

    def wait_stored(self, sp):
        for s in self.stored:
            sp.wait_ge(s.sem, s.base + s.per * self.core.pairs)


class InputNorm:

    def __init__(self, nc, core, ctx, tag, x):
        self.nc, self.core, self.x = nc, core, x
        self.xhat = ctx.enter_context(nc.sbuf_tensor(f"{tag}_xhat", [P, G, D], F32))
        self.stats = ctx.enter_context(nc.sbuf_tensor(f"{tag}_in_stats", [P, G, 6], F32))
        self.moments = ctx.enter_context(nc.sbuf_tensor(f"{tag}_in_moments", [P, G, 2], F32))
        self.log = ctx.enter_context(nc.sbuf_tensor(f"{tag}_in_log", [P, G], F32))
        self.rstd = ctx.enter_context(nc.sbuf_tensor(f"{tag}_in_rstd", [P, G], F32))
        self.stats_done = core.signals("in_stats_done", G)
        self.var_ready = core.signals("in_var_ready", G)
        self.log_done = core.signals("in_log_done", 1)
        self.rstd_ready = core.signals("in_rstd_ready", 1)
        self.ready = core.signals("xhat_ready", G)

    def dve_moments(self, dve, k, parity):
        nc = self.nc
        self.x.wait_loaded(dve, k, parity)
        for g in range(G):
            nc.vector.bn_stats(self.stats[:, g, :], self.x.graph(k, g)).then_inc(self.stats_done.sem, 1)
        for g in range(G):
            dve.wait_ge(self.stats_done.sem, at(self.stats_done, k, g + 1))
            dve.sem_inc(self.core.unwatched.sem, 1)
            nc.vector.bn_aggr(self.moments[:, g, :], self.stats[:, g, :]).then_inc(self.var_ready.sem, 1)

    def act_rstd(self, act, k):
        nc = self.nc
        act.wait_ge(self.var_ready.sem, at(self.var_ready, k, G))
        nc.scalar.activation(self.log[:, :], self.moments[:, :, 1], ACT.Ln, bias=self.core.ln_eps[:, :]
                             ).then_inc(self.log_done.sem, 1)
        act.wait_ge(self.log_done.sem, at(self.log_done, k, 1))
        nc.scalar.activation(self.rstd[:, :], self.log[:, :], ACT.Exp, scale=-0.5).then_inc(self.rstd_ready.sem, 1)

    def dve_xhat(self, dve, k):
        nc = self.nc
        dve.wait_ge(self.rstd_ready.sem, at(self.rstd_ready, k, 1))
        for g in range(G):
            nc.vector.tensor_scalar(self.xhat[:, g, :], self.x.graph(k, g), self.moments[:, g, 0:1],
                                    self.rstd[:, g:g + 1], ALU.subtract, ALU.mult).then_inc(self.ready.sem, 1)



def attention_phase(nc, core, names, biases, is_first):
    NP = core.pairs
    HP = HD + 1
    scale = D ** -0.5 if is_first else HD ** -0.5
    tag = "l0" if is_first else "l3"
    with ExitStack() as ctx:
        def sb(name, shape, dt=F32):
            return ctx.enter_context(nc.sbuf_tensor(f"{tag}_{name}", shape, dt))

        bv = sb("bv", [P, D])
        consts = [(bv[:, :], core.dram[biases[0]].partition_broadcast(P))]
        if is_first:
            bo = sb("bo", [P, D])
            consts.append((bo[:, :], core.dram[biases[1]].partition_broadcast(P)))
        else:
            bqk_raw = sb("bqk_raw", [P, 2, C])
            bqk = sb("bqk", [P, 2, C])
            beta = sb("beta", [P, 1])
            consts.append((bqk_raw[:, 0, :], core.dram[biases[1]]))
            consts.append((bqk_raw[:, 1, :], core.dram[biases[2]]))
            consts.append((beta[:, :], core.dram[biases[3]].partition_broadcast(P)))
        weights = load_weights(nc, core, ctx, names, consts)
        wq, wk, wv = weights[:3]

        x = Residual(nc, core, ctx, tag, core.dram["x" if is_first else "x_mid"], core.dram["x_mid" if is_first else "out"])
        norm = InputNorm(nc, core, ctx, tag, x)
        hT = Split(sb("hT_hi", [P, C, T], F32R), sb("hT_lo", [P, C, T], F32R))
        qT = sb("qT", [P, 2, C, T])
        kT = sb("kT", [P, 2, C, T])
        v = sb("v", [P, 2, G, HEADS, HP])
        adj = sb("adj", [P, 2, G, P])
        bias = sb("bias", [P, 2, G, P])
        s = sb("s", [P, G, R, C, P])
        probs = sb("probs", [P, G, R, C, P])
        s_max = sb("s_max", [P, G, R, C])
        s_shift = sb("s_shift", [P, G, R, C])
        s_abs = sb("s_abs", [P, G, R, C])
        probsT = sb("probsT", [P, G, C, R, P])
        rsum = sb("rsum", [P, G, C, R])
        factor = sb("factor", [P, G, C, R])
        o = sb("o", [P, G, C, R, HD])
        if is_first:
            oT = Split(sb("oT_hi", [P, G, C, P], F32R), sb("oT_lo", [P, G, C, P], F32R))
            xb = sb("xb", [P, G, D])

        SO = ctx.enter_context(nc.psum_tensor(f"{tag}_SO", [P, R, BANK], F32))
        S = SO[:, :, 0:C * P].rearrange("p r (c k) -> p r c k", c=C)
        O = SO[:, :, C * P:C * P + C * HP].rearrange("p r (c e) -> p r c e", c=C)
        back = [ctx.enter_context(nc.psum_tensor(f"{tag}_back{j}", [P, BANK], F32)) for j in range(2)]
        front = [ctx.enter_context(nc.psum_tensor(f"{tag}_front{j}", [P, BANK], F32)) for j in range(2)]

        sig = core.signals
        FI = 4
        BI = 5 if is_first else 3
        PROBS_T = [[g * C + c for c in range(C)] for g in range(G)]
        O_T = [2 * C + 2 * g for g in range(G)]
        OUT = [2 * C + 2 * g + 1 for g in range(G)]
        front_full = [sig(f"front_full{j}", FI) for j in range(2)]
        front_free = [sig(f"front_free{j}", FI) for j in range(2)]
        back_full = [sig(f"back_full{j}", BI) for j in range(2)]
        back_free = [sig(f"back_free{j}", BI) for j in range(2)]
        adj_in = [sig(f"adj_in{j}", 8) for j in range(2)]
        hi_ready = sig("hi_ready", 2)
        s_full = sig("s_full", G)
        s_taken = sig("s_taken", G)
        max_ready = sig("max_ready", G)
        shift_ready = sig("shift_ready", G)
        probs_ready = sig("probs_ready", G * C)
        o_full = sig("o_full", G)
        rsum_ready = sig("rsum_ready", G)
        o_ready = sig("o_ready", G)
        bias_ready = sig("bias_ready", 1)
        ones_set = core.signals.once("ones_set", 1)
        if is_first:
            abs_ready = sig("abs_ready", G)
            factor_ready = sig("factor_ready", G)
            oT_hi_ready = sig("oT_hi_ready", G)
            xb_ready = sig("xb_ready", G)
        else:
            x_done = sig("x_done", G)
            bias_step = sig("bias_step", 2)
            bqk_set = core.signals.once("bqk_set", 1)

        def wait_in(engine, signals, k, parity):
            engine.wait_ge(signals[parity].sem, dma_at(signals[parity], k, parity))

        core.signals.raise_fresh()
        block = ctx.enter_context(nc.Block())

        @block.sync
        def _(sp):
            def load_adj(k, parity):
                sp.wait_ge(bias_ready.sem, at(bias_ready, k - 1, 0))
                sp.sem_inc(core.unwatched.sem, 1)
                sp.dma_start(adj[:, parity, :, :],
                             core.dram["adj"][bass.ds(G * k, G), :, :].rearrange("g p d -> p g d")
                             ).then_inc(adj_in[parity].sem, 16)

            def store(k, parity):
                if is_first:
                    for n in OUT:
                        sp.wait_ge(back_free[n % 2].sem, at(back_free[n % 2], k, n // 2 + 1))
                        sp.sem_inc(core.unwatched.sem, 1)
                else:
                    sp.wait_ge(x_done.sem, at(x_done, k, G))
                    sp.sem_inc(core.unwatched.sem, 1)
                x.store(sp, k, parity)

            for k in range(2):
                x.load(sp, norm, k, k)
                load_adj(k, k)

            x.load(sp, norm, 2, 0)
            load_adj(2, 0)

            for k, parity in late_steps(sp, NP):
                x.load(sp, norm, k + 2, parity)
                load_adj(k + 2, parity)
                store(k - 1, 1 - parity)

            for k in range(NP - 3, NP):
                store(k, k % 2)
            x.wait_stored(sp)

        @block.tensor
        def _(pe):
            def take_front(k, n):
                pe.wait_ge(front_free[n % 2].sem, at(front_free[n % 2], k, n // 2))
                return front[n % 2]

            def take_back(k, n):
                pe.wait_ge(back_free[n % 2].sem, at(back_free[n % 2], k, n // 2))
                return back[n % 2]

            def transpose_h(k):
                pe.wait_ge(norm.ready.sem, at(norm.ready, k, G))
                for n, chunks in enumerate(((0, 1), (2,))):
                    slot = take_front(k, n)
                    for i, c in enumerate(chunks):
                        for g in range(G):
                            ins = nc.tensor.transpose(slot[:, i * T + g * P:i * T + (g + 1) * P],
                                                      norm.xhat[:, g, c * P:(c + 1) * P], core.ident[:, :])
                    ins.then_inc(front_full[n % 2].sem, 1)

            def project(k, which, o_c):
                w, n = weights[which], 2 + 2 * which + o_c // 2
                if o_c == 1:
                    slot = front[n % 2][:, T:2 * T]
                else:
                    if which == 0 and o_c == 0:
                        pe.wait_ge(front_free[1].sem, at(front_free[1], k, 1))
                    slot = take_front(k, n)[:, 0:T]
                f = slice(o_c * P, (o_c + 1) * P)
                ins = product(nc, slot, [(w.hi[:, c, f], w.lo[:, c, f]) for c in range(C)],
                              [(hT.hi[:, c, :], hT.lo[:, c, :]) for c in range(C)])
                if o_c > 0:
                    ins.then_inc(front_full[n % 2].sem, 1)

            def values(k, g):
                n = 6 + g
                slot = take_front(k, n)
                t = slice(g * P, (g + 1) * P)
                product(nc, slot[:, 0:D], [(hT.hi[:, c, t], hT.lo[:, c, t]) for c in range(C)],
                        [(wv.hi[:, c, :], wv.lo[:, c, :]) for c in range(C)]).then_inc(front_full[n % 2].sem, 1)

            def scores(k, parity, g, c):
                if c == 0:
                    pe.wait_ge(front_free[0].sem, at(front_free[0], k, 3))
                    pe.wait_ge(front_free[1].sem, at(front_free[1], k, 3))
                    pe.wait_ge(o_ready.sem, at(o_ready, k, 0))
                    pe.wait_ge(s_taken.sem, at(s_taken, k, g))
                t = slice(g * P, (g + 1) * P)
                for r in range(R):
                    rows = slice(r * HD, (r + 1) * HD)
                    ins = nc.tensor.matmul(S[:, r, c, :], qT[rows, parity, c, t], kT[rows, parity, c, t],
                                           start=True, stop=True)
                if c == C - 1:
                    ins.then_inc(s_full.sem, 1)

            def transpose_probs(k, g, c):
                n = PROBS_T[g][c]
                pe.wait_ge(probs_ready.sem, at(probs_ready, k, g * C + c + 1))
                slot = take_back(k, n)
                for r in range(R):
                    ins = nc.tensor.transpose(slot[:, r * P:(r + 1) * P], probs[:, g, r, c, :], core.ident[:, :])
                ins.then_inc(back_full[n % 2].sem, 1)

            def attend(k, parity, g, c):
                if c == 0:
                    pe.wait_ge(front_free[0].sem, at(front_free[0], k, 4))
                    pe.wait_ge(front_free[1].sem, at(front_free[1], k, 4))
                    pe.wait_ge(s_taken.sem, at(s_taken, k, G))
                    pe.wait_ge(o_ready.sem, at(o_ready, k, g))
                n = PROBS_T[g][c]
                pe.wait_ge(back_free[n % 2].sem, at(back_free[n % 2], k, n // 2 + 1))
                for r in range(R):
                    ins = nc.tensor.matmul(O[:, r, c, :], probsT[:, g, c, r, :], v[:, parity, g, c * R + r, :],
                                           start=True, stop=True)
                if c == C - 1:
                    ins.then_inc(o_full.sem, 1)

            def transpose_o(k, g):
                pe.wait_ge(o_ready.sem, at(o_ready, k, g + 1))
                n = O_T[g]
                slot = take_back(k, n)
                for c in range(C):
                    ins = nc.tensor.transpose(slot[:, c * P:(c + 1) * P],
                                              o[:, g, c, :, :].rearrange("p r e -> p (r e)"), core.ident[:, :])
                ins.then_inc(back_full[n % 2].sem, 1)

            def project_out(k, g):
                wo = weights[3]
                pe.wait_ge(back_free[O_T[g] % 2].sem, at(back_free[O_T[g] % 2], k, O_T[g] // 2 + 1))
                n = OUT[g]
                slot = take_back(k, n)
                product(nc, slot[:, 0:D], [(oT.hi[:, g, c, :], oT.lo[:, g, c, :]) for c in range(C)],
                        [(wo.hi[:, c, :], wo.lo[:, c, :]) for c in range(C)]).then_inc(back_full[n % 2].sem, 1)

            transpose_h(0)
            for which in range(2):
                for c in range(C):
                    project(0, which, c)
            values(0, 0)
            values(0, 1)
            transpose_h(1)
            scores(0, 0, 0, 0)

            for k, parity, more in steps(pe, NP):
                scores(k, parity, 0, 1)
                project(k + 1, 0, 0)
                scores(k, parity, 0, 2)
                project(k + 1, 0, 1)
                project(k + 1, 0, 2)
                scores(k, parity, 1, 0)
                project(k + 1, 1, 0)
                scores(k, parity, 1, 1)
                if is_first:
                    project(k + 1, 1, 1)
                    scores(k, parity, 1, 2)
                else:
                    scores(k, parity, 1, 2)
                    project(k + 1, 1, 1)
                transpose_probs(k, 0, 0)
                transpose_probs(k, 0, 1)
                project(k + 1, 1, 2)
                attend(k, parity, 0, 0)
                transpose_probs(k, 0, 2)
                attend(k, parity, 0, 1)
                attend(k, parity, 0, 2)
                transpose_probs(k, 1, 0)
                values(k + 1, 0)
                transpose_probs(k, 1, 1)
                attend(k, parity, 1, 0)
                transpose_probs(k, 1, 2)
                if is_first:
                    transpose_o(k, 0)
                    attend(k, parity, 1, 1)
                    attend(k, parity, 1, 2)
                    project_out(k, 0)
                    values(k + 1, 1)
                    transpose_o(k, 1)
                    if more:
                        transpose_h(k + 2)
                    scores(k + 1, 1 - parity, 0, 0)
                    project_out(k, 1)
                else:
                    attend(k, parity, 1, 1)
                    values(k + 1, 1)
                    attend(k, parity, 1, 2)
                    if more:
                        transpose_h(k + 2)
                    scores(k + 1, 1 - parity, 0, 0)

            k, parity = NP - 1, 1
            scores(k, parity, 0, 1)
            scores(k, parity, 0, 2)
            for c in range(C):
                scores(k, parity, 1, c)
            for g in range(G):
                for c in range(C):
                    transpose_probs(k, g, c)
                if is_first and g == 1:
                    transpose_o(k, 0)
                for c in range(C):
                    attend(k, parity, g, c)
            if is_first:
                project_out(k, 0)
                transpose_o(k, 1)
                project_out(k, 1)

        @block.scalar
        def _(act):
            def high_h(k):
                for n, chunks in enumerate(((0, 1), (2,))):
                    act.wait_ge(front_full[n].sem, at(front_full[n], k, 1))
                    src = front[n][:, 0:len(chunks) * T].rearrange("p (c t) -> p c t", t=T)
                    nc.scalar.activation(hT.hi[:, chunks[0]:chunks[-1] + 1, :], src, ACT.Relu).then_inc(hi_ready.sem, 1)

            def copy_qk(k, parity, which, half):
                n = 2 + 2 * which + half
                dst = (qT, kT)[which]
                chunks = ((0, 1), (2,))[half]
                act.wait_ge(front_full[n % 2].sem, at(front_full[n % 2], k, n // 2 + 1))
                if is_first:
                    src = front[n % 2][:, 0:len(chunks) * T].rearrange("p (c t) -> p c t", t=T)
                    ins = nc.scalar.activation(dst[:, parity, chunks[0]:chunks[-1] + 1, :], src, ACT.Copy,
                                               scale=scale if which == 0 else 1.0)
                else:
                    for i, c in enumerate(chunks):
                        ins = nc.scalar.activation(dst[:, parity, c, :], front[n % 2][:, i * T:(i + 1) * T],
                                                   ACT.Identity, bias=bqk[:, which, c:c + 1],
                                                   scale=scale if which == 0 else 1.0)
                ins.then_inc(front_free[n % 2].sem, 1)

            def exps(k, g, c):
                act.wait_ge(shift_ready.sem, at(shift_ready, k, g + 1))
                for r in range(R):
                    ins = nc.scalar.activation(probs[:, g, r, c, :], s[:, g, r, c, :], ACT.Exp,
                                               bias=s_shift[:, g, r, c:c + 1])
                ins.then_inc(probs_ready.sem, 1)

            def copy_probsT(k, g, c):
                n = PROBS_T[g][c]
                act.wait_ge(back_full[n % 2].sem, at(back_full[n % 2], k, n // 2 + 1))
                nc.scalar.activation(probsT[:, g, c].rearrange("p r k -> p (r k)"), back[n % 2][:, :],
                                     ACT.Copy).then_inc(back_free[n % 2].sem, 1)

            def high_o(k, g):
                n = O_T[g]
                act.wait_ge(back_full[n % 2].sem, at(back_full[n % 2], k, n // 2 + 1))
                nc.scalar.activation(oT.hi[:, g].rearrange("p c t -> p (c t)"), back[n % 2][:, 0:D],
                                     ACT.Copy).then_inc(oT_hi_ready.sem, 1)

            norm.act_rstd(act, 0)
            if not is_first:
                nc.scalar.activation(bqk[:, 0, :], bqk_raw[:, 0, :], ACT.Copy, scale=scale)
                nc.scalar.activation(bqk[:, 1, :], bqk_raw[:, 1, :], ACT.Copy).then_inc(bqk_set.sem, 1)
            high_h(0)
            if not is_first:
                act.wait_ge(bqk_set.sem, bqk_set.base + 1)
            norm.act_rstd(act, 1)
            for which in range(2):
                for half in range(2):
                    copy_qk(0, 0, which, half)
            high_h(1)

            for k, parity, more in steps(act, NP):
                copy_qk(k + 1, 1 - parity, 0, 0)
                copy_qk(k + 1, 1 - parity, 0, 1)
                for c in range(C):
                    exps(k, 0, c)
                copy_probsT(k, 0, 0)
                copy_qk(k + 1, 1 - parity, 1, 0)
                copy_probsT(k, 0, 1)
                copy_qk(k + 1, 1 - parity, 1, 1)
                copy_probsT(k, 0, 2)
                exps(k, 1, 0)
                exps(k, 1, 1)
                copy_probsT(k, 1, 0)
                exps(k, 1, 2)
                copy_probsT(k, 1, 1)
                if more:
                    norm.act_rstd(act, k + 2)
                copy_probsT(k, 1, 2)
                if is_first:
                    high_o(k, 0)
                    high_o(k, 1)
                if more:
                    high_h(k + 2)

            k = NP - 1
            for g in range(G):
                for c in range(C):
                    exps(k, g, c)
                for c in range(C):
                    copy_probsT(k, g, c)
            if is_first:
                high_o(k, 0)
                high_o(k, 1)

        @block.vector
        def _(dve):
            def low_h(k):
                for n, chunks in enumerate(((0, 1), (2,))):
                    dve.wait_ge(hi_ready.sem, at(hi_ready, k, n + 1))
                    cs = slice(chunks[0], chunks[-1] + 1)
                    src = front[n][:, 0:len(chunks) * T].rearrange("p (c t) -> p c t", t=T)
                    nc.vector.scalar_tensor_tensor(out=hT.lo[:, cs, :], in0=src, scalar=0.0,
                                                   in1=hT.hi[:, cs, :].bitcast(F32), op0=ALU.max,
                                                   op1=ALU.subtract).then_inc(front_free[n].sem, 1)

            def take_scores(k, parity, g):
                if g == 0:
                    dve.wait_ge(bias_ready.sem, at(bias_ready, k, 1))
                dve.wait_ge(s_full.sem, at(s_full, k, g + 1))
                dve.wait_ge(probs_ready.sem, at(probs_ready, k - 1, (g + 1) * C))
                b = bias[:, parity, g, :]
                nc.vector.tensor_tensor(s[:, g], S, b[:, None, None, :].to_broadcast([P, R, C, P]), ALU.add
                                        ).then_inc(s_taken.sem, 1)

            def shift_scores(k, g):
                dve.wait_ge(s_taken.sem, at(s_taken, k, g + 1))
                nc.vector.tensor_reduce(s_max[:, g], s[:, g], AX.X, ALU.max).then_inc(max_ready.sem, 1)
                dve.wait_ge(max_ready.sem, at(max_ready, k, g + 1))
                nc.vector.tensor_scalar(s_shift[:, g], s_max[:, g], -1.0, None, ALU.mult
                                        ).then_inc(shift_ready.sem, 1)

            def abs_scores(k, g):
                if is_first:
                    nc.vector.tensor_reduce(s_abs[:, g], s[:, g], AX.X, ALU.max, apply_absolute_value=True
                                            ).then_inc(abs_ready.sem, 1)

            def take_values(k, parity, g):
                dve.wait_ge(front_full[g].sem, at(front_full[g], k, FI))
                nc.vector.tensor_tensor(v[:, parity, g, :, 0:HD],
                                        front[g][:, 0:D].rearrange("p (h e) -> p h e", e=HD),
                                        bv[:, :].rearrange("p (h e) -> p h e", e=HD), ALU.add
                                        ).then_inc(front_free[g].sem, 1)

            def normalise(k, g):
                dve.wait_ge(o_full.sem, at(o_full, k, g + 1))
                sums = O[:, :, :, HD].rearrange("p r c -> p c r")
                nc.vector.reciprocal(rsum[:, g], sums).then_inc(rsum_ready.sem, 1)
                dve.wait_ge(rsum_ready.sem, at(rsum_ready, k, g + 1))
                f = rsum
                if is_first:
                    f = factor
                    dve.wait_ge(abs_ready.sem, at(abs_ready, k, g + 1))
                    nc.vector.scalar_tensor_tensor(
                        out=factor[:, g], in0=s_abs[:, g].rearrange("p r c -> p c r"), scalar=0.0,
                        in1=rsum[:, g], op0=ALU.not_equal, op1=ALU.mult).then_inc(factor_ready.sem, 1)
                    dve.wait_ge(factor_ready.sem, at(factor_ready, k, g + 1))
                nc.vector.tensor_tensor(o[:, g], O[:, :, :, 0:HD].rearrange("p r c e -> p c r e"),
                                        f[:, g, :, :, None].to_broadcast([P, C, R, HD]), ALU.mult
                                        ).then_inc(o_ready.sem, 1)

            def low_o(k, g):
                n = O_T[g]
                dve.wait_ge(oT_hi_ready.sem, at(oT_hi_ready, k, g + 1))
                nc.vector.tensor_tensor(oT.lo[:, g].rearrange("p c t -> p (c t)"), back[n % 2][:, 0:D],
                                        oT.hi[:, g].rearrange("p c t -> p (c t)").bitcast(F32), ALU.subtract
                                        ).then_inc(back_free[n % 2].sem, 1)

            def update_x(k, g):
                xg = x.graph(k, g)
                if is_first:
                    n = OUT[g]
                    dve.wait_ge(xb_ready.sem, at(xb_ready, k, g + 1))
                    dve.wait_ge(back_full[n % 2].sem, at(back_full[n % 2], k, n // 2 + 1))
                    nc.vector.tensor_tensor(xg, back[n % 2][:, 0:D], xb[:, g, :], ALU.add
                                            ).then_inc(back_free[n % 2].sem, 1)
                else:
                    dve.wait_ge(o_ready.sem, at(o_ready, k, g + 1))
                    nc.vector.tensor_tensor(xg, xg, o[:, g].rearrange("p c r e -> p (c r e)"), ALU.add
                                            ).then_inc(x_done.sem, 1)

            norm.dve_moments(dve, 0, 0)
            norm.dve_xhat(dve, 0)
            norm.dve_moments(dve, 1, 1)
            low_h(0)
            norm.dve_xhat(dve, 1)
            dve.wait_ge(ones_set.sem, ones_set.base + 1)
            take_values(0, 0, 0)
            take_values(0, 0, 1)
            low_h(1)

            for k, parity, more in steps(dve, NP):
                take_scores(k, parity, 0)
                shift_scores(k, 0)
                abs_scores(k, 0)
                take_scores(k, parity, 1)
                shift_scores(k, 1)
                if is_first:
                    if more:
                        norm.dve_moments(dve, k + 2, parity)
                    normalise(k, 0)
                    abs_scores(k, 1)
                    take_values(k + 1, 1 - parity, 0)
                    low_o(k, 0)
                    if more:
                        norm.dve_xhat(dve, k + 2)
                    normalise(k, 1)
                    take_values(k + 1, 1 - parity, 1)
                    update_x(k, 0)
                    low_o(k, 1)
                    if more:
                        low_h(k + 2)
                else:
                    if more:
                        norm.dve_moments(dve, k + 2, parity)
                    normalise(k, 0)
                    update_x(k, 0)
                    take_values(k + 1, 1 - parity, 0)
                    if more:
                        norm.dve_xhat(dve, k + 2)
                    take_values(k + 1, 1 - parity, 1)
                    normalise(k, 1)
                    if more:
                        low_h(k + 2)
                update_x(k, 1)

            k = NP - 1
            for g in range(G):
                take_scores(k, 1, g)
                shift_scores(k, g)
                abs_scores(k, g)
            normalise(k, 0)
            if is_first:
                low_o(k, 0)
            normalise(k, 1)
            update_x(k, 0)
            if is_first:
                low_o(k, 1)
            update_x(k, 1)

        @block.gpsimd
        def _(pool):
            def add_bo(k, parity):
                x.wait_loaded(pool, k, parity)
                for g in range(G):
                    n = OUT[g]
                    pool.wait_ge(back_free[n % 2].sem, at(back_free[n % 2], k - 1, n // 2 + 1))
                    nc.gpsimd.tensor_tensor(xb[:, g, :], x.graph(k, g), bo[:, :],
                                            ALU.add).then_inc(xb_ready.sem, 1)

            def make_bias(k, parity):
                wait_in(pool, adj_in, k, parity)
                pool.wait_ge(s_taken.sem, at(s_taken, k - 1, 0))
                pool.sem_inc(core.unwatched.sem, 1)
                if is_first:
                    nc.gpsimd.tensor_scalar(bias[:, parity], adj[:, parity], 2.0, 0.0, ALU.mult, ALU.add
                                            ).then_inc(bias_ready.sem, 1)
                    return
                nc.gpsimd.tensor_scalar(bias[:, parity], adj[:, parity], 0.0, -9e15, ALU.is_le, ALU.mult
                                        ).then_inc(bias_step.sem, 1)
                nc.gpsimd.tensor_scalar(adj[:, parity], adj[:, parity], beta[:, 0:1], 0.0, ALU.mult, ALU.add
                                        ).then_inc(bias_step.sem, 1)
                pool.wait_ge(bias_step.sem, at(bias_step, k, 2))
                nc.gpsimd.tensor_tensor(bias[:, parity], bias[:, parity], adj[:, parity], ALU.add
                                        ).then_inc(bias_ready.sem, 1)

            nc.gpsimd.memset(v[:, :, :, :, HD:HP], 1.0).then_inc(ones_set.sem, 1)
            make_bias(0, 0)

            for k, parity, more in steps(pool, NP):
                make_bias(k + 1, 1 - parity)
                if is_first:
                    add_bo(k, parity)

            if is_first:
                add_bo(NP - 1, 1)


    sig.end_phase()



class Stage:

    def __init__(self, nc, core, ctx, kind, index, weights, biases, norm):
        self.nc, self.core, self.kind, self.index, self.norm = nc, core, kind, index, norm
        self.weights, self.biases = weights, biases
        tag = f"{'first' if index == 0 else 'second'}"
        self.name = f"l{kind}_{tag}"
        sig = lambda n, per: core.signals(f"{tag}_{n}", per)

        def sb(name, shape, dt=F32):
            return ctx.enter_context(nc.sbuf_tensor(f"{self.name}_{name}", shape, dt))

        self.hT_f = sb("hT", [P, C, T])
        self.hT = Split(sb("hT_hi", [P, C, T], F32R), sb("hT_lo", [P, C, T], F32R))
        self.adj = sb("adj", [P, 2, G, P])
        self.c = sb("c", [P, G, D])
        self.t = sb("t", [P, G, D])
        self.stats = sb("stats", [P, G, 6])
        self.moments = sb("moments", [P, G, 2])
        self.log = sb("log", [P, G])
        self.rstd = sb("rstd", [P, G])
        self.r = sb("r", [P, G])
        self.q = sb("q", [P, G])
        if kind == 1:
            self.left = sb("hl", [P, G, D])
            self.right = sb("hr", [P, G, D])
            self.self_ = sb("hs", [P, G, D])
            self.self_bias = sb("hs_bias", [P, G, D])
            self.e = sb("e", [P, G, P])
            self.E = sb("delta", [P, G, P])
            self.ET = sb("deltaT", [P, G, 2, P])
            self.sum_e = sb("sum_e", [P, G])
            self.sum_d = sb("sum_d", [P, G])
            self.diag = sb("diag", [P, G])
            self.diag_r = sb("diag_r", [P, G])
            self.row_max = sb("row_max", [P, G])
            self.shift = sb("shift", [P, G])
            self.junk = sb("junk", [P, G, P])
        else:
            self.adjT = sb("adjT", [P, 2, G, P])
            self.mT = sb("mT", [P, 2, C, T])
            self.lin = sb("lin", [P, G, D + 1])
            self.w = sb("w", [P, 2, G, 2, P])
            self.uw = sb("uw", [P, G, 2, P])
            self.u = sb("u", [P, G, P])
            self.e = sb("e", [P, G, P])
            self.E = sb("deltaT", [P, G, P])
            self.std = sb("std", [P, G])
        ps = lambda n: ctx.enter_context(nc.psum_tensor(f"{self.name}_{n}", [P, BANK], F32))
        self.ring = [ps("ring0"), ps("ring1")]
        self.U = ps("U")
        self.ctx = ps("ctx")

        self.full = [sig(f"ring_full{j}", 4) for j in range(2)]
        self.free = [sig(f"ring_free{j}", 4) for j in range(2)]
        self.adj_in = [sig(f"adj_in{j}", 8 * kind) for j in range(2)]
        self.hi_ready = sig("hi_ready", 1)
        self.lo_ready = sig("lo_ready", 1)
        self.u_full = sig("u_full", 1)
        self.shift_ready = sig("shift_ready", 1)
        self.e_ready = sig("e_ready", G if kind == 1 else 1)
        self.E_ready = sig("delta_ready", G if kind == 1 else 1)
        if kind == 1:
            self.ET_full = sig("deltaT_full", 1)
            self.ET_ready = sig("deltaT_ready", 1)
            self.diag_ready = sig("diag_ready", 1)
            self.self_bias_ready = sig("self_bias_ready", G)
            self.self_ready = sig("self_ready", G)
        else:
            self.w_ready = sig("w_ready", 2)
        self.ctx_full = sig("ctx_full", G)
        self.ctx_free = sig("ctx_free", G)
        self.var_ready = sig("var_ready", G)
        self.log_done = sig("log_done", 1)
        self.rstd_ready = sig("rstd_ready", 1)
        self.t_ready = sig("t_ready", G)
        self.stats_done = sig("stats_done", G)
        self.q_done = sig("q_done", kind)
        self.r_done = sig("r_done", kind)
        if kind == 1:
            self.max_done = sig("max_done", 1)
            self.diag_done = sig("diag_done", G)
        else:
            self.uw_done = sig("uw_done", 1)
            self.std_done = sig("std_done", 1)
            self.inverse_done = sig("inverse_done", 1)
        if index == 1:
            self.final_link = sig("final_link", 3)
            self.final_done = sig("final_done", 1)


    def take(self, pe, k, n):
        pe.wait_ge(self.free[n % 2].sem, at(self.free[n % 2], k, n // 2))
        return self.ring[n % 2]

    def h_copied(self, engine, k):
        for slot in range(2):
            engine.wait_ge(self.free[slot].sem, at(self.free[slot], k, 1))

    def adj_loaded(self, engine, k, parity):
        engine.wait_ge(self.adj_in[parity].sem, dma_at(self.adj_in[parity], k, parity))


    def load_adj(self, sp, k, parity):
        sp.wait_ge(self.E_ready.sem, at(self.E_ready, k - 1, 0))
        sp.sem_inc(self.core.unwatched.sem, 1)
        sp.dma_start(self.adj[:, parity, :, :],
                     self.core.dram["adj"][bass.ds(G * k, G), :, :].rearrange("g p d -> p g d")
                     ).then_inc(self.adj_in[parity].sem, 16)
        if self.kind == 2:
            sp.dma_start(self.adjT[:, parity, :, :],
                         self.core.dram["adjT"][bass.ds(G * k, G), :, :].rearrange("g p d -> p g d")
                         ).then_inc(self.adj_in[parity].sem, 16)


    def pe_transpose_h(self, pe, k):
        nc = self.nc
        src, ready = self.source
        pe.wait_ge(ready.sem, at(ready, k, G))
        for n, chunks in enumerate(((0, 1), (2,))):
            slot = self.take(pe, k, n)
            for i, c in enumerate(chunks):
                for g in range(G):
                    ins = nc.tensor.transpose(slot[:, i * T + g * P:i * T + (g + 1) * P],
                                              src[:, g, c * P:(c + 1) * P], self.core.ident[:, :])
            ins.then_inc(self.full[n % 2].sem, 1)

    def pe_linear(self, pe, k, w, g, n):
        slot = self.take(pe, k, n)
        t = slice(g * P, (g + 1) * P)
        product(self.nc, slot[:, 0:D], [(self.hT.hi[:, c, t], self.hT.lo[:, c, t]) for c in range(C)],
                [(w.hi[:, c, :], w.lo[:, c, :]) for c in range(C)]).then_inc(self.full[n % 2].sem, 1)

    def pe_messages(self, pe, k, side, half):
        nc, w, n = self.nc, self.weights[side], 2 + 2 * side + half
        pe.wait_ge(self.lo_ready.sem, at(self.lo_ready, k, 1))
        slot = self.take(pe, k, n)
        for i, o_c in enumerate(((0, 1), (2,))[half]):
            f = slice(o_c * P, (o_c + 1) * P)
            ins = product(nc, slot[:, i * T:(i + 1) * T],
                          [(w.hi[:, c, f], w.lo[:, c, f]) for c in range(C)],
                          [(self.hT.hi[:, c, :], self.hT.lo[:, c, :]) for c in range(C)])
        ins.then_inc(self.full[n % 2].sem, 1)


    def pe_gram(self, pe, k):
        nc = self.nc
        self.h_copied(pe, k)
        pe.wait_ge(self.E_ready.sem, at(self.E_ready, k, 0))
        for g in range(G):
            t = slice(g * P, (g + 1) * P)
            for c in range(C):
                ins = nc.tensor.matmul(self.U[:, t], self.hT_f[:, c, t], self.hT_f[:, c, t],
                                       start=c == 0, stop=c == C - 1)
        ins.then_inc(self.u_full.sem, 1)

    def pe_linears(self, pe, k, g, which):
        pe.wait_ge(self.lo_ready.sem, at(self.lo_ready, k, 1))
        for i in which:
            self.pe_linear(pe, k, self.weights[i], g, 2 + 3 * g + i)

    def pe_transpose_delta(self, pe, k):
        nc = self.nc
        pe.wait_ge(self.E_ready.sem, at(self.E_ready, k, G))
        pe.wait_ge(self.ET_ready.sem, at(self.ET_ready, k, 0))
        for g in range(G):
            ins = nc.tensor.transpose(self.U[:, T + g * P:T + (g + 1) * P], self.E[:, g, :], self.core.ident[:, :])
        ins.then_inc(self.ET_full.sem, 1)

    def pe_context(self, pe, k, g):
        (self.pe_side_contexts if self.kind == 1 else self.pe_gather)(pe, k, g)

    def pe_side_contexts(self, pe, k, g):
        nc = self.nc
        if g == 0:
            pe.wait_ge(self.ET_ready.sem, at(self.ET_ready, k, 1))
        for n in (2 + 3 * g, 3 + 3 * g):
            pe.wait_ge(self.free[n % 2].sem, at(self.free[n % 2], k, n // 2 + 1))
        pe.wait_ge(self.ctx_free.sem, at(self.ctx_free, k, g))
        nc.tensor.matmul(self.ctx[:, 0:D], self.ET[:, g, 0, :], self.left[:, g, :], start=True, stop=False)
        nc.tensor.matmul(self.ctx[:, 0:D], self.ET[:, g, 1, :], self.right[:, g, :], start=False, stop=True
                         ).then_inc(self.ctx_full.sem, 1)


    def pe_scores(self, pe, k):
        nc = self.nc
        self.h_copied(pe, k)
        for n in (4, 5):
            pe.wait_ge(self.free[n % 2].sem, at(self.free[n % 2], k, n // 2 + 1))
        pe.wait_ge(self.shift_ready.sem, at(self.shift_ready, k, 0))
        for g in range(G):
            t = slice(g * P, (g + 1) * P)
            for side in range(2):
                out = self.U[:, (2 * g + side) * P:(2 * g + side + 1) * P]
                for c in range(C):
                    ins = nc.tensor.matmul(out, self.mT[:, side, c, t], self.hT_f[:, c, t],
                                           start=c == 0, stop=c == C - 1)
        ins.then_inc(self.u_full.sem, 1)

    def pe_gather(self, pe, k, g):
        nc = self.nc
        if g == 0:
            pe.wait_ge(self.E_ready.sem, at(self.E_ready, k, 1))
        n = 6 + g
        pe.wait_ge(self.free[n % 2].sem, at(self.free[n % 2], k, n // 2 + 1))
        pe.wait_ge(self.ctx_free.sem, at(self.ctx_free, k, g))
        nc.tensor.matmul(self.ctx[:, 0:D + 1], self.E[:, g, :], self.lin[:, g, :], start=True, stop=True
                         ).then_inc(self.ctx_full.sem, 1)


    def act_h(self, act, k):
        nc = self.nc
        for n, chunks in enumerate(((0, 1), (2,))):
            act.wait_ge(self.full[n].sem, at(self.full[n], k, 1))
            for i, c in enumerate(chunks):
                src = self.ring[n][:, i * T:(i + 1) * T]
                if self.index == 0:
                    ins = nc.scalar.activation(self.hT_f[:, c, :], src, ACT.Relu)
                else:
                    ins = nc.scalar.activation(self.hT_f[:, c, :], src, ACT.Relu, bias=self.betaT[:, c:c + 1],
                                               scale=self.gammaT[:, c:c + 1])
            ins.then_inc(self.free[n].sem, 1)
        self.h_copied(act, k)
        nc.scalar.activation(self.hT.hi[:, :, :], self.hT_f[:, :, :], ACT.Copy).then_inc(self.hi_ready.sem, 1)

    def act_exps(self, act, k):
        nc = self.nc
        act.wait_ge(self.shift_ready.sem, at(self.shift_ready, k, 1))
        for g in range(G):
            nc.scalar.activation(self.e[:, g, :], self.U[:, g * P:(g + 1) * P], ACT.Exp,
                                 bias=self.shift[:, g:g + 1], scale=D ** -0.5, accum_out=self.sum_e[:, g:g + 1]
                                 ).then_inc(self.e_ready.sem, 1)

    def act_self(self, act, k, g):
        nc = self.nc
        n = 4 + 3 * g
        if g == 0:
            act.wait_ge(self.diag_ready.sem, at(self.diag_ready, k, 1))
        act.wait_ge(self.full[n % 2].sem, at(self.full[n % 2], k, n // 2 + 1))
        nc.scalar.activation(self.self_[:, g, :], self.ring[n % 2][:, 0:D], ACT.Copy,
                             scale=self.diag_r[:, g:g + 1]).then_inc(self.free[n % 2].sem, 1)

    def act_messages(self, act, k, side, half):
        nc, n = self.nc, 2 + 2 * side + half
        chunks = ((0, 1), (2,))[half]
        act.wait_ge(self.full[n % 2].sem, at(self.full[n % 2], k, n // 2 + 1))
        nc.scalar.activation(self.mT[:, side, chunks[0]:chunks[-1] + 1, :],
                             self.ring[n % 2][:, 0:len(chunks) * T].rearrange("p (c t) -> p c t", t=T),
                             ACT.Copy).then_inc(self.free[n % 2].sem, 1)

    def act_exp_u(self, act, k):
        nc = self.nc
        act.wait_ge(self.shift_ready.sem, at(self.shift_ready, k, 1))
        nc.scalar.activation(self.e[:, :, :], self.u[:, :, :], ACT.Exp, scale=D ** -0.5).then_inc(self.e_ready.sem, 1)

    def act_rstd(self, act, k):
        nc = self.nc
        act.wait_ge(self.var_ready.sem, at(self.var_ready, k, G))
        if self.kind == 1:
            nc.scalar.activation(self.log[:, :], self.moments[:, :, 1], ACT.Ln, bias=self.core.eps_l1[:, :]
                                 ).then_inc(self.log_done.sem, 1)
            act.wait_ge(self.log_done.sem, at(self.log_done, k, 1))
            nc.scalar.activation(self.rstd[:, :], self.log[:, :], ACT.Exp, scale=-0.5).then_inc(self.rstd_ready.sem, 1)
        else:
            nc.scalar.activation(self.log[:, :], self.moments[:, :, 1], ACT.Ln, bias=self.core.eps_l2[:, :],
                                 scale=D / (D - 1)).then_inc(self.log_done.sem, 1)
            act.wait_ge(self.log_done.sem, at(self.log_done, k, 1))
            nc.scalar.activation(self.std[:, :], self.log[:, :], ACT.Exp, scale=0.5).then_inc(self.rstd_ready.sem, 1)


    def dve_low_h(self, dve, k):
        dve.wait_ge(self.hi_ready.sem, at(self.hi_ready, k, 1))
        self.nc.vector.tensor_tensor(self.hT.lo[:, :, :], self.hT_f[:, :, :], self.hT.hi[:, :, :].bitcast(F32),
                                     ALU.subtract).then_inc(self.lo_ready.sem, 1)

    def dve_shift(self, dve, k):
        nc = self.nc
        dve.wait_ge(self.u_full.sem, at(self.u_full, k, 1))
        nc.vector.tensor_reduce(self.row_max[:, :], self.U[:, 0:T].rearrange("p (g j) -> p g j", g=G),
                                AX.X, ALU.max).then_inc(self.max_done.sem, 1)
        dve.wait_ge(self.max_done.sem, at(self.max_done, k, 1))
        nc.vector.tensor_scalar(self.shift[:, :], self.row_max[:, :], -(D ** -0.5), None, ALU.mult
                                ).then_inc(self.shift_ready.sem, 1)

    def dve_delta(self, dve, k, parity):
        nc = self.nc
        self.adj_loaded(dve, k, parity)
        for g in range(G):
            dve.wait_ge(self.e_ready.sem, at(self.e_ready, k, g + 1))
            nc.vector.scalar_tensor_tensor(out=self.E[:, g, :], in0=self.e[:, g, :], scalar=1.0,
                                           in1=self.adj[:, parity, g, :], op0=ALU.mult, op1=ALU.mult,
                                           accum_out=self.sum_d[:, g:g + 1]).then_inc(self.E_ready.sem, 1)
        dve.wait_ge(self.E_ready.sem, at(self.E_ready, k, G))
        nc.vector.scalar_tensor_tensor(out=self.q[:, :], in0=self.sum_e[:, :], scalar=1e-10, in1=self.sum_d[:, :],
                                       op0=ALU.mult, op1=ALU.add).then_inc(self.q_done.sem, 1)
        for g in range(G):
            nc.vector.scalar_tensor_tensor(out=self.junk[:, g, :], in0=self.E[:, g, :], scalar=1.0,
                                           in1=self.core.ident[:, :], op0=ALU.mult, op1=ALU.mult,
                                           accum_out=self.diag[:, g:g + 1]).then_inc(self.diag_done.sem, 1)
        dve.wait_ge(self.q_done.sem, at(self.q_done, k, 1))
        nc.vector.reciprocal(self.r[:, :], self.q[:, :]).then_inc(self.r_done.sem, 1)
        dve.wait_ge(self.diag_done.sem, at(self.diag_done, k, G))
        dve.wait_ge(self.r_done.sem, at(self.r_done, k, 1))
        nc.vector.tensor_tensor(self.diag_r[:, :], self.diag[:, :], self.r[:, :], ALU.mult
                                ).then_inc(self.diag_ready.sem, 1)

    def dve_side(self, dve, k, g, i):
        n = 2 + 3 * g + i
        dve.wait_ge(self.full[n % 2].sem, at(self.full[n % 2], k, n // 2 + 1))
        self.nc.vector.tensor_tensor((self.left, self.right)[i][:, g, :], self.ring[n % 2][:, 0:D],
                                     self.biases[i][:, :], ALU.add).then_inc(self.free[n % 2].sem, 1)

    def dve_triangles(self, dve, k):
        nc = self.nc
        dve.wait_ge(self.ET_full.sem, at(self.ET_full, k, 1))
        src = self.U[:, T:2 * T].rearrange("p (g i) -> p g i", g=G)[:, :, None, :].to_broadcast([P, G, 2, P])
        mask = self.core.triangles[:, None, :, :].to_broadcast([P, G, 2, P])
        nc.vector.tensor_tensor(self.ET[:, :, :, :], src, mask, ALU.mult).then_inc(self.ET_ready.sem, 1)

    def dve_weighted(self, dve, k, parity):
        nc = self.nc
        dve.wait_ge(self.w_ready.sem, at(self.w_ready, k, 2))
        dve.wait_ge(self.u_full.sem, at(self.u_full, k, 1))
        nc.vector.tensor_tensor(self.uw[:, :, :, :].rearrange("p g s i -> p (g s i)"), self.U[:, :],
                                self.w[:, parity].rearrange("p g s i -> p (g s i)"), ALU.mult
                                ).then_inc(self.uw_done.sem, 1)
        dve.wait_ge(self.uw_done.sem, at(self.uw_done, k, 1))
        nc.vector.tensor_tensor(self.u[:, :, :], self.uw[:, :, 0, :], self.uw[:, :, 1, :], ALU.add
                                ).then_inc(self.shift_ready.sem, 1)

    def dve_delta_t(self, dve, k, parity):
        nc = self.nc
        dve.wait_ge(self.e_ready.sem, at(self.e_ready, k, 1))
        nc.vector.tensor_tensor(self.E[:, :, :], self.e[:, :, :], self.adjT[:, parity], ALU.mult
                                ).then_inc(self.E_ready.sem, 1)

    def dve_lin(self, dve, k, g):
        nc = self.nc
        n = 6 + g
        dve.wait_ge(self.full[n % 2].sem, at(self.full[n % 2], k, n // 2 + 1))
        nc.vector.tensor_tensor(self.lin[:, g, 0:D], self.ring[n % 2][:, 0:D], self.biases[0][:, :], ALU.add
                                ).then_inc(self.free[n % 2].sem, 1)

    def dve_context(self, dve, k, g):
        nc = self.nc
        dve.wait_ge(self.ctx_full.sem, at(self.ctx_full, k, g + 1))
        if self.kind == 1:
            dve.wait_ge(self.self_ready.sem, at(self.self_ready, k, g + 1))
            ins = nc.vector.scalar_tensor_tensor(out=self.c[:, g, :], in0=self.ctx[:, 0:D], scalar=self.r[:, g:g + 1],
                                                 in1=self.self_[:, g, :], op0=ALU.mult, op1=ALU.add)
        else:
            nc.vector.tensor_scalar(self.q[:, g:g + 1], self.ctx[:, D:D + 1], 1e-10, None, ALU.add
                                    ).then_inc(self.q_done.sem, 1)
            dve.wait_ge(self.q_done.sem, at(self.q_done, k, g + 1))
            nc.vector.reciprocal(self.r[:, g:g + 1], self.q[:, g:g + 1]).then_inc(self.r_done.sem, 1)
            dve.wait_ge(self.r_done.sem, at(self.r_done, k, g + 1))
            ins = nc.vector.tensor_scalar(self.c[:, g, :], self.ctx[:, 0:D], self.r[:, g:g + 1], None, ALU.mult)
        ins.then_inc(self.ctx_free.sem, 1)
        dve.wait_ge(self.ctx_free.sem, at(self.ctx_free, k, g + 1))
        nc.vector.bn_stats(self.stats[:, g, :], self.c[:, g, :]).then_inc(self.stats_done.sem, 1)
        dve.wait_ge(self.stats_done.sem, at(self.stats_done, k, g + 1))
        dve.sem_inc(self.core.unwatched.sem, 1)
        nc.vector.bn_aggr(self.moments[:, g, :], self.stats[:, g, :]).then_inc(self.var_ready.sem, 1)

    def dve_normalise(self, dve, k):
        nc = self.nc
        dve.wait_ge(self.rstd_ready.sem, at(self.rstd_ready, k, 1))
        if self.index == 1:
            dve.wait_ge(self.final_done.sem, at(self.final_done, k, 0))
        if self.kind == 2:
            nc.vector.tensor_scalar(self.std[:, :], self.std[:, :], 1e-3, None, ALU.add).then_inc(self.std_done.sem, 1)
            dve.wait_ge(self.std_done.sem, at(self.std_done, k, 1))
            nc.vector.reciprocal(self.rstd[:, :], self.std[:, :]).then_inc(self.inverse_done.sem, 1)
            dve.wait_ge(self.inverse_done.sem, at(self.inverse_done, k, 1))
        for g in range(G):
            nc.vector.tensor_scalar(self.t[:, g, :], self.c[:, g, :], self.moments[:, g, 0:1], self.rstd[:, g:g + 1],
                                    ALU.subtract, ALU.mult).then_inc(self.t_ready.sem, 1)


    def pool_self(self, pool, k):
        nc = self.nc
        pool.wait_ge(self.diag_ready.sem, at(self.diag_ready, k, 1))
        pool.sem_inc(self.core.unwatched.sem, 1)
        for g in range(G):
            nc.gpsimd.tensor_scalar(self.self_bias[:, g, :], self.biases[2][:, :], self.diag_r[:, g:g + 1], 0.0,
                                    ALU.mult, ALU.add).then_inc(self.self_bias_ready.sem, 1)
        for g in range(G):
            n = 4 + 3 * g
            pool.wait_ge(self.self_bias_ready.sem, at(self.self_bias_ready, k, g + 1))
            pool.wait_ge(self.free[n % 2].sem, at(self.free[n % 2], k, n // 2 + 1))
            nc.gpsimd.tensor_tensor(self.self_[:, g, :], self.self_[:, g, :], self.self_bias[:, g, :], ALU.add
                                    ).then_inc(self.self_ready.sem, 1)

    def pool_w(self, pool, k, parity):
        nc = self.nc
        self.adj_loaded(pool, k, parity)
        pool.wait_ge(self.uw_done.sem, at(self.uw_done, k - 1, 0))
        pool.sem_inc(self.core.unwatched.sem, 1)
        nc.gpsimd.affine_select(out=self.w[:, parity, :, 0, :], in_=self.adjT[:, parity], compare_op=ALU.is_ge, fill=0.0,
                                base=0, pattern=[[0, G], [-1, P]], channel_multiplier=1
                                ).then_inc(self.w_ready.sem, 1)
        nc.gpsimd.affine_select(out=self.w[:, parity, :, 1, :], in_=self.adj[:, parity], compare_op=ALU.is_gt, fill=0.0,
                                base=0, pattern=[[0, G], [1, P]], channel_multiplier=-1
                                ).then_inc(self.w_ready.sem, 1)

    def pool_final(self, pool, k):
        nc = self.nc
        pool.wait_ge(self.t_ready.sem, at(self.t_ready, k, G))
        wide = [P, G, D]
        x = self.x.pair(k)
        nc.gpsimd.tensor_tensor(self.t[:, :, :], self.t[:, :, :], self.gamma[:, None, :].to_broadcast(wide), ALU.mult
                                ).then_inc(self.final_link.sem, 1)
        pool.wait_ge(self.final_link.sem, at(self.final_link, k, 1))
        nc.gpsimd.tensor_tensor(self.t[:, :, :], self.t[:, :, :], self.beta[:, None, :].to_broadcast(wide), ALU.add
                                ).then_inc(self.final_link.sem, 1)
        pool.wait_ge(self.final_link.sem, at(self.final_link, k, 2))
        pool.sem_inc(self.core.unwatched.sem, 1)
        nc.gpsimd.tensor_scalar(self.t[:, :, :], self.t[:, :, :], 0.0, 0.0, ALU.max, ALU.add
                                ).then_inc(self.final_link.sem, 1)
        pool.wait_ge(self.final_link.sem, at(self.final_link, k, 3))
        nc.gpsimd.tensor_tensor(x, x, self.t[:, :, :], ALU.add).then_inc(self.final_done.sem, 1)


def graph_phase(nc, core, kind):
    NP = core.pairs
    names = {1: ["l1_wl{}", "l1_wr{}", "l1_ws{}"], 2: ["l2_left{}", "l2_right{}", "l2_lin{}"]}[kind]
    bias_names = {1: ["l1_bl{}", "l1_br{}", "l1_bs{}"], 2: ["l2_b{}"]}[kind]
    with ExitStack() as ctx:
        def sb(name, shape, dt=F32):
            return ctx.enter_context(nc.sbuf_tensor(f"g{kind}_{name}", shape, dt))

        biases = [[sb(b.format(j), [P, D]) for b in bias_names] for j in range(2)]
        gammaT, betaT = sb("gammaT", [P, C]), sb("betaT", [P, C])
        gamma, beta = sb("gamma", [P, D]), sb("beta", [P, D])
        dram = core.dram
        consts = [(biases[j][i][:, :], dram[b.format(j)].partition_broadcast(P))
                  for j in range(2) for i, b in enumerate(bias_names)]
        consts += [(gammaT[:, :], dram[f"l{kind}_gammaT"]), (betaT[:, :], dram[f"l{kind}_betaT"]),
                   (gamma[:, :], dram[f"l{kind}_gamma"].partition_broadcast(P)),
                   (beta[:, :], dram[f"l{kind}_beta"].partition_broadcast(P))]
        weights = load_weights(nc, core, ctx, [n.format(j) for j in range(2) for n in names], consts)
        x = Residual(nc, core, ctx, f"l{kind}", dram["x_mid"], dram["x_mid"])
        norm = InputNorm(nc, core, ctx, f"l{kind}", x)
        A = Stage(nc, core, ctx, kind, 0, weights[:3], biases[0], norm)
        B = Stage(nc, core, ctx, kind, 1, weights[3:], biases[1], norm)
        A.source = (norm.xhat, norm.ready)
        B.source = (A.t, A.t_ready)
        B.x = x
        B.gammaT, B.betaT, B.gamma, B.beta = gammaT, betaT, gamma, beta
        core.signals.raise_fresh()
        block = ctx.enter_context(nc.Block())

        @block.sync
        def _(sp):
            for k in range(2):
                x.load(sp, norm, k, k)
            for k in range(2):
                A.load_adj(sp, k, k)
            for k in range(2):
                B.load_adj(sp, k, k)

            def store(k, parity):
                sp.wait_ge(B.final_done.sem, at(B.final_done, k, 1))
                sp.sem_inc(core.unwatched.sem, 1)
                x.store(sp, k, parity)

            def load(k, parity):
                A.load_adj(sp, k, parity)
                x.load(sp, norm, k, parity)
                B.load_adj(sp, k, parity)

            load(2, 0)

            for k, parity in late_steps(sp, NP):
                load(k + 2, parity)
                store(k - 1, 1 - parity)

            for k in range(NP - 3, NP):
                store(k, k % 2)
            x.wait_stored(sp)

        @block.tensor
        def _(pe):
            def solo(S, k):
                if kind == 1:
                    S.pe_linears(pe, k, 0, (0, 1, 2))
                    S.pe_linears(pe, k, 1, (0,))
                    S.pe_transpose_delta(pe, k)
                    S.pe_linears(pe, k, 1, (1, 2))
                else:
                    S.pe_messages(pe, k, 0, 1)
                    S.pe_messages(pe, k, 1, 0)
                    S.pe_messages(pe, k, 1, 1)
                    S.pe_linear(pe, k, S.weights[2], 0, 6)
                    S.pe_scores(pe, k)
                    S.pe_linear(pe, k, S.weights[2], 1, 7)

            def start(S, k):
                S.pe_transpose_h(pe, k)
                if kind == 1:
                    S.pe_gram(pe, k)
                else:
                    S.pe_messages(pe, k, 0, 0)

            start(A, 0)
            solo(A, 0)
            A.pe_context(pe, 0, 0)
            start(A, 1)
            A.pe_context(pe, 0, 1)

            for k, parity, more in steps(pe, NP):
                if kind == 1:
                    B.pe_transpose_h(pe, k)
                    A.pe_linears(pe, k + 1, 0, (0, 1, 2))
                    B.pe_gram(pe, k)
                    A.pe_linears(pe, k + 1, 1, (0,))
                    A.pe_transpose_delta(pe, k + 1)
                    A.pe_linears(pe, k + 1, 1, (1, 2))
                    B.pe_linears(pe, k, 0, (0,))
                    A.pe_context(pe, k + 1, 0)
                    B.pe_linears(pe, k, 0, (1,))
                    A.pe_context(pe, k + 1, 1)
                    B.pe_linears(pe, k, 0, (2,))
                    B.pe_linears(pe, k, 1, (0,))
                    B.pe_transpose_delta(pe, k)
                    B.pe_linears(pe, k, 1, (1, 2))
                    if more:
                        A.pe_transpose_h(pe, k + 2)
                    B.pe_context(pe, k, 0)
                    if more:
                        A.pe_gram(pe, k + 2)
                    B.pe_context(pe, k, 1)
                else:
                    B.pe_transpose_h(pe, k)
                    A.pe_messages(pe, k + 1, 0, 1)
                    A.pe_messages(pe, k + 1, 1, 0)
                    A.pe_messages(pe, k + 1, 1, 1)
                    A.pe_linear(pe, k + 1, A.weights[2], 0, 6)
                    B.pe_messages(pe, k, 0, 0)
                    B.pe_messages(pe, k, 0, 1)
                    A.pe_scores(pe, k + 1)
                    B.pe_messages(pe, k, 1, 0)
                    B.pe_messages(pe, k, 1, 1)
                    A.pe_linear(pe, k + 1, A.weights[2], 1, 7)
                    A.pe_context(pe, k + 1, 0)
                    B.pe_scores(pe, k)
                    A.pe_context(pe, k + 1, 1)
                    if more:
                        A.pe_transpose_h(pe, k + 2)
                    B.pe_linear(pe, k, B.weights[2], 0, 6)
                    B.pe_linear(pe, k, B.weights[2], 1, 7)
                    B.pe_context(pe, k, 0)
                    if more:
                        A.pe_messages(pe, k + 2, 0, 0)
                    B.pe_context(pe, k, 1)

            start(B, NP - 1)
            solo(B, NP - 1)
            B.pe_context(pe, NP - 1, 0)
            B.pe_context(pe, NP - 1, 1)

        @block.scalar
        def _(act):
            def solo(S, k):
                if kind == 1:
                    S.act_exps(act, k)
                    S.act_self(act, k, 0)
                    S.act_self(act, k, 1)
                else:
                    for side, half in ((0, 1), (1, 0), (1, 1)):
                        S.act_messages(act, k, side, half)
                    S.act_exp_u(act, k)

            def start(S, k):
                S.act_h(act, k)
                if kind == 2:
                    S.act_messages(act, k, 0, 0)

            norm.act_rstd(act, 0)
            start(A, 0)
            norm.act_rstd(act, 1)
            solo(A, 0)
            start(A, 1)
            A.act_rstd(act, 0)

            def body_1(k, more):
                A.act_exps(act, k + 1)
                B.act_h(act, k)
                A.act_self(act, k + 1, 0)
                B.act_exps(act, k)
                A.act_self(act, k + 1, 1)
                if more:
                    norm.act_rstd(act, k + 2)
                B.act_self(act, k, 0)
                A.act_rstd(act, k + 1)
                B.act_self(act, k, 1)
                if more:
                    A.act_h(act, k + 2)
                B.act_rstd(act, k)

            def body_2(k, more, late):
                B.act_h(act, k)
                A.act_messages(act, k + 1, 0, 1)
                if late:
                    B.act_rstd(act, k - 1)
                A.act_messages(act, k + 1, 1, 0)
                A.act_messages(act, k + 1, 1, 1)
                B.act_messages(act, k, 0, 0)
                B.act_messages(act, k, 0, 1)
                if more:
                    norm.act_rstd(act, k + 2)
                A.act_exp_u(act, k + 1)
                B.act_messages(act, k, 1, 0)
                B.act_messages(act, k, 1, 1)
                B.act_exp_u(act, k)
                if more:
                    A.act_h(act, k + 2)
                A.act_rstd(act, k + 1)
                if more:
                    A.act_messages(act, k + 2, 0, 0)

            if kind == 1:
                for k, _, more in steps(act, NP):
                    body_1(k, more)
            else:
                body_2(0, True, False)
                for k, _ in late_steps(act, NP):
                    body_2(k, True, True)
                body_2(NP - 2, False, True)
                B.act_rstd(act, NP - 2)

            start(B, NP - 1)
            solo(B, NP - 1)
            B.act_rstd(act, NP - 1)

        @block.vector
        def _(dve):
            def solo(S, k, parity):
                if kind == 1:
                    S.dve_delta(dve, k, parity)
                    S.dve_side(dve, k, 0, 1)
                    S.dve_side(dve, k, 1, 0)
                    S.dve_triangles(dve, k)
                    S.dve_side(dve, k, 1, 1)
                else:
                    S.dve_lin(dve, k, 0)
                    S.dve_weighted(dve, k, parity)
                    S.dve_delta_t(dve, k, parity)
                    S.dve_lin(dve, k, 1)

            def start(S, k):
                S.dve_low_h(dve, k)
                if kind == 1:
                    S.dve_shift(dve, k)
                    S.dve_side(dve, k, 0, 0)

            if kind == 2:
                for S in (A, B):
                    nc.vector.memset(S.lin[:, :, D:D + 1], 1.0)
            norm.dve_moments(dve, 0, 0)
            norm.dve_xhat(dve, 0)
            norm.dve_moments(dve, 1, 1)
            start(A, 0)
            norm.dve_xhat(dve, 1)
            solo(A, 0, 0)
            A.dve_context(dve, 0, 0)
            A.dve_low_h(dve, 1)
            if kind == 1:
                A.dve_shift(dve, 1)
            A.dve_context(dve, 0, 1)
            A.dve_normalise(dve, 0)
            if kind == 1:
                A.dve_side(dve, 1, 0, 0)

            def body_1(k, parity, more):
                A.dve_delta(dve, k + 1, 1 - parity)
                A.dve_side(dve, k + 1, 0, 1)
                B.dve_low_h(dve, k)
                B.dve_shift(dve, k)
                if more:
                    norm.dve_moments(dve, k + 2, parity)
                A.dve_side(dve, k + 1, 1, 0)
                A.dve_triangles(dve, k + 1)
                B.dve_delta(dve, k, parity)
                A.dve_side(dve, k + 1, 1, 1)
                if more:
                    norm.dve_xhat(dve, k + 2)
                B.dve_side(dve, k, 0, 0)
                A.dve_context(dve, k + 1, 0)
                B.dve_side(dve, k, 0, 1)
                A.dve_context(dve, k + 1, 1)
                A.dve_normalise(dve, k + 1)
                B.dve_side(dve, k, 1, 0)
                B.dve_triangles(dve, k)
                B.dve_side(dve, k, 1, 1)
                B.dve_context(dve, k, 0)
                if more:
                    A.dve_low_h(dve, k + 2)
                    A.dve_shift(dve, k + 2)
                B.dve_context(dve, k, 1)
                if more:
                    A.dve_side(dve, k + 2, 0, 0)
                B.dve_normalise(dve, k)

            def body_2(k, parity, more, late):
                B.dve_low_h(dve, k)
                if more:
                    norm.dve_moments(dve, k + 2, parity)
                if late:
                    B.dve_normalise(dve, k - 1)
                A.dve_lin(dve, k + 1, 0)
                A.dve_weighted(dve, k + 1, 1 - parity)
                A.dve_delta_t(dve, k + 1, 1 - parity)
                if more:
                    norm.dve_xhat(dve, k + 2)
                A.dve_lin(dve, k + 1, 1)
                A.dve_context(dve, k + 1, 0)
                B.dve_weighted(dve, k, parity)
                A.dve_context(dve, k + 1, 1)
                B.dve_delta_t(dve, k, parity)
                B.dve_lin(dve, k, 0)
                if more:
                    A.dve_low_h(dve, k + 2)
                B.dve_lin(dve, k, 1)
                A.dve_normalise(dve, k + 1)
                B.dve_context(dve, k, 0)
                B.dve_context(dve, k, 1)

            if kind == 1:
                for k, parity, more in steps(dve, NP):
                    body_1(k, parity, more)
            else:
                body_2(0, 0, True, False)
                for k, parity in late_steps(dve, NP):
                    body_2(k, parity, True, True)
                body_2(NP - 2, 0, False, True)
                B.dve_normalise(dve, NP - 2)

            start(B, NP - 1)
            solo(B, NP - 1, 1)
            B.dve_context(dve, NP - 1, 0)
            B.dve_context(dve, NP - 1, 1)
            B.dve_normalise(dve, NP - 1)

        @block.gpsimd
        def _(pool):
            if kind == 1:
                A.pool_self(pool, 0)
            else:
                A.pool_w(pool, 0, 0)
                A.pool_w(pool, 1, 1)
                B.pool_w(pool, 0, 0)

            for k, parity, more in steps(pool, NP):
                if kind == 1:
                    A.pool_self(pool, k + 1)
                    B.pool_self(pool, k)
                else:
                    if more:
                        A.pool_w(pool, k + 2, parity)
                    B.pool_w(pool, k + 1, 1 - parity)
                B.pool_final(pool, k)

            if kind == 1:
                B.pool_self(pool, NP - 1)
            B.pool_final(pool, NP - 1)

    core.signals.end_phase()



def graph_layers_kernel(nc, dram, graphs, phases=(0, 1, 2, 3)):
    core = Core()
    core.dram, core.pairs = dram, graphs // G
    with ExitStack() as ctx:
        def sb(name, shape, dt=F32):
            return ctx.enter_context(nc.sbuf_tensor(name, shape, dt))

        core.signals = Signals(nc, ctx, core.pairs)

        core.unwatched = core.signals.once("unwatched", 0)
        dram["x_mid"] = nc.dram_tensor("x_mid", [graphs, P, D], F32, kind="Internal").ap()
        core.ident = sb("ident", [P, P])
        core.triangles = sb("triangles", [P, 2, P])
        core.ln_eps = sb("ln_eps", [P, 1])
        core.eps_l1 = sb("eps_l1", [P, 1])
        core.eps_l2 = sb("eps_l2", [P, 1])
        filled = core.signals.once("constants_filled", 5)
        with nc.Block() as block:
            @block.gpsimd
            def _(pool):
                nc.gpsimd.memset(core.ident[:, :], 0.0).then_inc(filled.sem, 1)
                nc.gpsimd.memset(core.triangles[:, :, :], 1.0).then_inc(filled.sem, 1)
                nc.gpsimd.memset(core.ln_eps[:, :], LN_EPS)
                nc.gpsimd.memset(core.eps_l1[:, :], 1e-12)
                nc.gpsimd.memset(core.eps_l2[:, :], 1e-18)
                pool.wait_ge(filled.sem, filled.base + 2)
                nc.gpsimd.affine_select(out=core.ident[:, :], in_=core.ident[:, :], compare_op=ALU.not_equal, fill=1.0,
                                        base=0, pattern=[[-1, P]], channel_multiplier=1).then_inc(filled.sem, 1)
                nc.gpsimd.affine_select(out=core.triangles[:, 0, :], in_=core.triangles[:, 0, :],
                                        compare_op=ALU.is_gt, fill=0.0, base=0, pattern=[[-1, P]],
                                        channel_multiplier=1).then_inc(filled.sem, 1)
                nc.gpsimd.affine_select(out=core.triangles[:, 1, :], in_=core.triangles[:, 1, :],
                                        compare_op=ALU.is_gt, fill=0.0, base=0, pattern=[[1, P]],
                                        channel_multiplier=-1).then_inc(filled.sem, 1)

            @block.scalar
            def _(act):
                nc.scalar.preload_act_table_set("natural_log_exp_and_others")

        if 0 in phases:
            attention_phase(nc, core, ["l0_wq", "l0_wk", "l0_wv", "l0_wo"], ["l0_bv", "l0_bo"], True)
        if 1 in phases:
            graph_phase(nc, core, 1)
        if 2 in phases:
            graph_phase(nc, core, 2)
        if 3 in phases:
            attention_phase(nc, core, ["l3_wq", "l3_wk", "l3_wv"], ["l3_bv", "l3_bq", "l3_bk", "l3_beta"], False)


def layout(inputs):
    import numpy as np

    def chunks(w):
        return np.ascontiguousarray(w.reshape(C, P, D).transpose(1, 0, 2))

    def column(b):
        return np.ascontiguousarray(b.reshape(C, P).T)

    a = {n: np.asarray(v) for n, v in inputs.items()}
    out = {"x": a["x"], "adj": a["adj"], "adjT": np.ascontiguousarray(a["adj"].transpose(0, 2, 1))}
    for name, key in (("wq", "Wq"), ("wk", "Wk"), ("wv", "Wv"), ("wo", "Wo")):
        out[f"l0_{name}"] = chunks(a[f"L0_gnn_{key}"].T)
    out["l0_bv"], out["l0_bo"] = a["L0_gnn_bv"], a["L0_gnn_bo"]
    for j in range(2):
        for s in "lsr":
            out[f"l1_w{s}{j}"] = chunks(a[f"L1_gnn_W{s}"][j].T)
            out[f"l1_b{s}{j}"] = a[f"L1_gnn_b{s}"][j]
        for name, key in (("left", "W_left"), ("right", "W_right"), ("lin", "W_lin")):
            out[f"l2_{name}{j}"] = chunks(a[f"L2_gnn_{key}"][j].T)
        out[f"l2_b{j}"] = a["L2_gnn_b_lin"][j]
    for layer, g, b in ((1, "L1_gnn_ln_w", "L1_gnn_ln_b"), (2, "L2_gnn_ln_a", "L2_gnn_ln_b")):
        out[f"l{layer}_gammaT"], out[f"l{layer}_betaT"] = column(a[g][0]), column(a[b][0])
        out[f"l{layer}_gamma"], out[f"l{layer}_beta"] = a[g][1], a[b][1]
    for name, key in (("wq", "Wq"), ("wk", "Wk"), ("wv", "Wv")):
        out[f"l3_{name}"] = chunks(a[f"L3_gnn_{key}"])
    out["l3_bq"], out["l3_bk"] = column(a["L3_gnn_bq"]), column(a["L3_gnn_bk"])
    out["l3_bv"], out["l3_beta"] = a["L3_gnn_bv"], a["L3_gnn_beta"].reshape(1)
    return {n: np.ascontiguousarray(v) for n, v in out.items()}


def kernel(**inputs):
    import concourse.bacc as _bacc
    from concourse.bass_utils import run_bass_kernel_spmd

    arrays = layout(inputs)
    nc = _bacc.Bacc("TRN2", target_bir_lowering=False, num_devices=1)
    dram = {n: nc.dram_tensor(f"in_{n}", a.shape, F32, kind="ExternalInput").ap() for n, a in arrays.items()}
    dram["out"] = nc.dram_tensor("out", arrays["x"].shape, F32, kind="ExternalOutput").ap()
    graph_layers_kernel(nc, dram, arrays["x"].shape[0])
    got = run_bass_kernel_spmd(nc, [{f"in_{n}": a for n, a in arrays.items()}], core_ids=[0])
    return got.results[0]["out"]
```

```python
from contextlib import ExitStack

import concourse.bass as bass
from concourse import mybir

F32 = mybir.dt.float32
F32R = mybir.dt.float32r
ALU = mybir.AluOpType
ACT = mybir.ActivationFunctionType
AX = mybir.AxisListType

P = 128
D = 384
C = D // P
G = 2
T = G * P
HEADS = 12
HD = D // HEADS
R = P // HD
BANK = 512
LN_EPS = 1e-5


class Signal:

    def __init__(self, sem, per, base):
        self.sem, self.per, self.base = sem, per, base


class Signals:

    START = 32

    def __init__(self, nc, ctx, pairs):
        self.nc, self.ctx, self.pairs = nc, ctx, pairs
        self.count, self.sems, self.open, self.fresh = {}, {}, [], []

    def sem(self, name, start):
        if name not in self.sems:
            self.sems[name] = self.ctx.enter_context(self.nc.semaphore(name))
            self.count[name] = start
            if start:
                self.fresh.append(self.sems[name])
        return self.sems[name]

    def __call__(self, name, per):
        sem = self.sem(name, self.START)
        self.open.append((name, per))
        return Signal(sem, per, self.count[name])

    def once(self, name, n):
        sem = self.sem(name, 0)
        self.count[name] += n
        return Signal(sem, 0, self.count[name] - n)

    def raise_fresh(self, sp):
        for sem in self.fresh:
            sp.sem_inc(sem, self.START)
        self.fresh = []

    def end_phase(self):
        for name, per in self.open:
            self.count[name] += per * self.pairs
        self.open = []


def at(signal, k, j):
    return signal.base + signal.per * k + j


def dma_at(signal, k, parity):
    return signal.base + signal.per * (k - parity) + 2 * signal.per


class Split:

    def __init__(self, hi, lo):
        self.hi, self.lo = hi, lo


def product(nc, out, left, right):
    n = len(left)
    for c in range(n):
        (lh, ll), (rh, rl) = left[c], right[c]
        nc.tensor.matmul(out, lh, rh, start=c == 0, stop=False)
        nc.tensor.matmul(out, lh, rl, start=False, stop=False)
        ins = nc.tensor.matmul(out, ll, rh, start=False, stop=c == n - 1)
    return ins


def steps(engine, pairs):
    with engine.Fori(0, (pairs - 2) // 2) as i:
        for parity in range(2):
            yield 2 * i + parity, parity, True
    yield pairs - 2, 0, False


def late_steps(engine, pairs):
    with engine.Fori(0, (pairs - 4) // 2) as i:
        yield 2 * i + 1, 1
        yield 2 * i + 2, 0
    yield pairs - 3, 1


class Core:
    pass


class Weights:

    MOST = 6
    BY_DVE = 3
    NAMES = [["l0_wq", "l0_wk", "l0_wv", "l0_wo"],
             ["l1_wl0", "l1_wr0", "l1_ws0", "l1_wl1", "l1_wr1", "l1_ws1"],
             ["l2_left0", "l2_right0", "l2_lin0", "l2_left1", "l2_right1", "l2_lin1"],
             ["l3_wq", "l3_wk", "l3_wv"]]

    def __init__(self, nc, core, ctx, phases):
        self.nc, self.core, self.phases = nc, core, phases
        self.raw = [ctx.enter_context(nc.sbuf_tensor(f"weight{j}_raw", [P, C, D], F32)) for j in range(self.MOST)]
        self.all_arrived = [core.signals.once(f"weight{j}_in", 0) for j in range(self.MOST)]
        self.hi_done = core.signals.once("weight_hi_done", 0)
        self.lo_done = core.signals.once("weight_lo_done", 0)
        self.pool_lo_done = core.signals.once("weight_pool_lo_done", 0)

    def begin_phase(self, ctx, phase):
        self.names = self.NAMES[phase]
        self.arrived = [self.core.signals.once(f"weight{j}_in", 16) for j in range(len(self.names))]
        self.hi_done = self.core.signals.once("weight_hi_done", len(self.names))
        self.by_dve = min(self.BY_DVE, len(self.names))
        self.lo_done = self.core.signals.once("weight_lo_done", self.by_dve)
        self.pool_lo_done = self.core.signals.once("weight_pool_lo_done", len(self.names) - self.by_dve)
        part = lambda name: ctx.enter_context(self.nc.sbuf_tensor(name, [P, C, D], F32R))
        self.parts = [Split(part(f"{n}_hi"), part(f"{n}_lo")) for n in self.names]
        later = [p for p in self.phases if p > phase]
        self.next = self.NAMES[later[0]] if later else []
        return self.parts

    def load(self, sp, names):
        for j, name in enumerate(names):
            sp.dma_start(self.raw[j][:, :, :], self.core.dram[name]).then_inc(self.all_arrived[j].sem, 16)

    def load_next(self, sp):
        if self.next:
            self.wait_all_split(sp)
            self.load(sp, self.next)

    def act_high(self, act, first, last):
        for j in range(first, last):
            act.wait_ge(self.arrived[j].sem, self.arrived[j].base + 16)
            self.nc.scalar.activation(self.parts[j].hi[:, :, :], self.raw[j][:, :, :], ACT.Copy
                                      ).then_inc(self.hi_done.sem, 1)

    def dve_low(self, dve, first, last):
        for j in range(first, last):
            dve.wait_ge(self.hi_done.sem, self.hi_done.base + j + 1)
            self.nc.vector.tensor_tensor(self.parts[j].lo[:, :, :], self.raw[j][:, :, :],
                                         self.parts[j].hi[:, :, :].bitcast(F32), ALU.subtract
                                         ).then_inc(self.lo_done.sem, 1)

    def pool_low(self, pool):
        for j in range(self.by_dve, len(self.names)):
            pool.wait_ge(self.hi_done.sem, self.hi_done.base + j + 1)
            self.nc.gpsimd.tensor_tensor(self.parts[j].lo[:, :, :], self.raw[j][:, :, :],
                                         self.parts[j].hi[:, :, :].bitcast(F32), ALU.subtract
                                         ).then_inc(self.pool_lo_done.sem, 1)

    def wait_split(self, pe, n):
        pe.wait_ge(self.lo_done.sem, self.lo_done.base + n)

    def wait_all_split(self, engine):
        self.wait_split(engine, self.by_dve)
        if len(self.names) > self.by_dve:
            engine.wait_ge(self.pool_lo_done.sem, self.pool_lo_done.base + len(self.names) - self.by_dve)


class Constants:

    def __init__(self, core, copies):
        self.copies = copies
        self.arrived = core.signals.once("constants_in", 16 * len(copies))

    def load(self, sp):
        for dst, src in self.copies:
            sp.dma_start(dst, src).then_inc(self.arrived.sem, 16)

    def wait(self, engine):
        engine.wait_ge(self.arrived.sem, self.arrived.base + 16 * len(self.copies))



class Residual:

    SLOTS = 4

    def __init__(self, nc, core, src, dst):
        self.nc, self.core, self.src, self.dst, self.buffer = nc, core, src, dst, core.x_places
        self.loaded = [core.signals(f"x_loaded{j}", 8) for j in range(2)]
        self.stored = [core.signals(f"x_stored{j}", 8) for j in range(2)]

    def pair(self, k):
        return self.buffer[:, bass.ds(G * (k & (self.SLOTS - 1)), G), :]

    def graph(self, k, g):
        return self.buffer[:, bass.ds(G * (k & (self.SLOTS - 1)) + g, 1), :][:, 0, :]

    def wait_loaded(self, engine, k, parity):
        engine.wait_ge(self.loaded[parity].sem, dma_at(self.loaded[parity], k, parity))

    def load(self, sp, norm, k, parity):
        sp.wait_ge(self.stored[parity].sem, dma_at(self.stored[parity], k - self.SLOTS, parity))
        sp.sem_inc(self.core.unwatched.sem, 1)
        sp.wait_ge(norm.ready.sem, at(norm.ready, k - 1, 0))
        sp.sem_inc(self.core.unwatched.sem, 1)
        sp.dma_start(self.pair(k), self.src[bass.ds(G * k, G), :, :].rearrange("g p d -> p g d")
                     ).then_inc(self.loaded[parity].sem, 16)

    def start(self, sp, norm):
        if not self.core.x_ahead:
            self.load(sp, norm, 0, 0)
            self.core.weights.load(sp, self.core.weights.names)
            self.load(sp, norm, 1, 1)

    def store(self, sp, k, parity):
        sp.dma_start(self.dst[bass.ds(G * k, G), :, :].rearrange("g p d -> p g d"), self.pair(k)
                     ).then_inc(self.stored[parity].sem, 16)

    def finish(self, sp, store):
        pairs = self.core.pairs
        ahead = self.core.x_ahead = bool(self.core.weights.next)

        def load_ahead(j):
            sp.wait_ge(self.stored[j].sem, self.stored[j].base + self.stored[j].per * (pairs - 2))
            sp.dma_start(self.pair(j), self.core.dram["x_mid"][G * j:G * j + G].rearrange("g p d -> p g d")
                         ).then_inc(self.loaded[j].sem, 16)

        store(pairs - 3, 1)
        if ahead:
            load_ahead(0)
        store(pairs - 2, 0)
        if ahead:
            load_ahead(1)
        store(pairs - 1, 1)
        if not ahead:
            for s in self.stored:
                sp.wait_ge(s.sem, s.base + s.per * pairs)


class InputNorm:

    def __init__(self, nc, core, ctx, tag, x):
        self.nc, self.core, self.x = nc, core, x
        self.xhat = ctx.enter_context(nc.sbuf_tensor(f"{tag}_xhat", [P, G, D], F32))
        self.stats = ctx.enter_context(nc.sbuf_tensor(f"{tag}_in_stats", [P, G, 6], F32))
        self.moments = ctx.enter_context(nc.sbuf_tensor(f"{tag}_in_moments", [P, G, 2], F32))
        self.log = ctx.enter_context(nc.sbuf_tensor(f"{tag}_in_log", [P, G], F32))
        self.rstd = ctx.enter_context(nc.sbuf_tensor(f"{tag}_in_rstd", [P, G], F32))
        self.stats_done = core.signals("in_stats_done", G)
        self.var_ready = core.signals("in_var_ready", G)
        self.log_done = core.signals("in_log_done", 1)
        self.rstd_ready = core.signals("in_rstd_ready", 1)
        self.ready = core.signals("xhat_ready", G)

    def dve_moments(self, dve, k, parity):
        nc = self.nc
        self.x.wait_loaded(dve, k, parity)
        for g in range(G):
            nc.vector.bn_stats(self.stats[:, g, :], self.x.graph(k, g)).then_inc(self.stats_done.sem, 1)
        for g in range(G):
            dve.wait_ge(self.stats_done.sem, at(self.stats_done, k, g + 1))
            dve.sem_inc(self.core.unwatched.sem, 1)
            nc.vector.bn_aggr(self.moments[:, g, :], self.stats[:, g, :]).then_inc(self.var_ready.sem, 1)

    def act_rstd(self, act, k):
        nc = self.nc
        act.wait_ge(self.var_ready.sem, at(self.var_ready, k, G))
        nc.scalar.activation(self.log[:, :], self.moments[:, :, 1], ACT.Ln, bias=self.core.ln_eps[:, :]
                             ).then_inc(self.log_done.sem, 1)
        act.wait_ge(self.log_done.sem, at(self.log_done, k, 1))
        nc.scalar.activation(self.rstd[:, :], self.log[:, :], ACT.Exp, scale=-0.5).then_inc(self.rstd_ready.sem, 1)

    def dve_xhat(self, dve, k):
        nc = self.nc
        dve.wait_ge(self.rstd_ready.sem, at(self.rstd_ready, k, 1))
        for g in range(G):
            nc.vector.tensor_scalar(self.xhat[:, g, :], self.x.graph(k, g), self.moments[:, g, 0:1],
                                    self.rstd[:, g:g + 1], ALU.subtract, ALU.mult).then_inc(self.ready.sem, 1)



def attention_phase(nc, core, biases, is_first):
    NP = core.pairs
    HP = HD + 1
    scale = D ** -0.5 if is_first else HD ** -0.5
    tag = "l0" if is_first else "l3"
    with ExitStack() as ctx:
        def sb(name, shape, dt=F32):
            return ctx.enter_context(nc.sbuf_tensor(f"{tag}_{name}", shape, dt))

        bv = sb("bv", [P, D])
        consts = [(bv[:, :], core.dram[biases[0]].partition_broadcast(P))]
        if is_first:
            bo = sb("bo", [P, D])
            consts.append((bo[:, :], core.dram[biases[1]].partition_broadcast(P)))
        else:
            bqk_raw = sb("bqk_raw", [P, 2, C])
            bqk = sb("bqk", [P, 2, C])
            beta = sb("beta", [P, 1])
            consts.append((bqk_raw[:, 0, :], core.dram[biases[1]]))
            consts.append((bqk_raw[:, 1, :], core.dram[biases[2]]))
            consts.append((beta[:, :], core.dram[biases[3]].partition_broadcast(P)))
        constants = Constants(core, consts)
        weights = core.weights.begin_phase(ctx, 0 if is_first else 3)
        wq, wk, wv = weights[:3]

        x = Residual(nc, core, core.dram["x" if is_first else "x_mid"], core.dram["x_mid" if is_first else "out"])
        norm = InputNorm(nc, core, ctx, tag, x)
        hT = Split(sb("hT_hi", [P, C, T], F32R), sb("hT_lo", [P, C, T], F32R))
        qT = sb("qT", [P, 2, C, T])
        kT = sb("kT", [P, 2, C, T])
        v = sb("v", [P, 2, G, HEADS, HP])
        adj = sb("adj", [P, 2, G, P])
        bias = sb("bias", [P, 2, G, P])
        s = sb("s", [P, G, R, C, P])
        probs = sb("probs", [P, G, R, C, P])
        s_max = sb("s_max", [P, G, R, C])
        s_shift = sb("s_shift", [P, G, R, C])
        s_abs = sb("s_abs", [P, G, R, C])
        probsT = sb("probsT", [P, G, C, R, P])
        rsum = sb("rsum", [P, G, C, R])
        factor = sb("factor", [P, G, C, R])
        o = sb("o", [P, G, C, R, HD])
        if is_first:
            oT = Split(sb("oT_hi", [P, G, C, P], F32R), sb("oT_lo", [P, G, C, P], F32R))
            xb = sb("xb", [P, G, D])

        SO = ctx.enter_context(nc.psum_tensor(f"{tag}_SO", [P, R, BANK], F32))
        S = SO[:, :, 0:C * P].rearrange("p r (c k) -> p r c k", c=C)
        O = SO[:, :, C * P:C * P + C * HP].rearrange("p r (c e) -> p r c e", c=C)
        back = [ctx.enter_context(nc.psum_tensor(f"{tag}_back{j}", [P, BANK], F32)) for j in range(2)]
        front = [ctx.enter_context(nc.psum_tensor(f"{tag}_front{j}", [P, BANK], F32)) for j in range(2)]

        sig = core.signals
        FI = 4
        BI = 5 if is_first else 3
        PROBS_T = [[g * C + c for c in range(C)] for g in range(G)]
        O_T = [2 * C + 2 * g for g in range(G)]
        OUT = [2 * C + 2 * g + 1 for g in range(G)]
        front_full = [sig(f"front_full{j}", FI) for j in range(2)]
        front_free = [sig(f"front_free{j}", FI) for j in range(2)]
        back_full = [sig(f"back_full{j}", BI) for j in range(2)]
        back_free = [sig(f"back_free{j}", BI) for j in range(2)]
        adj_in = [sig(f"adj_in{j}", 8) for j in range(2)]
        hi_ready = sig("hi_ready", 2)
        s_full = sig("s_full", G)
        s_taken = sig("s_taken", G)
        max_ready = sig("max_ready", G)
        shift_ready = sig("shift_ready", G)
        probs_ready = sig("probs_ready", G * C)
        o_full = sig("o_full", G)
        rsum_ready = sig("rsum_ready", G)
        o_ready = sig("o_ready", G)
        bias_ready = sig("bias_ready", 1)
        ones_set = core.signals.once("ones_set", 1)
        if is_first:
            abs_ready = sig("abs_ready", G)
            factor_ready = sig("factor_ready", G)
            oT_hi_ready = sig("oT_hi_ready", G)
            xb_ready = sig("xb_ready", G)
        else:
            x_done = sig("x_done", G)
            bias_step = sig("bias_step", 2)
            bqk_set = core.signals.once("bqk_set", 1)

        def wait_in(engine, signals, k, parity):
            engine.wait_ge(signals[parity].sem, dma_at(signals[parity], k, parity))

        block = ctx.enter_context(nc.Block())

        @block.sync
        def _(sp):
            def load_adj(k, parity):
                sp.wait_ge(bias_ready.sem, at(bias_ready, k - 1, 0))
                sp.sem_inc(core.unwatched.sem, 1)
                sp.dma_start(adj[:, parity, :, :],
                             core.dram["adj"][bass.ds(G * k, G), :, :].rearrange("g p d -> p g d")
                             ).then_inc(adj_in[parity].sem, 16)

            def store(k, parity):
                if is_first:
                    for n in OUT:
                        sp.wait_ge(back_free[n % 2].sem, at(back_free[n % 2], k, n // 2 + 1))
                        sp.sem_inc(core.unwatched.sem, 1)
                else:
                    sp.wait_ge(x_done.sem, at(x_done, k, G))
                    sp.sem_inc(core.unwatched.sem, 1)
                x.store(sp, k, parity)

            core.signals.raise_fresh(sp)
            x.start(sp, norm)
            for k in range(2):
                load_adj(k, k)
            constants.load(sp)
            core.weights.load_next(sp)

            x.load(sp, norm, 2, 0)
            load_adj(2, 0)

            for k, parity in late_steps(sp, NP):
                x.load(sp, norm, k + 2, parity)
                load_adj(k + 2, parity)
                store(k - 1, 1 - parity)

            x.finish(sp, store)

        @block.tensor
        def _(pe):
            def take_front(k, n):
                pe.wait_ge(front_free[n % 2].sem, at(front_free[n % 2], k, n // 2))
                return front[n % 2]

            def take_back(k, n):
                pe.wait_ge(back_free[n % 2].sem, at(back_free[n % 2], k, n // 2))
                return back[n % 2]

            def transpose_h(k, n):
                pe.wait_ge(norm.ready.sem, at(norm.ready, k, G))
                slot = take_front(k, n)
                for i, c in enumerate(((0, 1), (2,))[n]):
                    for g in range(G):
                        ins = nc.tensor.transpose(slot[:, i * T + g * P:i * T + (g + 1) * P],
                                                  norm.xhat[:, g, c * P:(c + 1) * P], core.ident[:, :])
                ins.then_inc(front_full[n % 2].sem, 1)

            def project(k, which, o_c):
                w, n = weights[which], 2 + 2 * which + o_c // 2
                if o_c == 1:
                    slot = front[n % 2][:, T:2 * T]
                else:
                    if which == 0 and o_c == 0:
                        pe.wait_ge(front_free[1].sem, at(front_free[1], k, 1))
                    slot = take_front(k, n)[:, 0:T]
                f = slice(o_c * P, (o_c + 1) * P)
                ins = product(nc, slot, [(w.hi[:, c, f], w.lo[:, c, f]) for c in range(C)],
                              [(hT.hi[:, c, :], hT.lo[:, c, :]) for c in range(C)])
                if o_c > 0:
                    ins.then_inc(front_full[n % 2].sem, 1)

            def values(k, g):
                n = 6 + g
                slot = take_front(k, n)
                t = slice(g * P, (g + 1) * P)
                product(nc, slot[:, 0:D], [(hT.hi[:, c, t], hT.lo[:, c, t]) for c in range(C)],
                        [(wv.hi[:, c, :], wv.lo[:, c, :]) for c in range(C)]).then_inc(front_full[n % 2].sem, 1)

            def scores(k, parity, g, c):
                if c == 0:
                    pe.wait_ge(front_free[0].sem, at(front_free[0], k, 3))
                    pe.wait_ge(front_free[1].sem, at(front_free[1], k, 3))
                    pe.wait_ge(o_ready.sem, at(o_ready, k, 0))
                    pe.wait_ge(s_taken.sem, at(s_taken, k, g))
                t = slice(g * P, (g + 1) * P)
                for r in range(R):
                    rows = slice(r * HD, (r + 1) * HD)
                    ins = nc.tensor.matmul(S[:, r, c, :], qT[rows, parity, c, t], kT[rows, parity, c, t],
                                           start=True, stop=True)
                if c == C - 1:
                    ins.then_inc(s_full.sem, 1)

            def transpose_probs(k, g, c):
                n = PROBS_T[g][c]
                pe.wait_ge(probs_ready.sem, at(probs_ready, k, g * C + c + 1))
                slot = take_back(k, n)
                for r in range(R):
                    ins = nc.tensor.transpose(slot[:, r * P:(r + 1) * P], probs[:, g, r, c, :], core.ident[:, :])
                ins.then_inc(back_full[n % 2].sem, 1)

            def attend(k, parity, g, c):
                if c == 0:
                    pe.wait_ge(front_free[0].sem, at(front_free[0], k, 4))
                    pe.wait_ge(front_free[1].sem, at(front_free[1], k, 4))
                    pe.wait_ge(s_taken.sem, at(s_taken, k, G))
                    pe.wait_ge(o_ready.sem, at(o_ready, k, g))
                n = PROBS_T[g][c]
                pe.wait_ge(back_free[n % 2].sem, at(back_free[n % 2], k, n // 2 + 1))
                for r in range(R):
                    ins = nc.tensor.matmul(O[:, r, c, :], probsT[:, g, c, r, :], v[:, parity, g, c * R + r, :],
                                           start=True, stop=True)
                if c == C - 1:
                    ins.then_inc(o_full.sem, 1)

            def transpose_o(k, g):
                pe.wait_ge(o_ready.sem, at(o_ready, k, g + 1))
                n = O_T[g]
                slot = take_back(k, n)
                for c in range(C):
                    ins = nc.tensor.transpose(slot[:, c * P:(c + 1) * P],
                                              o[:, g, c, :, :].rearrange("p r e -> p (r e)"), core.ident[:, :])
                ins.then_inc(back_full[n % 2].sem, 1)

            def project_out(k, g):
                wo = weights[3]
                pe.wait_ge(back_free[O_T[g] % 2].sem, at(back_free[O_T[g] % 2], k, O_T[g] // 2 + 1))
                n = OUT[g]
                slot = take_back(k, n)
                product(nc, slot[:, 0:D], [(oT.hi[:, g, c, :], oT.lo[:, g, c, :]) for c in range(C)],
                        [(wo.hi[:, c, :], wo.lo[:, c, :]) for c in range(C)]).then_inc(back_full[n % 2].sem, 1)

            transpose_h(0, 0)
            transpose_h(0, 1)
            for which in range(2):
                core.weights.wait_split(pe, which + 1)
                for c in range(C):
                    project(0, which, c)
            core.weights.wait_all_split(pe)
            values(0, 0)
            values(0, 1)
            transpose_h(1, 0)
            transpose_h(1, 1)
            scores(0, 0, 0, 0)

            for k, parity, more in steps(pe, NP):
                scores(k, parity, 0, 1)
                project(k + 1, 0, 0)
                scores(k, parity, 0, 2)
                project(k + 1, 0, 1)
                project(k + 1, 0, 2)
                if is_first:
                    project(k + 1, 1, 0)
                    scores(k, parity, 1, 0)
                    scores(k, parity, 1, 1)
                    project(k + 1, 1, 1)
                    scores(k, parity, 1, 2)
                else:
                    scores(k, parity, 1, 0)
                    project(k + 1, 1, 0)
                    scores(k, parity, 1, 1)
                    scores(k, parity, 1, 2)
                    project(k + 1, 1, 1)
                transpose_probs(k, 0, 0)
                transpose_probs(k, 0, 1)
                project(k + 1, 1, 2)
                transpose_probs(k, 0, 2)
                attend(k, parity, 0, 0)
                attend(k, parity, 0, 1)
                if is_first:
                    values(k + 1, 0)
                    attend(k, parity, 0, 2)
                    transpose_probs(k, 1, 0)
                else:
                    attend(k, parity, 0, 2)
                    transpose_probs(k, 1, 0)
                    values(k + 1, 0)
                transpose_probs(k, 1, 1)
                attend(k, parity, 1, 0)
                transpose_probs(k, 1, 2)
                if is_first:
                    transpose_o(k, 0)
                    attend(k, parity, 1, 1)
                    values(k + 1, 1)
                    attend(k, parity, 1, 2)
                    project_out(k, 0)
                    transpose_o(k, 1)
                    if more:
                        transpose_h(k + 2, 0)
                    scores(k + 1, 1 - parity, 0, 0)
                    if more:
                        transpose_h(k + 2, 1)
                    project_out(k, 1)
                else:
                    attend(k, parity, 1, 1)
                    attend(k, parity, 1, 2)
                    values(k + 1, 1)
                    if more:
                        transpose_h(k + 2, 0)
                    scores(k + 1, 1 - parity, 0, 0)
                    if more:
                        transpose_h(k + 2, 1)

            k, parity = NP - 1, 1
            scores(k, parity, 0, 1)
            scores(k, parity, 0, 2)
            for c in range(C):
                scores(k, parity, 1, c)
            for g in range(G):
                for c in range(C):
                    transpose_probs(k, g, c)
                if is_first and g == 1:
                    transpose_o(k, 0)
                for c in range(C):
                    attend(k, parity, g, c)
            if is_first:
                project_out(k, 0)
                transpose_o(k, 1)
                project_out(k, 1)

        @block.scalar
        def _(act):
            def high_h(k):
                for n, chunks in enumerate(((0, 1), (2,))):
                    act.wait_ge(front_full[n].sem, at(front_full[n], k, 1))
                    src = front[n][:, 0:len(chunks) * T].rearrange("p (c t) -> p c t", t=T)
                    nc.scalar.activation(hT.hi[:, chunks[0]:chunks[-1] + 1, :], src, ACT.Relu).then_inc(hi_ready.sem, 1)

            def copy_qk(k, parity, which, half):
                n = 2 + 2 * which + half
                dst = (qT, kT)[which]
                chunks = ((0, 1), (2,))[half]
                act.wait_ge(front_full[n % 2].sem, at(front_full[n % 2], k, n // 2 + 1))
                if is_first:
                    src = front[n % 2][:, 0:len(chunks) * T].rearrange("p (c t) -> p c t", t=T)
                    ins = nc.scalar.activation(dst[:, parity, chunks[0]:chunks[-1] + 1, :], src, ACT.Copy,
                                               scale=scale if which == 0 else 1.0)
                else:
                    for i, c in enumerate(chunks):
                        ins = nc.scalar.activation(dst[:, parity, c, :], front[n % 2][:, i * T:(i + 1) * T],
                                                   ACT.Identity, bias=bqk[:, which, c:c + 1],
                                                   scale=scale if which == 0 else 1.0)
                ins.then_inc(front_free[n % 2].sem, 1)

            def exps(k, g, c):
                act.wait_ge(shift_ready.sem, at(shift_ready, k, g + 1))
                for r in range(R):
                    ins = nc.scalar.activation(probs[:, g, r, c, :], s[:, g, r, c, :], ACT.Exp,
                                               bias=s_shift[:, g, r, c:c + 1])
                ins.then_inc(probs_ready.sem, 1)

            def copy_probsT(k, g, c):
                n = PROBS_T[g][c]
                act.wait_ge(back_full[n % 2].sem, at(back_full[n % 2], k, n // 2 + 1))
                nc.scalar.activation(probsT[:, g, c].rearrange("p r k -> p (r k)"), back[n % 2][:, :],
                                     ACT.Copy).then_inc(back_free[n % 2].sem, 1)

            def high_o(k, g):
                n = O_T[g]
                act.wait_ge(back_full[n % 2].sem, at(back_full[n % 2], k, n // 2 + 1))
                nc.scalar.activation(oT.hi[:, g].rearrange("p c t -> p (c t)"), back[n % 2][:, 0:D],
                                     ACT.Copy).then_inc(oT_hi_ready.sem, 1)

            core.weights.act_high(act, 0, 1)
            norm.act_rstd(act, 0)
            core.weights.act_high(act, 1, 2)
            high_h(0)
            core.weights.act_high(act, 2, len(weights))
            if not is_first:
                constants.wait(act)
                nc.scalar.activation(bqk[:, 0, :], bqk_raw[:, 0, :], ACT.Copy, scale=scale)
                nc.scalar.activation(bqk[:, 1, :], bqk_raw[:, 1, :], ACT.Copy).then_inc(bqk_set.sem, 1)
                act.wait_ge(bqk_set.sem, bqk_set.base + 1)
            norm.act_rstd(act, 1)
            for which in range(2):
                for half in range(2):
                    copy_qk(0, 0, which, half)
            high_h(1)

            for k, parity, more in steps(act, NP):
                copy_qk(k + 1, 1 - parity, 0, 0)
                copy_qk(k + 1, 1 - parity, 0, 1)
                exps(k, 0, 0)
                exps(k, 0, 1)
                exps(k, 0, 2)
                copy_probsT(k, 0, 0)
                copy_qk(k + 1, 1 - parity, 1, 0)
                copy_probsT(k, 0, 1)
                copy_qk(k + 1, 1 - parity, 1, 1)
                copy_probsT(k, 0, 2)
                exps(k, 1, 0)
                exps(k, 1, 1)
                copy_probsT(k, 1, 0)
                exps(k, 1, 2)
                copy_probsT(k, 1, 1)
                if more:
                    norm.act_rstd(act, k + 2)
                copy_probsT(k, 1, 2)
                if is_first:
                    high_o(k, 0)
                    high_o(k, 1)
                if more:
                    high_h(k + 2)

            k = NP - 1
            for g in range(G):
                for c in range(C):
                    exps(k, g, c)
                for c in range(C):
                    copy_probsT(k, g, c)
            if is_first:
                high_o(k, 0)
                high_o(k, 1)

        @block.vector
        def _(dve):
            def low_h(k):
                for n, chunks in enumerate(((0, 1), (2,))):
                    dve.wait_ge(hi_ready.sem, at(hi_ready, k, n + 1))
                    cs = slice(chunks[0], chunks[-1] + 1)
                    src = front[n][:, 0:len(chunks) * T].rearrange("p (c t) -> p c t", t=T)
                    nc.vector.scalar_tensor_tensor(out=hT.lo[:, cs, :], in0=src, scalar=0.0,
                                                   in1=hT.hi[:, cs, :].bitcast(F32), op0=ALU.max,
                                                   op1=ALU.subtract).then_inc(front_free[n].sem, 1)

            def take_scores(k, parity, g):
                if g == 0:
                    dve.wait_ge(bias_ready.sem, at(bias_ready, k, 1))
                dve.wait_ge(s_full.sem, at(s_full, k, g + 1))
                dve.wait_ge(probs_ready.sem, at(probs_ready, k - 1, (g + 1) * C))
                b = bias[:, parity, g, :]
                nc.vector.tensor_tensor(s[:, g], S, b[:, None, None, :].to_broadcast([P, R, C, P]), ALU.add
                                        ).then_inc(s_taken.sem, 1)

            def shift_scores(k, g):
                dve.wait_ge(s_taken.sem, at(s_taken, k, g + 1))
                nc.vector.tensor_reduce(s_max[:, g], s[:, g], AX.X, ALU.max).then_inc(max_ready.sem, 1)
                dve.wait_ge(max_ready.sem, at(max_ready, k, g + 1))
                nc.vector.tensor_scalar(s_shift[:, g], s_max[:, g], -1.0, None, ALU.mult
                                        ).then_inc(shift_ready.sem, 1)

            def abs_scores(k, g):
                if is_first:
                    nc.vector.tensor_reduce(s_abs[:, g], s[:, g], AX.X, ALU.max, apply_absolute_value=True
                                            ).then_inc(abs_ready.sem, 1)

            def take_values(k, parity, g):
                dve.wait_ge(front_full[g].sem, at(front_full[g], k, FI))
                nc.vector.tensor_tensor(v[:, parity, g, :, 0:HD],
                                        front[g][:, 0:D].rearrange("p (h e) -> p h e", e=HD),
                                        bv[:, :].rearrange("p (h e) -> p h e", e=HD), ALU.add
                                        ).then_inc(front_free[g].sem, 1)

            def normalise(k, g):
                dve.wait_ge(o_full.sem, at(o_full, k, g + 1))
                sums = O[:, :, :, HD].rearrange("p r c -> p c r")
                nc.vector.reciprocal(rsum[:, g], sums).then_inc(rsum_ready.sem, 1)
                dve.wait_ge(rsum_ready.sem, at(rsum_ready, k, g + 1))
                f = rsum
                if is_first:
                    f = factor
                    dve.wait_ge(abs_ready.sem, at(abs_ready, k, g + 1))
                    nc.vector.scalar_tensor_tensor(
                        out=factor[:, g], in0=s_abs[:, g].rearrange("p r c -> p c r"), scalar=0.0,
                        in1=rsum[:, g], op0=ALU.not_equal, op1=ALU.mult).then_inc(factor_ready.sem, 1)
                    dve.wait_ge(factor_ready.sem, at(factor_ready, k, g + 1))
                nc.vector.tensor_tensor(o[:, g], O[:, :, :, 0:HD].rearrange("p r c e -> p c r e"),
                                        f[:, g, :, :, None].to_broadcast([P, C, R, HD]), ALU.mult
                                        ).then_inc(o_ready.sem, 1)

            def low_o(k, g):
                n = O_T[g]
                dve.wait_ge(oT_hi_ready.sem, at(oT_hi_ready, k, g + 1))
                nc.vector.tensor_tensor(oT.lo[:, g].rearrange("p c t -> p (c t)"), back[n % 2][:, 0:D],
                                        oT.hi[:, g].rearrange("p c t -> p (c t)").bitcast(F32), ALU.subtract
                                        ).then_inc(back_free[n % 2].sem, 1)

            def update_x(k, g):
                xg = x.graph(k, g)
                if is_first:
                    n = OUT[g]
                    dve.wait_ge(xb_ready.sem, at(xb_ready, k, g + 1))
                    dve.wait_ge(back_full[n % 2].sem, at(back_full[n % 2], k, n // 2 + 1))
                    nc.vector.tensor_tensor(xg, back[n % 2][:, 0:D], xb[:, g, :], ALU.add
                                            ).then_inc(back_free[n % 2].sem, 1)
                else:
                    dve.wait_ge(o_ready.sem, at(o_ready, k, g + 1))
                    nc.vector.tensor_tensor(xg, xg, o[:, g].rearrange("p c r e -> p (c r e)"), ALU.add
                                            ).then_inc(x_done.sem, 1)

            norm.dve_moments(dve, 0, 0)
            norm.dve_xhat(dve, 0)
            core.weights.dve_low(dve, 0, 1)
            low_h(0)
            core.weights.dve_low(dve, 1, 3)
            norm.dve_moments(dve, 1, 1)
            norm.dve_xhat(dve, 1)
            constants.wait(dve)
            dve.wait_ge(ones_set.sem, ones_set.base + 1)
            take_values(0, 0, 0)
            take_values(0, 0, 1)
            low_h(1)

            for k, parity, more in steps(dve, NP):
                take_scores(k, parity, 0)
                shift_scores(k, 0)
                abs_scores(k, 0)
                take_scores(k, parity, 1)
                shift_scores(k, 1)
                if is_first:
                    if more:
                        norm.dve_moments(dve, k + 2, parity)
                    normalise(k, 0)
                    abs_scores(k, 1)
                    take_values(k + 1, 1 - parity, 0)
                    low_o(k, 0)
                    if more:
                        norm.dve_xhat(dve, k + 2)
                    take_values(k + 1, 1 - parity, 1)
                    normalise(k, 1)
                    update_x(k, 0)
                    low_o(k, 1)
                    if more:
                        low_h(k + 2)
                else:
                    if more:
                        norm.dve_moments(dve, k + 2, parity)
                    normalise(k, 0)
                    update_x(k, 0)
                    take_values(k + 1, 1 - parity, 0)
                    if more:
                        norm.dve_xhat(dve, k + 2)
                    normalise(k, 1)
                    take_values(k + 1, 1 - parity, 1)
                    if more:
                        low_h(k + 2)
                update_x(k, 1)

            k = NP - 1
            for g in range(G):
                take_scores(k, 1, g)
                shift_scores(k, g)
                abs_scores(k, g)
            normalise(k, 0)
            if is_first:
                low_o(k, 0)
            normalise(k, 1)
            update_x(k, 0)
            if is_first:
                low_o(k, 1)
            update_x(k, 1)

        @block.gpsimd
        def _(pool):
            def add_bo(k, parity):
                x.wait_loaded(pool, k, parity)
                for g in range(G):
                    n = OUT[g]
                    pool.wait_ge(back_free[n % 2].sem, at(back_free[n % 2], k - 1, n // 2 + 1))
                    nc.gpsimd.tensor_tensor(xb[:, g, :], x.graph(k, g), bo[:, :],
                                            ALU.add).then_inc(xb_ready.sem, 1)

            def make_bias(k, parity):
                wait_in(pool, adj_in, k, parity)
                pool.wait_ge(s_taken.sem, at(s_taken, k - 1, 0))
                pool.sem_inc(core.unwatched.sem, 1)
                if is_first:
                    nc.gpsimd.tensor_scalar(bias[:, parity], adj[:, parity], 2.0, 0.0, ALU.mult, ALU.add
                                            ).then_inc(bias_ready.sem, 1)
                    return
                nc.gpsimd.tensor_scalar(bias[:, parity], adj[:, parity], 0.0, -9e15, ALU.is_le, ALU.mult
                                        ).then_inc(bias_step.sem, 1)
                nc.gpsimd.tensor_scalar(adj[:, parity], adj[:, parity], beta[:, 0:1], 0.0, ALU.mult, ALU.add
                                        ).then_inc(bias_step.sem, 1)
                pool.wait_ge(bias_step.sem, at(bias_step, k, 2))
                nc.gpsimd.tensor_tensor(bias[:, parity], bias[:, parity], adj[:, parity], ALU.add
                                        ).then_inc(bias_ready.sem, 1)

            nc.gpsimd.memset(v[:, :, :, :, HD:HP], 1.0).then_inc(ones_set.sem, 1)
            core.weights.pool_low(pool)
            constants.wait(pool)
            make_bias(0, 0)

            for k, parity, more in steps(pool, NP):
                make_bias(k + 1, 1 - parity)
                if is_first:
                    add_bo(k, parity)

            if is_first:
                add_bo(NP - 1, 1)


    sig.end_phase()



class Stage:

    def __init__(self, nc, core, ctx, kind, index, weights, biases, norm):
        self.nc, self.core, self.kind, self.index, self.norm = nc, core, kind, index, norm
        self.weights, self.biases = weights, biases
        tag = f"{'first' if index == 0 else 'second'}"
        self.name = f"l{kind}_{tag}"
        sig = lambda n, per: core.signals(f"{tag}_{n}", per)

        def sb(name, shape, dt=F32):
            return ctx.enter_context(nc.sbuf_tensor(f"{self.name}_{name}", shape, dt))

        self.hT_f = sb("hT", [P, C, T])
        self.hT = Split(sb("hT_hi", [P, C, T], F32R), sb("hT_lo", [P, C, T], F32R))
        self.adj = sb("adj", [P, 2, G, P])
        self.c = sb("c", [P, G, D])
        self.t = sb("t", [P, G, D])
        self.stats = sb("stats", [P, G, 6])
        self.moments = sb("moments", [P, G, 2])
        self.log = sb("log", [P, G])
        self.rstd = sb("rstd", [P, G])
        self.r = sb("r", [P, G])
        self.q = sb("q", [P, G])
        if kind == 1:
            self.left = sb("hl", [P, G, D])
            self.right = sb("hr", [P, G, D])
            self.self_ = sb("hs", [P, G, D])
            self.self_bias = sb("hs_bias", [P, G, D])
            self.e = sb("e", [P, G, P])
            self.E = sb("delta", [P, G, P])
            self.ET = sb("deltaT", [P, G, 2, P])
            self.sum_e = sb("sum_e", [P, G])
            self.sum_d = sb("sum_d", [P, G])
            self.diag = sb("diag", [P, G])
            self.diag_r = sb("diag_r", [P, G])
            self.row_max = sb("row_max", [P, G])
            self.shift = sb("shift", [P, G])
            self.junk = sb("junk", [P, G, P])
        else:
            self.adjT = sb("adjT", [P, 2, G, P])
            self.mT = sb("mT", [P, 2, C, T])
            self.lin = sb("lin", [P, G, D + 1])
            self.w = sb("w", [P, 2, G, 2, P])
            self.uw = sb("uw", [P, G, 2, P])
            self.u = sb("u", [P, G, P])
            self.e = sb("e", [P, G, P])
            self.E = sb("deltaT", [P, G, P])
            self.std = sb("std", [P, G])
        ps = lambda n: ctx.enter_context(nc.psum_tensor(f"{self.name}_{n}", [P, BANK], F32))
        self.ring = [ps("ring0"), ps("ring1")]
        self.U = ps("U")
        self.ctx = ps("ctx")

        self.full = [sig(f"ring_full{j}", 4) for j in range(2)]
        self.free = [sig(f"ring_free{j}", 4) for j in range(2)]
        self.adj_in = [sig(f"adj_in{j}", 8 * kind) for j in range(2)]
        self.hi_ready = sig("hi_ready", 1)
        self.lo_ready = sig("lo_ready", 1)
        self.u_full = sig("u_full", 1)
        self.shift_ready = sig("shift_ready", 1)
        self.e_ready = sig("e_ready", G if kind == 1 else 1)
        self.E_ready = sig("delta_ready", G if kind == 1 else 1)
        if kind == 1:
            self.ET_full = sig("deltaT_full", 1)
            self.ET_ready = sig("deltaT_ready", 1)
            self.diag_ready = sig("diag_ready", 1)
            self.self_bias_ready = sig("self_bias_ready", G)
            self.self_ready = sig("self_ready", G)
        else:
            self.w_ready = sig("w_ready", 2)
        self.ctx_full = sig("ctx_full", G)
        self.ctx_free = sig("ctx_free", G)
        self.var_ready = sig("var_ready", G)
        self.log_done = sig("log_done", 1)
        self.rstd_ready = sig("rstd_ready", 1)
        self.t_ready = sig("t_ready", G)
        self.stats_done = sig("stats_done", G)
        self.q_done = sig("q_done", kind)
        self.r_done = sig("r_done", kind)
        if kind == 1:
            self.max_done = sig("max_done", 1)
            self.diag_done = sig("diag_done", G)
        else:
            self.uw_done = sig("uw_done", 1)
            self.std_done = sig("std_done", 1)
            self.inverse_done = sig("inverse_done", 1)
        if index == 1:
            self.scaled = sig("scaled", G)
            self.relu_done = sig("relu_done", 1)
            self.final_done = sig("final_done", 1)


    def take(self, pe, k, n):
        pe.wait_ge(self.free[n % 2].sem, at(self.free[n % 2], k, n // 2))
        return self.ring[n % 2]

    def h_copied(self, engine, k):
        for slot in range(2):
            engine.wait_ge(self.free[slot].sem, at(self.free[slot], k, 1))

    def adj_loaded(self, engine, k, parity):
        engine.wait_ge(self.adj_in[parity].sem, dma_at(self.adj_in[parity], k, parity))


    def load_adj(self, sp, k, parity):
        sp.wait_ge(self.E_ready.sem, at(self.E_ready, k - 1, 0))
        sp.sem_inc(self.core.unwatched.sem, 1)
        sp.dma_start(self.adj[:, parity, :, :],
                     self.core.dram["adj"][bass.ds(G * k, G), :, :].rearrange("g p d -> p g d")
                     ).then_inc(self.adj_in[parity].sem, 16)
        if self.kind == 2:
            sp.dma_start(self.adjT[:, parity, :, :],
                         self.core.dram["adjT"][bass.ds(G * k, G), :, :].rearrange("g p d -> p g d")
                         ).then_inc(self.adj_in[parity].sem, 16)


    def pe_transpose_h(self, pe, k):
        nc = self.nc
        src, ready = self.source
        pe.wait_ge(ready.sem, at(ready, k, G))
        for n, chunks in enumerate(((0, 1), (2,))):
            slot = self.take(pe, k, n)
            for i, c in enumerate(chunks):
                for g in range(G):
                    ins = nc.tensor.transpose(slot[:, i * T + g * P:i * T + (g + 1) * P],
                                              src[:, g, c * P:(c + 1) * P], self.core.ident[:, :])
            ins.then_inc(self.full[n % 2].sem, 1)

    def pe_linear(self, pe, k, w, g, n):
        slot = self.take(pe, k, n)
        t = slice(g * P, (g + 1) * P)
        product(self.nc, slot[:, 0:D], [(self.hT.hi[:, c, t], self.hT.lo[:, c, t]) for c in range(C)],
                [(w.hi[:, c, :], w.lo[:, c, :]) for c in range(C)]).then_inc(self.full[n % 2].sem, 1)

    def pe_messages(self, pe, k, side, half):
        nc, w, n = self.nc, self.weights[side], 2 + 2 * side + half
        pe.wait_ge(self.lo_ready.sem, at(self.lo_ready, k, 1))
        slot = self.take(pe, k, n)
        for i, o_c in enumerate(((0, 1), (2,))[half]):
            f = slice(o_c * P, (o_c + 1) * P)
            ins = product(nc, slot[:, i * T:(i + 1) * T],
                          [(w.hi[:, c, f], w.lo[:, c, f]) for c in range(C)],
                          [(self.hT.hi[:, c, :], self.hT.lo[:, c, :]) for c in range(C)])
        ins.then_inc(self.full[n % 2].sem, 1)


    def pe_gram(self, pe, k):
        nc = self.nc
        self.h_copied(pe, k)
        pe.wait_ge(self.E_ready.sem, at(self.E_ready, k, 0))
        for g in range(G):
            t = slice(g * P, (g + 1) * P)
            for c in range(C):
                ins = nc.tensor.matmul(self.U[:, t], self.hT_f[:, c, t], self.hT_f[:, c, t],
                                       start=c == 0, stop=c == C - 1)
        ins.then_inc(self.u_full.sem, 1)

    def pe_linears(self, pe, k, g, which):
        pe.wait_ge(self.lo_ready.sem, at(self.lo_ready, k, 1))
        for i in which:
            self.pe_linear(pe, k, self.weights[i], g, 2 + 3 * g + i)

    def pe_transpose_delta(self, pe, k):
        nc = self.nc
        pe.wait_ge(self.E_ready.sem, at(self.E_ready, k, G))
        pe.wait_ge(self.ET_ready.sem, at(self.ET_ready, k, 0))
        for g in range(G):
            ins = nc.tensor.transpose(self.U[:, T + g * P:T + (g + 1) * P], self.E[:, g, :], self.core.ident[:, :])
        ins.then_inc(self.ET_full.sem, 1)

    def pe_context(self, pe, k, g):
        (self.pe_side_contexts if self.kind == 1 else self.pe_gather)(pe, k, g)

    def pe_side_contexts(self, pe, k, g):
        nc = self.nc
        if g == 0:
            pe.wait_ge(self.ET_ready.sem, at(self.ET_ready, k, 1))
        for n in (2 + 3 * g, 3 + 3 * g):
            pe.wait_ge(self.free[n % 2].sem, at(self.free[n % 2], k, n // 2 + 1))
        pe.wait_ge(self.ctx_free.sem, at(self.ctx_free, k, g))
        nc.tensor.matmul(self.ctx[:, 0:D], self.ET[:, g, 0, :], self.left[:, g, :], start=True, stop=False)
        nc.tensor.matmul(self.ctx[:, 0:D], self.ET[:, g, 1, :], self.right[:, g, :], start=False, stop=True
                         ).then_inc(self.ctx_full.sem, 1)


    def pe_scores(self, pe, k):
        nc = self.nc
        self.h_copied(pe, k)
        for n in (4, 5):
            pe.wait_ge(self.free[n % 2].sem, at(self.free[n % 2], k, n // 2 + 1))
        pe.wait_ge(self.shift_ready.sem, at(self.shift_ready, k, 0))
        for g in range(G):
            t = slice(g * P, (g + 1) * P)
            for side in range(2):
                out = self.U[:, (2 * g + side) * P:(2 * g + side + 1) * P]
                for c in range(C):
                    ins = nc.tensor.matmul(out, self.mT[:, side, c, t], self.hT_f[:, c, t],
                                           start=c == 0, stop=c == C - 1)
        ins.then_inc(self.u_full.sem, 1)

    def pe_gather(self, pe, k, g):
        nc = self.nc
        if g == 0:
            pe.wait_ge(self.E_ready.sem, at(self.E_ready, k, 1))
        n = 6 + g
        pe.wait_ge(self.free[n % 2].sem, at(self.free[n % 2], k, n // 2 + 1))
        pe.wait_ge(self.ctx_free.sem, at(self.ctx_free, k, g))
        nc.tensor.matmul(self.ctx[:, 0:D + 1], self.E[:, g, :], self.lin[:, g, :], start=True, stop=True
                         ).then_inc(self.ctx_full.sem, 1)


    def act_h(self, act, k):
        nc = self.nc
        for n, chunks in enumerate(((0, 1), (2,))):
            act.wait_ge(self.full[n].sem, at(self.full[n], k, 1))
            for i, c in enumerate(chunks):
                src = self.ring[n][:, i * T:(i + 1) * T]
                if self.index == 0:
                    ins = nc.scalar.activation(self.hT_f[:, c, :], src, ACT.Relu)
                else:
                    ins = nc.scalar.activation(self.hT_f[:, c, :], src, ACT.Relu, bias=self.betaT[:, c:c + 1],
                                               scale=self.gammaT[:, c:c + 1])
            ins.then_inc(self.free[n].sem, 1)
        self.h_copied(act, k)
        nc.scalar.activation(self.hT.hi[:, :, :], self.hT_f[:, :, :], ACT.Copy).then_inc(self.hi_ready.sem, 1)

    def act_exps(self, act, k):
        nc = self.nc
        act.wait_ge(self.shift_ready.sem, at(self.shift_ready, k, 1))
        for g in range(G):
            nc.scalar.activation(self.e[:, g, :], self.U[:, g * P:(g + 1) * P], ACT.Exp,
                                 bias=self.shift[:, g:g + 1], scale=D ** -0.5, accum_out=self.sum_e[:, g:g + 1]
                                 ).then_inc(self.e_ready.sem, 1)

    def act_self(self, act, k, g):
        nc = self.nc
        n = 4 + 3 * g
        if g == 0:
            act.wait_ge(self.diag_ready.sem, at(self.diag_ready, k, 1))
        act.wait_ge(self.full[n % 2].sem, at(self.full[n % 2], k, n // 2 + 1))
        nc.scalar.activation(self.self_[:, g, :], self.ring[n % 2][:, 0:D], ACT.Copy,
                             scale=self.diag_r[:, g:g + 1]).then_inc(self.free[n % 2].sem, 1)

    def act_messages(self, act, k, side, half):
        nc, n = self.nc, 2 + 2 * side + half
        chunks = ((0, 1), (2,))[half]
        act.wait_ge(self.full[n % 2].sem, at(self.full[n % 2], k, n // 2 + 1))
        nc.scalar.activation(self.mT[:, side, chunks[0]:chunks[-1] + 1, :],
                             self.ring[n % 2][:, 0:len(chunks) * T].rearrange("p (c t) -> p c t", t=T),
                             ACT.Copy).then_inc(self.free[n % 2].sem, 1)

    def act_exp_u(self, act, k):
        nc = self.nc
        act.wait_ge(self.shift_ready.sem, at(self.shift_ready, k, 1))
        nc.scalar.activation(self.e[:, :, :], self.u[:, :, :], ACT.Exp, scale=D ** -0.5).then_inc(self.e_ready.sem, 1)

    def act_rstd(self, act, k):
        nc = self.nc
        act.wait_ge(self.var_ready.sem, at(self.var_ready, k, G))
        if self.kind == 1:
            nc.scalar.activation(self.log[:, :], self.moments[:, :, 1], ACT.Ln, bias=self.core.eps_l1[:, :]
                                 ).then_inc(self.log_done.sem, 1)
            act.wait_ge(self.log_done.sem, at(self.log_done, k, 1))
            nc.scalar.activation(self.rstd[:, :], self.log[:, :], ACT.Exp, scale=-0.5).then_inc(self.rstd_ready.sem, 1)
        else:
            nc.scalar.activation(self.log[:, :], self.moments[:, :, 1], ACT.Ln, bias=self.core.eps_l2[:, :],
                                 scale=D / (D - 1)).then_inc(self.log_done.sem, 1)
            act.wait_ge(self.log_done.sem, at(self.log_done, k, 1))
            nc.scalar.activation(self.std[:, :], self.log[:, :], ACT.Exp, scale=0.5).then_inc(self.rstd_ready.sem, 1)


    def dve_low_h(self, dve, k):
        dve.wait_ge(self.hi_ready.sem, at(self.hi_ready, k, 1))
        self.nc.vector.tensor_tensor(self.hT.lo[:, :, :], self.hT_f[:, :, :], self.hT.hi[:, :, :].bitcast(F32),
                                     ALU.subtract).then_inc(self.lo_ready.sem, 1)

    def dve_shift(self, dve, k):
        nc = self.nc
        dve.wait_ge(self.u_full.sem, at(self.u_full, k, 1))
        nc.vector.tensor_reduce(self.row_max[:, :], self.U[:, 0:T].rearrange("p (g j) -> p g j", g=G),
                                AX.X, ALU.max).then_inc(self.max_done.sem, 1)
        dve.wait_ge(self.max_done.sem, at(self.max_done, k, 1))
        nc.vector.tensor_scalar(self.shift[:, :], self.row_max[:, :], -(D ** -0.5), None, ALU.mult
                                ).then_inc(self.shift_ready.sem, 1)

    def dve_delta(self, dve, k, parity):
        nc = self.nc
        self.adj_loaded(dve, k, parity)
        for g in range(G):
            dve.wait_ge(self.e_ready.sem, at(self.e_ready, k, g + 1))
            nc.vector.scalar_tensor_tensor(out=self.E[:, g, :], in0=self.e[:, g, :], scalar=1.0,
                                           in1=self.adj[:, parity, g, :], op0=ALU.mult, op1=ALU.mult,
                                           accum_out=self.sum_d[:, g:g + 1]).then_inc(self.E_ready.sem, 1)
        dve.wait_ge(self.E_ready.sem, at(self.E_ready, k, G))
        nc.vector.scalar_tensor_tensor(out=self.q[:, :], in0=self.sum_e[:, :], scalar=1e-10, in1=self.sum_d[:, :],
                                       op0=ALU.mult, op1=ALU.add).then_inc(self.q_done.sem, 1)
        for g in range(G):
            nc.vector.scalar_tensor_tensor(out=self.junk[:, g, :], in0=self.E[:, g, :], scalar=1.0,
                                           in1=self.core.ident[:, :], op0=ALU.mult, op1=ALU.mult,
                                           accum_out=self.diag[:, g:g + 1]).then_inc(self.diag_done.sem, 1)
        dve.wait_ge(self.q_done.sem, at(self.q_done, k, 1))
        nc.vector.reciprocal(self.r[:, :], self.q[:, :]).then_inc(self.r_done.sem, 1)
        dve.wait_ge(self.diag_done.sem, at(self.diag_done, k, G))
        dve.wait_ge(self.r_done.sem, at(self.r_done, k, 1))
        nc.vector.tensor_tensor(self.diag_r[:, :], self.diag[:, :], self.r[:, :], ALU.mult
                                ).then_inc(self.diag_ready.sem, 1)

    def dve_side(self, dve, k, g, i):
        n = 2 + 3 * g + i
        dve.wait_ge(self.full[n % 2].sem, at(self.full[n % 2], k, n // 2 + 1))
        self.nc.vector.tensor_tensor((self.left, self.right)[i][:, g, :], self.ring[n % 2][:, 0:D],
                                     self.biases[i][:, :], ALU.add).then_inc(self.free[n % 2].sem, 1)

    def dve_triangles(self, dve, k):
        nc = self.nc
        dve.wait_ge(self.ET_full.sem, at(self.ET_full, k, 1))
        src = self.U[:, T:2 * T].rearrange("p (g i) -> p g i", g=G)[:, :, None, :].to_broadcast([P, G, 2, P])
        mask = self.core.triangles[:, None, :, :].to_broadcast([P, G, 2, P])
        nc.vector.tensor_tensor(self.ET[:, :, :, :], src, mask, ALU.mult).then_inc(self.ET_ready.sem, 1)

    def dve_weighted(self, dve, k, parity):
        nc = self.nc
        dve.wait_ge(self.w_ready.sem, at(self.w_ready, k, 2))
        dve.wait_ge(self.u_full.sem, at(self.u_full, k, 1))
        nc.vector.tensor_tensor(self.uw[:, :, :, :].rearrange("p g s i -> p (g s i)"), self.U[:, :],
                                self.w[:, parity].rearrange("p g s i -> p (g s i)"), ALU.mult
                                ).then_inc(self.uw_done.sem, 1)
        dve.wait_ge(self.uw_done.sem, at(self.uw_done, k, 1))
        nc.vector.tensor_tensor(self.u[:, :, :], self.uw[:, :, 0, :], self.uw[:, :, 1, :], ALU.add
                                ).then_inc(self.shift_ready.sem, 1)

    def dve_delta_t(self, dve, k, parity):
        nc = self.nc
        dve.wait_ge(self.e_ready.sem, at(self.e_ready, k, 1))
        nc.vector.tensor_tensor(self.E[:, :, :], self.e[:, :, :], self.adjT[:, parity], ALU.mult
                                ).then_inc(self.E_ready.sem, 1)

    def dve_lin(self, dve, k, g):
        nc = self.nc
        n = 6 + g
        dve.wait_ge(self.full[n % 2].sem, at(self.full[n % 2], k, n // 2 + 1))
        nc.vector.tensor_tensor(self.lin[:, g, 0:D], self.ring[n % 2][:, 0:D], self.biases[0][:, :], ALU.add
                                ).then_inc(self.free[n % 2].sem, 1)

    def dve_context(self, dve, k, g):
        nc = self.nc
        dve.wait_ge(self.ctx_full.sem, at(self.ctx_full, k, g + 1))
        if self.kind == 1:
            dve.wait_ge(self.self_ready.sem, at(self.self_ready, k, g + 1))
            ins = nc.vector.scalar_tensor_tensor(out=self.c[:, g, :], in0=self.ctx[:, 0:D], scalar=self.r[:, g:g + 1],
                                                 in1=self.self_[:, g, :], op0=ALU.mult, op1=ALU.add)
        else:
            nc.vector.tensor_scalar(self.q[:, g:g + 1], self.ctx[:, D:D + 1], 1e-10, None, ALU.add
                                    ).then_inc(self.q_done.sem, 1)
            dve.wait_ge(self.q_done.sem, at(self.q_done, k, g + 1))
            nc.vector.reciprocal(self.r[:, g:g + 1], self.q[:, g:g + 1]).then_inc(self.r_done.sem, 1)
            dve.wait_ge(self.r_done.sem, at(self.r_done, k, g + 1))
            ins = nc.vector.tensor_scalar(self.c[:, g, :], self.ctx[:, 0:D], self.r[:, g:g + 1], None, ALU.mult)
        ins.then_inc(self.ctx_free.sem, 1)
        dve.wait_ge(self.ctx_free.sem, at(self.ctx_free, k, g + 1))
        nc.vector.bn_stats(self.stats[:, g, :], self.c[:, g, :]).then_inc(self.stats_done.sem, 1)
        dve.wait_ge(self.stats_done.sem, at(self.stats_done, k, g + 1))
        dve.sem_inc(self.core.unwatched.sem, 1)
        nc.vector.bn_aggr(self.moments[:, g, :], self.stats[:, g, :]).then_inc(self.var_ready.sem, 1)

    def dve_normalise(self, dve, k):
        nc = self.nc
        dve.wait_ge(self.rstd_ready.sem, at(self.rstd_ready, k, 1))
        if self.index == 1:
            dve.wait_ge(self.final_done.sem, at(self.final_done, k, 0))
        if self.kind == 2:
            nc.vector.tensor_scalar(self.std[:, :], self.std[:, :], 1e-3, None, ALU.add).then_inc(self.std_done.sem, 1)
            dve.wait_ge(self.std_done.sem, at(self.std_done, k, 1))
            nc.vector.reciprocal(self.rstd[:, :], self.std[:, :]).then_inc(self.inverse_done.sem, 1)
            dve.wait_ge(self.inverse_done.sem, at(self.inverse_done, k, 1))
        if self.index == 0:
            for g in range(G):
                nc.vector.tensor_scalar(self.t[:, g, :], self.c[:, g, :], self.moments[:, g, 0:1], self.rstd[:, g:g + 1],
                                        ALU.subtract, ALU.mult).then_inc(self.t_ready.sem, 1)
            return
        for g in range(G):
            nc.vector.scalar_tensor_tensor(out=self.t[:, g, :], in0=self.c[:, g, :], scalar=self.moments[:, g, 0:1],
                                           in1=self.gamma[:, :], op0=ALU.subtract, op1=ALU.mult
                                           ).then_inc(self.scaled.sem, 1)
        for g in range(G):
            dve.wait_ge(self.scaled.sem, at(self.scaled, k, g + 1))
            nc.vector.scalar_tensor_tensor(out=self.t[:, g, :], in0=self.t[:, g, :], scalar=self.rstd[:, g:g + 1],
                                           in1=self.beta[:, :], op0=ALU.mult, op1=ALU.add
                                           ).then_inc(self.t_ready.sem, 1)


    def pool_self(self, pool, k):
        nc = self.nc
        pool.wait_ge(self.diag_ready.sem, at(self.diag_ready, k, 1))
        pool.sem_inc(self.core.unwatched.sem, 1)
        for g in range(G):
            nc.gpsimd.tensor_scalar(self.self_bias[:, g, :], self.biases[2][:, :], self.diag_r[:, g:g + 1], 0.0,
                                    ALU.mult, ALU.add).then_inc(self.self_bias_ready.sem, 1)
        for g in range(G):
            n = 4 + 3 * g
            pool.wait_ge(self.self_bias_ready.sem, at(self.self_bias_ready, k, g + 1))
            pool.wait_ge(self.free[n % 2].sem, at(self.free[n % 2], k, n // 2 + 1))
            nc.gpsimd.tensor_tensor(self.self_[:, g, :], self.self_[:, g, :], self.self_bias[:, g, :], ALU.add
                                    ).then_inc(self.self_ready.sem, 1)

    def pool_w(self, pool, k, parity):
        nc = self.nc
        self.adj_loaded(pool, k, parity)
        pool.wait_ge(self.uw_done.sem, at(self.uw_done, k - 1, 0))
        pool.sem_inc(self.core.unwatched.sem, 1)
        nc.gpsimd.affine_select(out=self.w[:, parity, :, 0, :], in_=self.adjT[:, parity], compare_op=ALU.is_ge, fill=0.0,
                                base=0, pattern=[[0, G], [-1, P]], channel_multiplier=1
                                ).then_inc(self.w_ready.sem, 1)
        nc.gpsimd.affine_select(out=self.w[:, parity, :, 1, :], in_=self.adj[:, parity], compare_op=ALU.is_gt, fill=0.0,
                                base=0, pattern=[[0, G], [1, P]], channel_multiplier=-1
                                ).then_inc(self.w_ready.sem, 1)

    def final(self, engine, ops, k):
        engine.wait_ge(self.t_ready.sem, at(self.t_ready, k, G))
        engine.sem_inc(self.core.unwatched.sem, 1)
        ops.tensor_scalar(self.t[:, :, :], self.t[:, :, :], 0.0, 0.0, ALU.max, ALU.add).then_inc(self.relu_done.sem, 1)
        engine.wait_ge(self.relu_done.sem, at(self.relu_done, k, 1))
        x = self.x.pair(k)
        ops.tensor_tensor(x, x, self.t[:, :, :], ALU.add).then_inc(self.final_done.sem, 1)


def graph_phase(nc, core, kind):
    NP = core.pairs
    bias_names = {1: ["l1_bl{}", "l1_br{}", "l1_bs{}"], 2: ["l2_b{}"]}[kind]
    with ExitStack() as ctx:
        def sb(name, shape, dt=F32):
            return ctx.enter_context(nc.sbuf_tensor(f"g{kind}_{name}", shape, dt))

        biases = [[sb(b.format(j), [P, D]) for b in bias_names] for j in range(2)]
        gammaT, betaT = sb("gammaT", [P, C]), sb("betaT", [P, C])
        gamma, beta = sb("gamma", [P, D]), sb("beta", [P, D])
        dram = core.dram
        consts = [(biases[j][i][:, :], dram[b.format(j)].partition_broadcast(P))
                  for j in range(2) for i, b in enumerate(bias_names)]
        consts += [(gammaT[:, :], dram[f"l{kind}_gammaT"]), (betaT[:, :], dram[f"l{kind}_betaT"]),
                   (gamma[:, :], dram[f"l{kind}_gamma"].partition_broadcast(P)),
                   (beta[:, :], dram[f"l{kind}_beta"].partition_broadcast(P))]
        constants = Constants(core, consts)
        weights = core.weights.begin_phase(ctx, kind)
        x = Residual(nc, core, dram["x_mid"], dram["x_mid"])
        norm = InputNorm(nc, core, ctx, f"l{kind}", x)
        A = Stage(nc, core, ctx, kind, 0, weights[:3], biases[0], norm)
        B = Stage(nc, core, ctx, kind, 1, weights[3:], biases[1], norm)
        A.source = (norm.xhat, norm.ready)
        B.source = (A.t, A.t_ready)
        B.x = x
        B.gammaT, B.betaT, B.gamma, B.beta = gammaT, betaT, gamma, beta
        block = ctx.enter_context(nc.Block())

        @block.sync
        def _(sp):
            core.signals.raise_fresh(sp)
            x.start(sp, norm)
            A.load_adj(sp, 0, 0)
            constants.load(sp)
            A.load_adj(sp, 1, 1)
            for k in range(2):
                B.load_adj(sp, k, k)
            core.weights.load_next(sp)

            def store(k, parity):
                sp.wait_ge(B.final_done.sem, at(B.final_done, k, 1))
                sp.sem_inc(core.unwatched.sem, 1)
                x.store(sp, k, parity)

            def load(k, parity):
                A.load_adj(sp, k, parity)
                x.load(sp, norm, k, parity)
                B.load_adj(sp, k, parity)

            load(2, 0)

            for k, parity in late_steps(sp, NP):
                load(k + 2, parity)
                store(k - 1, 1 - parity)

            x.finish(sp, store)

        @block.tensor
        def _(pe):
            def solo(S, k):
                if kind == 1:
                    core.weights.wait_split(pe, 2)
                    S.pe_linears(pe, k, 0, (0, 1))
                    core.weights.wait_split(pe, 3)
                    S.pe_linears(pe, k, 0, (2,))
                    S.pe_linears(pe, k, 1, (0,))
                    S.pe_transpose_delta(pe, k)
                    S.pe_linears(pe, k, 1, (1, 2))
                else:
                    S.pe_messages(pe, k, 0, 1)
                    core.weights.wait_split(pe, 2)
                    S.pe_messages(pe, k, 1, 0)
                    S.pe_messages(pe, k, 1, 1)
                    core.weights.wait_split(pe, 3)
                    S.pe_linear(pe, k, S.weights[2], 0, 6)
                    S.pe_scores(pe, k)
                    S.pe_linear(pe, k, S.weights[2], 1, 7)

            def start(S, k):
                S.pe_transpose_h(pe, k)
                if kind == 1:
                    S.pe_gram(pe, k)
                else:
                    core.weights.wait_split(pe, 1)
                    S.pe_messages(pe, k, 0, 0)

            start(A, 0)
            solo(A, 0)
            A.pe_context(pe, 0, 0)
            start(A, 1)
            A.pe_context(pe, 0, 1)
            core.weights.wait_all_split(pe)

            for k, parity, more in steps(pe, NP):
                if kind == 1:
                    B.pe_transpose_h(pe, k)
                    A.pe_linears(pe, k + 1, 0, (0, 1, 2))
                    B.pe_gram(pe, k)
                    A.pe_linears(pe, k + 1, 1, (0,))
                    A.pe_transpose_delta(pe, k + 1)
                    A.pe_linears(pe, k + 1, 1, (1, 2))
                    B.pe_linears(pe, k, 0, (0,))
                    A.pe_context(pe, k + 1, 0)
                    B.pe_linears(pe, k, 0, (1,))
                    A.pe_context(pe, k + 1, 1)
                    B.pe_linears(pe, k, 0, (2,))
                    B.pe_linears(pe, k, 1, (0,))
                    B.pe_transpose_delta(pe, k)
                    B.pe_linears(pe, k, 1, (1, 2))
                    if more:
                        A.pe_transpose_h(pe, k + 2)
                    B.pe_context(pe, k, 0)
                    if more:
                        A.pe_gram(pe, k + 2)
                    B.pe_context(pe, k, 1)
                else:
                    A.pe_messages(pe, k + 1, 0, 1)
                    B.pe_transpose_h(pe, k)
                    A.pe_messages(pe, k + 1, 1, 0)
                    A.pe_messages(pe, k + 1, 1, 1)
                    A.pe_linear(pe, k + 1, A.weights[2], 0, 6)
                    B.pe_messages(pe, k, 0, 0)
                    B.pe_messages(pe, k, 0, 1)
                    A.pe_scores(pe, k + 1)
                    B.pe_messages(pe, k, 1, 0)
                    B.pe_messages(pe, k, 1, 1)
                    A.pe_linear(pe, k + 1, A.weights[2], 1, 7)
                    A.pe_context(pe, k + 1, 0)
                    B.pe_scores(pe, k)
                    A.pe_context(pe, k + 1, 1)
                    if more:
                        A.pe_transpose_h(pe, k + 2)
                    B.pe_linear(pe, k, B.weights[2], 0, 6)
                    B.pe_linear(pe, k, B.weights[2], 1, 7)
                    B.pe_context(pe, k, 0)
                    if more:
                        A.pe_messages(pe, k + 2, 0, 0)
                    B.pe_context(pe, k, 1)

            start(B, NP - 1)
            solo(B, NP - 1)
            B.pe_context(pe, NP - 1, 0)
            B.pe_context(pe, NP - 1, 1)

        @block.scalar
        def _(act):
            def solo(S, k):
                if kind == 1:
                    S.act_exps(act, k)
                    S.act_self(act, k, 0)
                    S.act_self(act, k, 1)
                else:
                    for side, half in ((0, 1), (1, 0), (1, 1)):
                        S.act_messages(act, k, side, half)
                    S.act_exp_u(act, k)

            def start(S, k):
                S.act_h(act, k)
                if kind == 2:
                    S.act_messages(act, k, 0, 0)

            core.weights.act_high(act, 0, 1)
            norm.act_rstd(act, 0)
            core.weights.act_high(act, 1, 2)
            A.act_h(act, 0)
            core.weights.act_high(act, 2, 3)
            norm.act_rstd(act, 1)
            if kind == 2:
                A.act_messages(act, 0, 0, 0)
            if kind == 1:
                A.act_exps(act, 0)
                core.weights.act_high(act, 3, 6)
                A.act_self(act, 0, 0)
                A.act_self(act, 0, 1)
            else:
                A.act_messages(act, 0, 0, 1)
                core.weights.act_high(act, 3, 4)
                A.act_messages(act, 0, 1, 0)
                core.weights.act_high(act, 4, 5)
                A.act_messages(act, 0, 1, 1)
                core.weights.act_high(act, 5, 6)
                A.act_exp_u(act, 0)
            constants.wait(act)
            start(A, 1)
            A.act_rstd(act, 0)

            def body_1(k, more):
                A.act_exps(act, k + 1)
                B.act_h(act, k)
                A.act_self(act, k + 1, 0)
                B.act_exps(act, k)
                A.act_self(act, k + 1, 1)
                if more:
                    norm.act_rstd(act, k + 2)
                B.act_self(act, k, 0)
                A.act_rstd(act, k + 1)
                B.act_self(act, k, 1)
                if more:
                    A.act_h(act, k + 2)
                B.act_rstd(act, k)

            def body_2(k, more, late):
                A.act_messages(act, k + 1, 0, 1)
                B.act_h(act, k)
                A.act_messages(act, k + 1, 1, 0)
                if late:
                    B.act_rstd(act, k - 1)
                A.act_messages(act, k + 1, 1, 1)
                B.act_messages(act, k, 0, 0)
                B.act_messages(act, k, 0, 1)
                if more:
                    norm.act_rstd(act, k + 2)
                A.act_exp_u(act, k + 1)
                B.act_messages(act, k, 1, 0)
                B.act_messages(act, k, 1, 1)
                B.act_exp_u(act, k)
                if more:
                    A.act_h(act, k + 2)
                A.act_rstd(act, k + 1)
                if more:
                    A.act_messages(act, k + 2, 0, 0)

            if kind == 1:
                for k, _, more in steps(act, NP):
                    body_1(k, more)
            else:
                body_2(0, True, False)
                for k, _ in late_steps(act, NP):
                    body_2(k, True, True)
                body_2(NP - 2, False, True)
                B.act_rstd(act, NP - 2)

            start(B, NP - 1)
            solo(B, NP - 1)
            B.act_rstd(act, NP - 1)

        @block.vector
        def _(dve):
            def solo(S, k, parity):
                if kind == 1:
                    S.dve_delta(dve, k, parity)
                    S.dve_side(dve, k, 0, 1)
                    S.dve_side(dve, k, 1, 0)
                    S.dve_triangles(dve, k)
                    S.dve_side(dve, k, 1, 1)
                else:
                    S.dve_lin(dve, k, 0)
                    S.dve_weighted(dve, k, parity)
                    S.dve_delta_t(dve, k, parity)
                    S.dve_lin(dve, k, 1)

            def start(S, k):
                S.dve_low_h(dve, k)
                if kind == 1:
                    S.dve_shift(dve, k)
                    S.dve_side(dve, k, 0, 0)

            if kind == 2:
                for S in (A, B):
                    nc.vector.memset(S.lin[:, :, D:D + 1], 1.0)
            norm.dve_moments(dve, 0, 0)
            norm.dve_xhat(dve, 0)
            core.weights.dve_low(dve, 0, 2)
            constants.wait(dve)
            A.dve_low_h(dve, 0)
            if kind == 1:
                A.dve_shift(dve, 0)
            norm.dve_moments(dve, 1, 1)
            core.weights.dve_low(dve, 2, 3)
            if kind == 1:
                A.dve_side(dve, 0, 0, 0)
            norm.dve_xhat(dve, 1)
            solo(A, 0, 0)
            A.dve_context(dve, 0, 0)
            A.dve_low_h(dve, 1)
            if kind == 1:
                A.dve_shift(dve, 1)
            A.dve_context(dve, 0, 1)
            A.dve_normalise(dve, 0)
            if kind == 1:
                A.dve_side(dve, 1, 0, 0)

            def body_1(k, parity, more, late):
                A.dve_delta(dve, k + 1, 1 - parity)
                A.dve_side(dve, k + 1, 0, 1)
                if late:
                    B.dve_normalise(dve, k - 1)
                B.dve_low_h(dve, k)
                A.dve_side(dve, k + 1, 1, 0)
                B.dve_shift(dve, k)
                A.dve_triangles(dve, k + 1)
                A.dve_side(dve, k + 1, 1, 1)
                if more:
                    norm.dve_moments(dve, k + 2, parity)
                B.dve_delta(dve, k, parity)
                if more:
                    norm.dve_xhat(dve, k + 2)
                B.dve_side(dve, k, 0, 0)
                A.dve_context(dve, k + 1, 0)
                B.dve_side(dve, k, 0, 1)
                A.dve_context(dve, k + 1, 1)
                A.dve_normalise(dve, k + 1)
                B.dve_side(dve, k, 1, 0)
                B.dve_triangles(dve, k)
                B.dve_side(dve, k, 1, 1)
                B.dve_context(dve, k, 0)
                if more:
                    A.dve_low_h(dve, k + 2)
                    A.dve_shift(dve, k + 2)
                B.dve_context(dve, k, 1)
                if more:
                    A.dve_side(dve, k + 2, 0, 0)

            def body_2(k, parity, more, late):
                B.dve_low_h(dve, k)
                if more:
                    norm.dve_moments(dve, k + 2, parity)
                if late:
                    B.dve_normalise(dve, k - 1)
                A.dve_lin(dve, k + 1, 0)
                A.dve_weighted(dve, k + 1, 1 - parity)
                A.dve_delta_t(dve, k + 1, 1 - parity)
                if more:
                    norm.dve_xhat(dve, k + 2)
                A.dve_lin(dve, k + 1, 1)
                A.dve_context(dve, k + 1, 0)
                B.dve_weighted(dve, k, parity)
                A.dve_context(dve, k + 1, 1)
                B.dve_delta_t(dve, k, parity)
                B.dve_lin(dve, k, 0)
                if more:
                    A.dve_low_h(dve, k + 2)
                B.dve_lin(dve, k, 1)
                B.dve_context(dve, k, 0)
                A.dve_normalise(dve, k + 1)
                B.dve_context(dve, k, 1)

            body = body_1 if kind == 1 else body_2
            body(0, 0, True, False)
            for k, parity in late_steps(dve, NP):
                body(k, parity, True, True)
            body(NP - 2, 0, False, True)
            B.dve_normalise(dve, NP - 2)

            start(B, NP - 1)
            solo(B, NP - 1, 1)
            B.dve_context(dve, NP - 1, 0)
            B.dve_context(dve, NP - 1, 1)
            B.dve_normalise(dve, NP - 1)
            B.final(dve, nc.vector, NP - 1)

        @block.gpsimd
        def _(pool):
            if kind == 1:
                core.weights.pool_low(pool)
                constants.wait(pool)
                A.pool_self(pool, 0)
            else:
                A.pool_w(pool, 0, 0)
                A.pool_w(pool, 1, 1)
                B.pool_w(pool, 0, 0)
                core.weights.pool_low(pool)
                constants.wait(pool)

            def body(k, parity, more, late):
                if kind == 1:
                    A.pool_self(pool, k + 1)
                else:
                    if more:
                        A.pool_w(pool, k + 2, parity)
                    B.pool_w(pool, k + 1, 1 - parity)
                if late:
                    B.final(pool, nc.gpsimd, k - 1)
                if kind == 1:
                    B.pool_self(pool, k)

            body(0, 0, True, False)
            for k, parity in late_steps(pool, NP):
                body(k, parity, True, True)
            body(NP - 2, 0, False, True)
            B.final(pool, nc.gpsimd, NP - 2)
            if kind == 1:
                B.pool_self(pool, NP - 1)

    core.signals.end_phase()



def graph_layers_kernel(nc, dram, graphs, phases=(0, 1, 2, 3)):
    core = Core()
    core.dram, core.pairs = dram, graphs // G
    with ExitStack() as ctx:
        def sb(name, shape, dt=F32):
            return ctx.enter_context(nc.sbuf_tensor(name, shape, dt))

        core.signals = Signals(nc, ctx, core.pairs)

        core.unwatched = core.signals.once("unwatched", 0)
        dram["x_mid"] = nc.dram_tensor("x_mid", [graphs, P, D], F32, kind="Internal").ap()
        core.ident = sb("ident", [P, P])
        core.triangles = sb("triangles", [P, 2, P])
        core.ln_eps = sb("ln_eps", [P, 1])
        core.eps_l1 = sb("eps_l1", [P, 1])
        core.eps_l2 = sb("eps_l2", [P, 1])
        core.x_places = sb("x", [P, Residual.SLOTS * G, D])
        core.x_ahead = False
        core.weights = Weights(nc, core, ctx, phases)
        filled = core.signals.once("constants_filled", 5)
        with nc.Block() as block:
            @block.gpsimd
            def _(pool):
                nc.gpsimd.memset(core.ident[:, :], 0.0).then_inc(filled.sem, 1)
                nc.gpsimd.memset(core.triangles[:, :, :], 1.0).then_inc(filled.sem, 1)
                nc.gpsimd.memset(core.ln_eps[:, :], LN_EPS)
                nc.gpsimd.memset(core.eps_l1[:, :], 1e-12)
                nc.gpsimd.memset(core.eps_l2[:, :], 1e-18)
                pool.wait_ge(filled.sem, filled.base + 2)
                nc.gpsimd.affine_select(out=core.ident[:, :], in_=core.ident[:, :], compare_op=ALU.not_equal, fill=1.0,
                                        base=0, pattern=[[-1, P]], channel_multiplier=1).then_inc(filled.sem, 1)
                nc.gpsimd.affine_select(out=core.triangles[:, 0, :], in_=core.triangles[:, 0, :],
                                        compare_op=ALU.is_gt, fill=0.0, base=0, pattern=[[-1, P]],
                                        channel_multiplier=1).then_inc(filled.sem, 1)
                nc.gpsimd.affine_select(out=core.triangles[:, 1, :], in_=core.triangles[:, 1, :],
                                        compare_op=ALU.is_gt, fill=0.0, base=0, pattern=[[1, P]],
                                        channel_multiplier=-1).then_inc(filled.sem, 1)

            @block.scalar
            def _(act):
                nc.scalar.preload_act_table_set("natural_log_exp_and_others")

        if 0 in phases:
            attention_phase(nc, core, ["l0_bv", "l0_bo"], True)
        if 1 in phases:
            graph_phase(nc, core, 1)
        if 2 in phases:
            graph_phase(nc, core, 2)
        if 3 in phases:
            attention_phase(nc, core, ["l3_bv", "l3_bq", "l3_bk", "l3_beta"], False)


def layout(inputs):
    import numpy as np

    def chunks(w):
        return np.ascontiguousarray(w.reshape(C, P, D).transpose(1, 0, 2))

    def column(b):
        return np.ascontiguousarray(b.reshape(C, P).T)

    a = {n: np.asarray(v) for n, v in inputs.items()}
    out = {"x": a["x"], "adj": a["adj"], "adjT": np.ascontiguousarray(a["adj"].transpose(0, 2, 1))}
    for name, key in (("wq", "Wq"), ("wk", "Wk"), ("wv", "Wv"), ("wo", "Wo")):
        out[f"l0_{name}"] = chunks(a[f"L0_gnn_{key}"].T)
    out["l0_bv"], out["l0_bo"] = a["L0_gnn_bv"], a["L0_gnn_bo"]
    for j in range(2):
        for s in "lsr":
            out[f"l1_w{s}{j}"] = chunks(a[f"L1_gnn_W{s}"][j].T)
            out[f"l1_b{s}{j}"] = a[f"L1_gnn_b{s}"][j]
        for name, key in (("left", "W_left"), ("right", "W_right"), ("lin", "W_lin")):
            out[f"l2_{name}{j}"] = chunks(a[f"L2_gnn_{key}"][j].T)
        out[f"l2_b{j}"] = a["L2_gnn_b_lin"][j]
    for layer, g, b in ((1, "L1_gnn_ln_w", "L1_gnn_ln_b"), (2, "L2_gnn_ln_a", "L2_gnn_ln_b")):
        out[f"l{layer}_gammaT"], out[f"l{layer}_betaT"] = column(a[g][0]), column(a[b][0])
        out[f"l{layer}_gamma"], out[f"l{layer}_beta"] = a[g][1], a[b][1]
    for name, key in (("wq", "Wq"), ("wk", "Wk"), ("wv", "Wv")):
        out[f"l3_{name}"] = chunks(a[f"L3_gnn_{key}"])
    out["l3_bq"], out["l3_bk"] = column(a["L3_gnn_bq"]), column(a["L3_gnn_bk"])
    out["l3_bv"], out["l3_beta"] = a["L3_gnn_bv"], a["L3_gnn_beta"].reshape(1)
    return {n: np.ascontiguousarray(v) for n, v in out.items()}


def kernel(**inputs):
    import concourse.bacc as _bacc
    from concourse.bass_utils import run_bass_kernel_spmd

    arrays = layout(inputs)
    nc = _bacc.Bacc("TRN2", target_bir_lowering=False, num_devices=1)
    dram = {n: nc.dram_tensor(f"in_{n}", a.shape, F32, kind="ExternalInput").ap() for n, a in arrays.items()}
    dram["out"] = nc.dram_tensor("out", arrays["x"].shape, F32, kind="ExternalOutput").ap()
    graph_layers_kernel(nc, dram, arrays["x"].shape[0])
    got = run_bass_kernel_spmd(nc, [{f"in_{n}": a for n, a in arrays.items()}], core_ids=[0])
    return got.results[0]["out"]
```
